# Optimizing a Trainium2 kernel written in Bass

```python
import numpy as np
import jax
import jax.numpy as jnp

def _softmax(x, axis=-1):
    return jax.nn.softmax(x, axis=axis)

def _gelu(x):
    return jax.nn.gelu(x, approximate=True)

def _silu(x):
    return jax.nn.silu(x)

def _sigmoid(x):
    return jax.nn.sigmoid(x)

def _layernorm(x, axis=-1, eps=1e-05):
    m = jnp.mean(x, axis=axis, keepdims=True)
    v = jnp.var(x, axis=axis, keepdims=True)
    return (x - m) / jnp.sqrt(v + eps)

def _scatter_add(tgt, idx, src, axis=0):
    return tgt.at[idx].add(src)

def _segment_sum(src, seg, n):
    return jax.ops.segment_sum(src, seg, n)
kernel_name = 'mk_adaln_d2_jaxref_r8_cb9fd0'

def setup_inputs(seed: int=0):
    np.random.seed(seed)
    _w = jnp.asarray

    def _L0_attn_setup():
        import jax, jax.numpy as jnp
        import numpy as np
        ROPE_THETA = 10000.0
        INF_APPROX = 1e+30
        D_HEAD = 128

        def _rope(x, theta=ROPE_THETA):
            *_, L, D = x.shape
            half = D // 2
            pos = jnp.arange(L, dtype=jnp.float32)[:, None]
            freqs = jnp.power(theta, -jnp.arange(half, dtype=jnp.float32) / half)[None, :]
            angles = pos * freqs
            cos = jnp.cos(angles).astype(x.dtype)
            sin = jnp.sin(angles).astype(x.dtype)
            even, odd = jnp.split(x, 2, axis=-1)
            r_even = even * cos - odd * sin
            r_odd = even * sin + odd * cos
            return jnp.concatenate([r_even, r_odd], axis=-1)
        key = jax.random.key(seed)
        kx, kq, kk, kv, ko = jax.random.split(key, 5)
        B, T, M, D, G, H = (2, 128, 256, 128, 4, 4)
        std_m = M ** (-0.5)
        std_d = D ** (-0.5)
        return {'x': jax.random.normal(kx, (B, T, M), jnp.float32), 'w_aq': jax.random.normal(kq, (G, H, M, D), jnp.float32) * std_m, 'w_ak': jax.random.normal(kk, (G, M, D), jnp.float32) * std_m, 'w_av': jax.random.normal(kv, (G, M, D), jnp.float32) * std_m, 'w_ao': jax.random.normal(ko, (G, H, D, M), jnp.float32) * std_d}
    _L0_attn_in = _L0_attn_setup()

    def _L0_ffn_setup():
        import jax, jax.numpy as jnp
        import numpy as np
        EPS = 1e-07
        CURVATURE = 1.0
        MAX_NORM_RATIO = 0.99
        B, L, N, K = (4, 256, 256, 256)

        def _ternary_init(key, n, k):
            rand = jax.random.normal(key, (n, k), dtype=jnp.float32)
            threshold = 0.5 * jnp.mean(jnp.abs(rand))
            return jnp.where(rand > threshold, 1.0, jnp.where(rand < -threshold, -1.0, 0.0)).astype(jnp.float32)
        key = jax.random.key(seed)
        kx, kw = jax.random.split(key)
        x = jax.random.normal(kx, (B, L, N), dtype=jnp.float32)
        weight = _ternary_init(kw, N, K)
        scale = jnp.full((K,), 1.0 / np.sqrt(N), dtype=jnp.float32)
        return {'x': x, 'weight': weight, 'scale': scale}
    _L0_ffn_in = _L0_ffn_setup()
    _L0_c = _w((lambda *s: np.random.randn(*s).astype(np.float32) * 0.05)(2, 256))
    _L0_wmod = _w((lambda *s: np.random.randn(*s).astype(np.float32) * 0.05)(256, 6 * 256) * 256 ** (-0.5))

    def _L1_attn_setup():
        import jax, jax.numpy as jnp
        import numpy as np
        B, S, D, H = (2, 256, 256, 16)
        QR, KVR = (96, 64)
        DN, DR, DV = (128, 64, 128)
        EPS = 1e-06
        WSCALE = 0.02

        def rms_norm(x, w, eps=EPS):
            return x * jax.lax.rsqrt(jnp.mean(x * x, axis=-1, keepdims=True) + eps) * w

        def rope_cos_sin(seq_len, d):
            inv = 1.0 / 10000.0 ** (jnp.arange(0, d, 2, dtype=jnp.float32) / d)
            t = jnp.arange(seq_len, dtype=jnp.float32)
            f = jnp.outer(t, inv)
            return (jnp.cos(f)[:, None, :], jnp.sin(f)[:, None, :])

        def apply_rope(x, cos, sin):
            x1, x2 = (x[..., 0::2], x[..., 1::2])
            o1 = x1 * cos - x2 * sin
            o2 = x1 * sin + x2 * cos
            return jnp.stack([o1, o2], axis=-1).reshape(x.shape)
        key = jax.random.key(seed)
        ks = jax.random.split(key, 10)
        return {'x': jax.random.normal(ks[0], (B, S, D), jnp.float32), 'wq_down': jax.random.normal(ks[1], (D, QR), jnp.float32) * WSCALE, 'q_norm_w': jnp.ones((QR,), jnp.float32), 'wq_up': jax.random.normal(ks[2], (QR, H * DN), jnp.float32) * WSCALE, 'wq_rope': jax.random.normal(ks[3], (QR, H * DR), jnp.float32) * WSCALE, 'wkv_down': jax.random.normal(ks[4], (D, KVR), jnp.float32) * WSCALE, 'kv_norm_w': jnp.ones((KVR,), jnp.float32), 'wkv_up': jax.random.normal(ks[5], (KVR, H * (DN + DV)), jnp.float32) * WSCALE, 'wk_rope': jax.random.normal(ks[6], (D, DR), jnp.float32) * WSCALE, 'wo': jax.random.normal(ks[7], (H * DV, D), jnp.float32) * WSCALE}
    _L1_attn_in = _L1_attn_setup()

    def _L1_ffn_setup():
        import jax, jax.numpy as jnp
        import numpy as np
        B, T = (1, 64)
        DIM = 256
        MOE_INTER = 176
        N_EXPERTS = 64
        TOPK = 6
        N_SHARED = 2
        SHARED_INTER = N_SHARED * MOE_INTER
        CAPACITY = 128
        ROUTE_SCALE = 1.0
        key = jax.random.key(seed)
        ks = jax.random.split(key, 8)

        def w(k, shape, fan_in):
            return jax.random.normal(k, shape, jnp.float32) * fan_in ** (-0.5)
        return {'x': jax.random.normal(ks[0], (B, T, DIM), jnp.float32), 'gate_w': w(ks[1], (N_EXPERTS, DIM), DIM), 'w1': w(ks[2], (N_EXPERTS, MOE_INTER, DIM), DIM), 'w2': w(ks[3], (N_EXPERTS, DIM, MOE_INTER), MOE_INTER), 'w3': w(ks[4], (N_EXPERTS, MOE_INTER, DIM), DIM), 'sw1': w(ks[5], (SHARED_INTER, DIM), DIM), 'sw2': w(ks[6], (DIM, SHARED_INTER), SHARED_INTER), 'sw3': w(ks[7], (SHARED_INTER, DIM), DIM)}
    _L1_ffn_in = _L1_ffn_setup()
    _L1_c = _w((lambda *s: np.random.randn(*s).astype(np.float32) * 0.05)(2, 256))
    _L1_wmod = _w((lambda *s: np.random.randn(*s).astype(np.float32) * 0.05)(256, 6 * 256) * 256 ** (-0.5))
    _d = {'L0_attn_x': _L0_attn_in['x'], 'L0_attn_w_aq': _L0_attn_in['w_aq'], 'L0_attn_w_ak': _L0_attn_in['w_ak'], 'L0_attn_w_av': _L0_attn_in['w_av'], 'L0_attn_w_ao': _L0_attn_in['w_ao'], 'L0_ffn_weight': _L0_ffn_in['weight'], 'L0_ffn_scale': _L0_ffn_in['scale'], 'L0_c': _L0_c, 'L0_wmod': _L0_wmod, 'L1_attn_wq_down': _L1_attn_in['wq_down'], 'L1_attn_q_norm_w': _L1_attn_in['q_norm_w'], 'L1_attn_wq_up': _L1_attn_in['wq_up'], 'L1_attn_wq_rope': _L1_attn_in['wq_rope'], 'L1_attn_wkv_down': _L1_attn_in['wkv_down'], 'L1_attn_kv_norm_w': _L1_attn_in['kv_norm_w'], 'L1_attn_wkv_up': _L1_attn_in['wkv_up'], 'L1_attn_wk_rope': _L1_attn_in['wk_rope'], 'L1_attn_wo': _L1_attn_in['wo'], 'L1_ffn_gate_w': _L1_ffn_in['gate_w'], 'L1_ffn_w1': _L1_ffn_in['w1'], 'L1_ffn_w2': _L1_ffn_in['w2'], 'L1_ffn_w3': _L1_ffn_in['w3'], 'L1_ffn_sw1': _L1_ffn_in['sw1'], 'L1_ffn_sw2': _L1_ffn_in['sw2'], 'L1_ffn_sw3': _L1_ffn_in['sw3'], 'L1_c': _L1_c, 'L1_wmod': _L1_wmod}
    _x0 = _d['L0_attn_x']
    _d['L0_attn_x'] = jax.random.normal(jax.random.fold_in(jax.random.key(seed), 1), (2, 1024, 256), dtype=_x0.dtype)
    del _x0
    return _d

def reference(L0_attn_x, L0_attn_w_aq, L0_attn_w_ak, L0_attn_w_av, L0_attn_w_ao, L0_ffn_weight, L0_ffn_scale, L0_c, L0_wmod, L1_attn_wq_down, L1_attn_q_norm_w, L1_attn_wq_up, L1_attn_wq_rope, L1_attn_wkv_down, L1_attn_kv_norm_w, L1_attn_wkv_up, L1_attn_wk_rope, L1_attn_wo, L1_ffn_gate_w, L1_ffn_w1, L1_ffn_w2, L1_ffn_w3, L1_ffn_sw1, L1_ffn_sw2, L1_ffn_sw3, L1_c, L1_wmod):

    def _L0_attn_ref(x, w_aq, w_ak, w_av, w_ao):
        import jax, jax.numpy as jnp
        import numpy as np
        ROPE_THETA = 10000.0
        INF_APPROX = 1e+30
        D_HEAD = 128

        def _rope(x, theta=ROPE_THETA):
            *_, L, D = x.shape
            half = D // 2
            pos = jnp.arange(L, dtype=jnp.float32)[:, None]
            freqs = jnp.power(theta, -jnp.arange(half, dtype=jnp.float32) / half)[None, :]
            angles = pos * freqs
            cos = jnp.cos(angles).astype(x.dtype)
            sin = jnp.sin(angles).astype(x.dtype)
            even, odd = jnp.split(x, 2, axis=-1)
            r_even = even * cos - odd * sin
            r_odd = even * sin + odd * cos
            return jnp.concatenate([r_even, r_odd], axis=-1)
        B, T, M = x.shape
        q = jnp.einsum('bim,ghmd->bghid', x, w_aq)
        k = jnp.einsum('bim,gmd->bgid', x, w_ak)
        v = jnp.einsum('bim,gmd->bgid', x, w_av)
        q = _rope(q)
        k = _rope(k)
        qk_mult = jnp.asarray(D_HEAD ** (-0.25), dtype=x.dtype)
        s = jnp.einsum('bghid,bgjd->bghij', q * qk_mult, k * qk_mult)
        i = jnp.arange(T)[:, None]
        j = jnp.arange(T)[None, :]
        mask = (i < j).astype(s.dtype)
        s = s - jnp.asarray(INF_APPROX, dtype=s.dtype) * mask
        p = jax.nn.softmax(s, axis=-1)
        o = jnp.einsum('bghij,bgjd->bghid', p, v)
        r = jnp.einsum('bghid,ghdm->bim', o, w_ao)
        return r

    def _L0_ffn_ref(x, weight, scale):
        import jax, jax.numpy as jnp
        import numpy as np
        EPS = 1e-07
        CURVATURE = 1.0
        MAX_NORM_RATIO = 0.99
        B, L, N, K = (4, 256, 256, 256)

        def _ternary_init(key, n, k):
            rand = jax.random.normal(key, (n, k), dtype=jnp.float32)
            threshold = 0.5 * jnp.mean(jnp.abs(rand))
            return jnp.where(rand > threshold, 1.0, jnp.where(rand < -threshold, -1.0, 0.0)).astype(jnp.float32)
        sqrt_c = jnp.sqrt(jnp.float32(CURVATURE))
        out = jnp.einsum('bln,nk->blk', x, weight) * scale
        v_norm = jnp.maximum(jnp.linalg.norm(out, axis=-1, keepdims=True), EPS)
        scaled_norm = sqrt_c * v_norm
        out = out * (jnp.tanh(scaled_norm) / (scaled_norm + EPS))
        max_norm = MAX_NORM_RATIO / sqrt_c
        o_norm = jnp.maximum(jnp.linalg.norm(out, axis=-1, keepdims=True), EPS)
        out = out * jnp.minimum(max_norm / o_norm, 1.0)
        return out.astype(x.dtype)

    def _L1_attn_ref(x, wq_down, q_norm_w, wq_up, wq_rope, wkv_down, kv_norm_w, wkv_up, wk_rope, wo):
        import jax, jax.numpy as jnp
        import numpy as np
        B, S, D, H = (2, 256, 256, 16)
        QR, KVR = (96, 64)
        DN, DR, DV = (128, 64, 128)
        EPS = 1e-06
        WSCALE = 0.02

        def rms_norm(x, w, eps=EPS):
            return x * jax.lax.rsqrt(jnp.mean(x * x, axis=-1, keepdims=True) + eps) * w

        def rope_cos_sin(seq_len, d):
            inv = 1.0 / 10000.0 ** (jnp.arange(0, d, 2, dtype=jnp.float32) / d)
            t = jnp.arange(seq_len, dtype=jnp.float32)
            f = jnp.outer(t, inv)
            return (jnp.cos(f)[:, None, :], jnp.sin(f)[:, None, :])

        def apply_rope(x, cos, sin):
            x1, x2 = (x[..., 0::2], x[..., 1::2])
            o1 = x1 * cos - x2 * sin
            o2 = x1 * sin + x2 * cos
            return jnp.stack([o1, o2], axis=-1).reshape(x.shape)
        bs, seq_len, _ = x.shape
        qc = rms_norm(x @ wq_down, q_norm_w)
        q_nope = (qc @ wq_up).reshape(bs, seq_len, H, DN)
        q_pe = (qc @ wq_rope).reshape(bs, seq_len, H, DR)
        kvc = rms_norm(x @ wkv_down, kv_norm_w)
        kv = (kvc @ wkv_up).reshape(bs, seq_len, H, DN + DV)
        k_nope, v = (kv[..., :DN], kv[..., DN:])
        k_rope = (x @ wk_rope).reshape(bs, seq_len, 1, DR)
        cos, sin = rope_cos_sin(seq_len, DR)
        q_pe = apply_rope(q_pe, cos, sin)
        k_rope = apply_rope(k_rope, cos, sin)
        k_rope = jnp.broadcast_to(k_rope, (bs, seq_len, H, DR))
        q = jnp.concatenate([q_nope, q_pe], axis=-1)
        k = jnp.concatenate([k_nope, k_rope], axis=-1)
        scale = 1.0 / np.sqrt(DN + DR).astype(np.float32)
        scores = jnp.einsum('bqhd,bkhd->bhqk', q, k) * scale
        mask = jnp.triu(jnp.full((seq_len, seq_len), -jnp.inf, jnp.float32), k=1)
        probs = jax.nn.softmax(scores.astype(jnp.float32) + mask, axis=-1).astype(q.dtype)
        out = jnp.einsum('bhqk,bkhd->bqhd', probs, v).reshape(bs, seq_len, H * DV)
        return out @ wo

    def _L1_ffn_ref(x, gate_w, w1, w2, w3, sw1, sw2, sw3):
        import jax, jax.numpy as jnp
        import numpy as np
        B, T = (1, 64)
        DIM = 256
        MOE_INTER = 176
        N_EXPERTS = 64
        TOPK = 6
        N_SHARED = 2
        SHARED_INTER = N_SHARED * MOE_INTER
        CAPACITY = 128
        ROUTE_SCALE = 1.0
        Bb, Tt, D = x.shape
        xf = x.reshape(-1, D)
        N = xf.shape[0]
        logits = xf @ gate_w.T
        scores = jax.nn.softmax(logits, axis=-1)
        gate_vals, idx = jax.lax.top_k(scores, TOPK)
        gate_vals = gate_vals * ROUTE_SCALE
        E = gate_w.shape[0]
        fe = idx.reshape(-1)
        ft = jnp.repeat(jnp.arange(N), TOPK)
        onehot = (fe[:, None] == jnp.arange(E)[None, :]).astype(jnp.int32)
        pos = jnp.take_along_axis(jnp.cumsum(onehot, axis=0) - 1, fe[:, None], axis=1)[:, 0]
        keep = pos < CAPACITY
        buf = jnp.full((E, CAPACITY), N, dtype=jnp.int32)
        buf = buf.at[fe, pos].set(ft.astype(jnp.int32), mode='drop')
        xpad = jnp.concatenate([xf, jnp.zeros((1, D), xf.dtype)], axis=0)
        xe = xpad[buf]
        h = jax.nn.silu(jnp.einsum('ecd,eid->eci', xe, w1)) * jnp.einsum('ecd,eid->eci', xe, w3)
        ye = jnp.einsum('eci,edi->ecd', h, w2)
        pc = jnp.minimum(pos, CAPACITY - 1)
        op = ye[fe, pc] * keep[:, None].astype(ye.dtype)
        routed = (op * gate_vals.reshape(-1)[:, None]).reshape(N, TOPK, D).sum(axis=1)
        z = jax.nn.silu(xf @ sw1.T) * (xf @ sw3.T) @ sw2.T
        return (routed + z).reshape(Bb, Tt, D)
    x = L0_attn_x
    mod = (_silu(L0_c) @ L0_wmod).reshape(L0_c.shape[0], 6, 1, -1)
    sa, ca, ga, sb, cb, gb = (mod[:, 0], mod[:, 1], mod[:, 2], mod[:, 3], mod[:, 4], mod[:, 5])
    ga = (2 * (ga >= 0) - 1) * jnp.maximum(jnp.abs(ga), 0.25)
    gb = (2 * (gb >= 0) - 1) * jnp.maximum(jnp.abs(gb), 0.25)
    h = _layernorm(x, axis=-1) * (1 + ca) + sa
    x = x + ga * _L0_attn_ref(h, L0_attn_w_aq, L0_attn_w_ak, L0_attn_w_av, L0_attn_w_ao)
    h = _layernorm(x, axis=-1) * (1 + cb) + sb
    x = x + gb * _L0_ffn_ref(h, L0_ffn_weight, L0_ffn_scale)
    mod = (_silu(L1_c) @ L1_wmod).reshape(L1_c.shape[0], 6, 1, -1)
    sa, ca, ga, sb, cb, gb = (mod[:, 0], mod[:, 1], mod[:, 2], mod[:, 3], mod[:, 4], mod[:, 5])
    ga = (2 * (ga >= 0) - 1) * jnp.maximum(jnp.abs(ga), 0.25)
    gb = (2 * (gb >= 0) - 1) * jnp.maximum(jnp.abs(gb), 0.25)
    h = _layernorm(x, axis=-1) * (1 + ca) + sa
    x = x + ga * _L1_attn_ref(h, L1_attn_wq_down, L1_attn_q_norm_w, L1_attn_wq_up, L1_attn_wq_rope, L1_attn_wkv_down, L1_attn_kv_norm_w, L1_attn_wkv_up, L1_attn_wk_rope, L1_attn_wo)
    h = _layernorm(x, axis=-1) * (1 + cb) + sb
    x = x + gb * _L1_ffn_ref(h, L1_ffn_gate_w, L1_ffn_w1, L1_ffn_w2, L1_ffn_w3, L1_ffn_sw1, L1_ffn_sw2, L1_ffn_sw3)
    return x

_drawn_inputs = setup_inputs


def setup_inputs(seed=0):
    import zlib

    import numpy as np

    out = dict(_drawn_inputs(seed))
    spreads = {'L0_ffn_scale': (0.0625, 0.6),
     'L1_attn_q_norm_w': (1.0, 0.6),
     'L1_attn_kv_norm_w': (1.0, 0.6)}
    factors = {'L0_ffn_weight': 3.612,
     'L1_attn_wq_down': 8.0,
     'L1_attn_wq_up': 8.0,
     'L1_attn_wq_rope': 8.0,
     'L1_attn_wkv_down': 8.0,
     'L1_attn_wkv_up': 8.0,
     'L1_attn_wk_rope': 8.0,
     'L1_attn_wo': 8.0,
     'L1_ffn_gate_w': 8.0,
     'L1_ffn_w1': 7.388,
     'L1_ffn_w2': 6.969,
     'L1_ffn_w3': 6.915,
     'L1_ffn_sw1': 8.0,
     'L1_ffn_sw2': 8.0,
     'L1_ffn_sw3': 8.0}
    for name, (base, spread) in spreads.items():
        noise = np.random.default_rng([zlib.crc32(name.encode()), seed]).standard_normal(out[name].shape)
        drawn = base * np.exp(spread * noise) if base else spread * noise
        out[name] = jnp.asarray(drawn.astype(out[name].dtype))
    for name, factor in factors.items():
        out[name] = (out[name] * factor).astype(out[name].dtype)
    return out
```

```python
from contextlib import ExitStack

import concourse.bass as bass
from concourse import mybir

F32 = mybir.dt.float32
BF16 = mybir.dt.bfloat16
U32 = mybir.dt.uint32
ALU = mybir.AluOpType
ACT = mybir.ActivationFunctionType
AX = mybir.AxisListType

P = 128
B, T, M = 2, 1024, 256
KT = M // P
TT = T // P
NT = B * TT
G, HG = 4, 4
D = 128
QR, KVR, DR, DV = 96, 64, 64, 128
RAW = QR + KVR + DR
E, I, TOPK, CAP = 64, 176, 6, 128
I2 = I - P
SI = 352
SLOTS = E * CAP
RING = 8
LN_EPS, RMS_EPS, HYP_EPS, MAX_NORM = 1e-5, 1e-6, 1e-7, 0.99
L1_SCALE = float((128 + DR) ** -0.5)


def attention_steps():
    steps, turn = [], 0
    for i in range(TT + 1):
        work = []
        if i:
            for j in range(i):
                work.append(("T", i - 1, j, turn + j))
                if j:
                    work.append(("A", i - 1, j - 1, turn + j - 1))
            work.append(("A", i - 1, i - 1, turn + i - 1))
            work.append(("R", i - 1, 0, 0))
            turn += i
        done = 0
        for h in range(HG):
            if i < TT:
                steps.append(("S", i, h, HG * i + h))
            if h == 0 and i >= 2:
                steps.append(("O", i - 2, 0, 0))
            upto = len(work) * (h + 1) // HG
            steps += work[done:upto]
            done = upto
    steps.append(("O", TT - 1, 0, 0))
    return steps, turn


STEPS, TURNS = attention_steps()
NS = HG * TT


def settle(eng, passed):
    eng.sem_inc(passed, 1)


def program(nc, a, out):
    with ExitStack() as ctx:
        def sb(name, shape, dt=F32):
            return ctx.enter_context(nc.sbuf_tensor(name, shape, dt))

        def sem(name):
            return ctx.enter_context(nc.semaphore(name))

        hd = nc.dram_tensor("h_rows", (B * T + P, M), F32, kind="Internal").ap()
        table = nc.dram_tensor("slot_table", (SLOTS + NT * TOPK * P, 2), F32, kind="Internal").ap()
        acc = nc.dram_tensor("routed_sum", (B * T + P, M), F32, kind="Internal").ap()

        X = sb("X", [P, NT, M])
        big = sb("big", [P, 13312])
        hT = sb("hT", [P, KT, B * T])
        vbig = sb("vbig", [P, NT, 512])
        ident = sb("ident", [P, P])
        identb = sb("identb", [P, P], BF16)
        maskb = sb("maskb", [P, P], BF16)
        trib = sb("trib", [P, P], BF16)
        onesb = sb("onesb", [P, P], BF16)
        iota = sb("iota", [P, E])
        dumps = sb("dumps", [P, NT, TOPK])
        tokid = sb("tokid", [P, NT])
        att = sb("att", [P, 10496])
        rope = att[:, 0:2048].rearrange("p (w t) -> p w t", w=2)
        Wq1 = att[0:QR, 2048:4096].rearrange("p (h n) -> p h n", h=16)
        Wvo = att[:, 4096:6144].rearrange("p (h m) -> p h m", h=8)
        WQ = att[:, 6144:7424].rearrange("p (k h d) -> p k h d", k=KT, h=HG + 1)
        WOr = att[:, 7424:8448].rearrange("p (h m) -> p h m", h=HG)
        rinv64 = att[:, 7424:7936].rearrange("p (u n) -> p u n", u=2)
        WO = att[:, 8448:9472].rearrange("p (h m) -> p h m", h=HG)
        Vs = att[:, 9472:10496].rearrange("p (t d) -> p t d", t=TT)
        ring = att[:, 0:7680].rearrange("p (u n) -> p u n", u=RING)
        ring2 = att[0:I2, 7680:9728].rearrange("p (u n) -> p u n", u=RING)
        cT = sb("cT", [P, KT, 4])
        sg = sb("sg", [P, KT, 4])
        sc = sb("sc", [P, KT, 4])
        modT = sb("modT", [P, 2, 12, B])
        gm = sb("gm", [P, 4, B, M])
        sm = sb("sm", [P, 2, B, M])
        Wff = sb("Wff", [P, KT, M])
        sc_bc = sb("sc_bc", [P, M])
        Wdown = sb("Wdown", [P, KT, RAW])
        qw_bc = sb("qw_bc", [P, QR])
        kvw_bc = sb("kvw_bc", [P, KVR])
        gateT = sb("gateT", [P, KT, E])
        st = sb("st", [P, NT, 6])
        t16 = sb("t16", [P, 12, NT])
        rtv = sb("rtv", [P, 4 * T])
        rt = rtv[:, :].rearrange("p (u w t) -> p u w t", u=2, w=2)
        gs = rtv[:, 0:2048].rearrange("p (a b m) -> p a b m", a=4, b=B)
        scb = rtv[:, 2048:3072].rearrange("p (k c n) -> p k c n", k=KT, c=4)
        Wv = rtv[:, 3072:4096].rearrange("p (k n) -> p k n", k=KT)
        kcs = rtv[:, 0:1024].rearrange("p (w t r) -> p w t r", w=2, t=TT)
        sw13 = rtv[:, 0:1536].rearrange("p (k w n) -> p k w n", k=KT, w=2)
        sw2 = rtv[:, 1536:2304].rearrange("p (k m) -> p k m", k=3)
        nmax = sb("nmax", [P, 2])
        rsum = sb("rsum", [P, 2, HG])
        rinv = sb("rinv", [P, 2, HG])
        PTs = sb("PTs", [P, 2, HG * P])
        Rs = sb("Rs", [P, HG * P])
        OTs = sb("OTs", [P, HG * P])
        xn = Rs[:, :].rearrange("p (u m) -> p u m", u=2)
        hTs = PTs[:, 0, :].rearrange("p (u k q) -> p u k q", u=2, k=KT)
        sq = OTs[:, :].rearrange("p (u m) -> p u m", u=2)

        Pr = big[:, 0:8192].rearrange("p (u h k) -> p u h k", u=2, h=HG)
        QT = big[:, 8192:12288].rearrange("p (h t) -> p h t", h=HG)
        Krope = big[:, 12288:13312]
        wmod = big[:, 0:6144].rearrange("p (l k n) -> p l k n", l=2, k=KT)
        vflat = vbig[:, :, :].rearrange("p t n -> p (t n)")
        wqu = vflat[:, 0:1536].rearrange("p (h n) -> p h n", h=16)
        wku = vflat[:, 1536:2560].rearrange("p (h n) -> p h n", h=16)
        wvu = vflat[:, 2560:3584].rearrange("p (h n) -> p h n", h=16)
        wo1 = vflat[:, 3584:7680].rearrange("p (h n) -> p h n", h=16)
        ffo = vbig[:, :, 0:M]
        raw = vbig[:, :, 0:RAW]
        rope_a = vbig[:, :, 256:320]
        rope_b = vbig[:, :, 320:384]
        V1 = vbig[:, :, 384:448]
        qcT = hT[0:QR, 0, :]
        KT1 = hT[:, 1, :]
        qn = xn
        hrow = big[:, 0:512].rearrange("p (u n) -> p u n", u=2)
        actA = big[:, 512:1280].rearrange("p (u n) -> p u n", u=2)
        actB = big[:, 1280:1664]
        actT = big[:, 1664:2432].rearrange("p (u n) -> p u n", u=2)
        zero = big[:, 2432:2688]
        xe = big[:, 2688:3200].rearrange("p (u n) -> p u n", u=2)
        xeT = big[:, 3200:3712].rearrange("p (u n) -> p u n", u=2)
        eg = big[:, 3712:4064].rearrange("p (u n) -> p u n", u=2)
        eh = big[:, 4064:4416].rearrange("p (u n) -> p u n", u=2)
        ehT = big[:, 4416:4928].rearrange("p (u n) -> p u n", u=2)
        ys = big[:, 4928:5440].rearrange("p (u n) -> p u n", u=2)
        slots = big[:, 5440:5568].rearrange("p (e c) -> p e c", c=2)
        ohm = big[:, 5632:11776].rearrange("p (t k e) -> p t k e", t=NT, k=TOPK)
        prob = big[:, 11776:12800].rearrange("p (t e) -> p t e", t=NT)
        lg = rtv[:, 2304:3328].rearrange("p (t e) -> p t e", t=NT)
        ohb = hT[:, :, :].rearrange("p k t -> p (k t)")[:, 0:3072].bitcast(BF16)
        oh = ohb.rearrange("p (t k e) -> p t k e", t=NT, k=TOPK)
        maskt = hT[:, 1, 1024:1536].bitcast(BF16).rearrange("p (t e) -> p t e", t=NT)
        seen = hT[:, 1, 1536:2048].bitcast(BF16).rearrange("p (t e) -> p t e", t=NT)
        top8 = rtv[:, 3328:3456].rearrange("p (t k) -> p t k", t=NT)
        idx8 = rtv[:, 3456:3584].bitcast(U32).rearrange("p (t k) -> p t k", t=NT)
        idxf = rtv[:, 3584:3712].rearrange("p (t k) -> p t k", t=NT)
        posk = rtv[:, 3712:3808].rearrange("p (t k) -> p t k", t=NT)
        slotf = rtv[:, 3808:3904].rearrange("p (t k) -> p t k", t=NT)
        over = rtv[:, 3904:4000].rearrange("p (t k) -> p t k", t=NT)
        slotu = rtv[:, 4000:4096].bitcast(U32).rearrange("p (t k) -> p t k", t=NT)
        pay = big[:, 12800:12992].rearrange("p (t k c) -> p t k c", t=NT, k=TOPK)
        slotc = sb("slotc", [P, 2, TOPK], U32)
        payc = sb("payc", [P, 2, TOPK, 2])
        toku = sb("toku", [P, E], U32)
        tokc = sb("tokc", [P, 4], U32)
        zall = vbig[:, :, 256:512]
        accs = vbig[:, :, 0:M]

        ps = [ctx.enter_context(nc.psum_tensor(f"ps{i}", [P, 512], F32)) for i in range(4)]
        sco = [ctx.enter_context(nc.psum_tensor(f"sco{i}", [P, 1024], F32)) for i in range(2)]
        ptp, OTp, mis = ps[0:2], ps[2], ps[3]

        s_act, s_pool = sem("act_waits_passed"), sem("pool_waits_passed")
        s_x = sem("x_loaded")
        s_c = sem("consts_loaded")
        s_wm = sem("wmod_loaded")
        s_w1 = sem("l1_weights_loaded")
        s_sw = sem("small_weights_loaded")
        s_ch = sem("vector_chain")
        s_ac = sem("scalar_chain")
        s_sg = sem("c_silu")
        s_mT = sem("modT_matmuls")
        s_mTc = sem("modT_copied")
        s_mb = sem("mod_rows_matmuls")
        s_mbc = sem("mod_rows_copied")
        s_gm = sem("gates_ready")
        s_cw = sem("joined_weight_matmuls")
        s_cwc = sem("joined_weights_copied")
        s_rope1 = sem("l1_rope_loaded")
        s_q1 = sem("qrope_scaled")
        s_sws = sem("shared_weights_loaded")

        LNS = {}
        for ph in "ABCD":
            names = ["stats", "var", "std", "ready", "turned", "hT"]
            names += ["xn", "mm", "used"] if ph != "D" else ["xn"]
            names += ["free"] if ph == "A" else []
            LNS[ph] = {k: sem(f"{k}_{ph}") for k in names}
        s_fss, s_ffv, s_fft, s_fff = sem("ffn_squares"), sem("ffn_norm"), sem("ffn_tanh"), sem("ffn_done")
        s_rss, s_rms, s_rmsd, s_none = sem("raw_squares"), sem("rms_root_in"), sem("rms_root"), None
        s_qk1, s_qk1t, s_qk1c, s_v1 = sem("l1_rows"), sem("l1_turned"), sem("l1_turned_copied"), sem("l1_values_copied")
        AT = {}
        for L in (0, 1):
            names = ["wos", "vs", "proj", "ropem", "qk", "scores", "nmax", "exp", "turn", "ptA", "ptV", "av", "rinv", "rt",
                     "rs", "ot", "op", "xadd"]
            names += ["wq", "wo"] if L == 0 else ["wqs", "qlow"]
            AT[L] = {k: sem(f"{k}_L{L}") for k in names}
        s_hrow, s_hp = sem("h_rows_made"), sem("h_row_parts")
        s_hst = [sem(f"h_rows_stored_{u}") for u in range(2)]
        s_sct = [sem(f"slots_stored_{u}") for u in range(2)]
        s_xe = [sem(f"expert_rows_{u}") for u in range(2)]
        s_lg, s_lgc, s_sh, s_sact, s_dv, s_shf, s_z, s_zf = (
            sem("logits"), sem("logits_copied"), sem("shared_products"), sem("shared_exp"), sem("shared_chain"),
            sem("shared_hidden"), sem("shared_out"), sem("shared_out_copied"))
        s_sub, s_ex, s_mk, s_pos, s_slot, s_stage = (
            sem("logits_shifted"), sem("exps"), sem("choice_mask"), sem("positions"), sem("slots_made"),
            sem("slots_staged"))
        s_seen = sem("seen_chain")
        s_pad, s_zero, s_tab, s_tok = sem("dram_set"), sem("zero_tile"), sem("table_loaded"), sem("token_ids")
        s_ew = [sem(f"expert_weights_{u}") for u in range(RING)]
        s_tc, s_xt, s_xc, s_gu, s_eg, s_ed, s_eh, s_ht, s_hc, s_y, s_ys, s_add = (
            sem("expert_ids"), sem("expert_turned"), sem("expert_turned_copied"), sem("expert_up"),
            sem("expert_exp"), sem("expert_chain"), sem("expert_hidden"), sem("hidden_turned"), sem("hidden_copied"),
            sem("expert_down"), sem("expert_scaled"), sem("expert_added"))
        s_accl, s_fin, s_out = sem("sums_loaded"), sem("out_ready"), sem("out_stored")

        block = ctx.enter_context(nc.Block())
        xv = a["x"].rearrange("b (t p) m -> p (b t) m", p=P)
        ov = out.rearrange("b (t p) m -> p (b t) m", p=P)

        @block.sync
        def _(sp):
            sp.dma_start(cT[:], a["cT"]).then_inc(s_c, 16)
            sp.dma_start(ident[:], a["ident"]).then_inc(s_c, 16)
            for t, n in ((identb, "identb"), (maskb, "maskb"), (trib, "trib"), (onesb, "onesb"), (iota, "iota"),
                         (dumps, "dumps"), (tokid, "tokid"), (rope, "rope0")):
                sp.dma_start(t[:], a[n]).then_inc(s_c, 16)
            sp.dma_start(X[:], xv).then_inc(s_x, 16)
            sp.dma_start(wmod, a["wmod"]).then_inc(s_wm, 16)
            sp.dma_start(Wv, a["wv"]).then_inc(s_sw, 16)
            sp.dma_start(wqu, a["wqu"]).then_inc(s_w1, 16)
            sp.dma_start(wku, a["wku"]).then_inc(s_w1, 16)
            sp.dma_start(wvu, a["wvu"]).then_inc(s_w1, 16)
            sp.dma_start(wo1, a["wo1"]).then_inc(s_w1, 16)
            sp.dma_start(Wq1[:, :, KVR:D], a["wqr"]).then_inc(s_w1, 16)
            for t, n in ((Wff, "wff"), (Wdown, "wdown"), (gateT, "gateT")):
                sp.dma_start(t[:], a[n]).then_inc(s_sw, 16)
            sp.dma_start(sc_bc[:], a["ffs"].to_broadcast([P, M])).then_inc(s_sw, 16)
            sp.dma_start(qw_bc[:], a["qw"].to_broadcast([P, QR])).then_inc(s_sw, 16)
            sp.dma_start(kvw_bc[:], a["kvw"].to_broadcast([P, KVR])).then_inc(s_sw, 16)
            sp.dma_start(table[0:SLOTS, :].rearrange("(p n) c -> p (n c)", p=P), a["pads"]).then_inc(s_pad, 16)
            s = AT[0]
            with sp.Fori(0, B) as b:
                with sp.Fori(0, G) as g:
                    n = b * G + g
                    sp.wait_ge(s["proj"], n * 5 + 1)
                    sp.dma_start(WQ, a["wq"][g]).then_inc(s["wq"], 16)
                    sp.wait_ge(s["wos"], n + 1)
                    sp.dma_start(WOr, a["wo0"][g]).then_inc(s["wo"], 16)
            sp.wait_ge(s["ropem"], 5 * B * G + 1)
            sp.dma_start(rope, a["rope1"]).then_inc(s_rope1, 16)
            sp.wait_ge(s["qk"], 5 * B * G + 1)
            sp.dma_start(kcs, a["kcs"]).then_inc(s_rope1, 16)
            sp.wait_ge(AT[1]["qk"], 4 * B * G + 1)
            sp.dma_start(sw13, a["sw13"]).then_inc(s_sws, 16)
            sp.dma_start(sw2, a["sw2"]).then_inc(s_sws, 16)
            sp.wait_ge(AT[1]["xadd"], B * G * TT + 1)
            for u in range(RING):
                sp.dma_start(ring[:, u, :], a["we"][u]).then_inc(s_ew[u], 16)
                sp.dma_start(ring2[:, u, :], a["we2"][u]).then_inc(s_ew[u], 16)
            sp.wait_ge(s_zero, 1)
            sp.dma_start(hd[B * T:B * T + P, :], zero).then_inc(s_pad, 16)
            sp.dma_start(acc.rearrange("(t p) m -> p t m", p=P), zero.unsqueeze(1).to_broadcast([P, NT + 1, M])).then_inc(s_pad, 16)
            with sp.Fori(0, NT // 2) as it:
                for u in range(2):
                    sp.wait_ge(s_hrow, it * 2 + (u + 3))
                    sp.dma_start(hd[bass.ds((it * 2 + u) * P, P), :], hrow[:, u, :]).then_inc(s_hst[u], 16)
            for u in range(2):
                sp.wait_ge(s_sct[u], 16 * (NT // 2) * TOPK)
            sp.dma_start(slots, table[0:SLOTS, :].rearrange("(p e) c -> p e c", e=E)).then_inc(s_tab, 16)
            with sp.Fori(1, E // RING) as r:
                for u in range(RING):
                    sp.wait_ge(s_y, (r - 1) * RING + (u + 1))
                    sp.dma_start(ring[:, u, :], a["we"][r * RING + u]).then_inc(s_ew[u], 16)
                    sp.dma_start(ring2[:, u, :], a["we2"][r * RING + u]).then_inc(s_ew[u], 16)
            sp.wait_ge(s_add, 16 * E)
            for b in range(B):
                sp.dma_start(accs[:, b * TT:(b + 1) * TT, :],
                             acc[b * T:(b + 1) * T, :].rearrange("(t p) m -> p t m", p=P)).then_inc(s_accl, 16)
                sp.wait_ge(s_accl, 16 * (b + 1))
            for b in range(B):
                sp.wait_ge(s_fin, b + 1)
                sp.dma_start(ov[:, b * TT:(b + 1) * TT, :], X[:, b * TT:(b + 1) * TT, :]).then_inc(s_out, 16)
            sp.wait_ge(s_out, 32)
            for u in range(2):
                sp.wait_ge(s_hst[u], 16 * (NT // 2) + 16)
            sp.wait_ge(s_pad, 48)

        @block.tensor
        def _(pe):
            mm, tr = nc.tensor.matmul, nc.tensor.transpose
            pe.wait_ge(s_sg, 1)
            pe.wait_ge(s_wm, 16)
            for l in range(2):
                for c in range(12):
                    for k in range(KT):
                        last = mm(mis[:, 24 * l + 2 * c:24 * l + 2 * c + 2], wmod[:, l, k, c * P:(c + 1) * P],
                                  sc[:, k, 2 * l:2 * l + 2], start=(k == 0), stop=(k == KT - 1))
            last.then_inc(s_mT, 1)
            for n, (l, c) in enumerate(((0, 2), (0, 5), (1, 2), (1, 5), (1, 3), (1, 4))):
                if n >= 2:
                    pe.wait_ge(s_mbc, n - 1)
                for b in range(B):
                    for k in range(KT):
                        last = mm(ptp[n % 2][:, b * M:(b + 1) * M], scb[:, k, 2 * l + b, :],
                                  wmod[:, l, k, c * M:(c + 1) * M], start=(k == 0), stop=(k == KT - 1))
                last.then_inc(s_mb, 1)
            pe.wait_ge(s_w1, 80)
            for h in range(16):
                last = mm(sco[0][0:QR, h * KVR:(h + 1) * KVR], wqu[:, h, :], wku[:, h, :], start=True, stop=True)
            last.then_inc(s_cw, 1)
            for h in range(16):
                half = KVR * (h % 2)
                if h % 8 == 0 and h:
                    pe.wait_ge(s_cwc, h // 8 + 1)
                last = mm(sco[1][half:half + KVR, (h // 2) % 4 * M:(h // 2) % 4 * M + M], wvu[:, h, :], wo1[:, h, :],
                          start=True, stop=True)
                if h % 8 == 7:
                    last.then_inc(s_cw, 1)

            def turn_h(ph, t, u):
                s = LNS[ph]
                pe.wait_ge(s["xn"] if ph != "D" else s_hrow, t + 1 if ph != "D" else t + 3)
                src = xn if ph != "D" else hrow
                pe.wait_ge(s["hT"], t + 1)
                for k in range(KT):
                    last = tr(ptp[u][:, k * P:(k + 1) * P], src[:, u, k * P:(k + 1) * P], ident[:])
                last.then_inc(s["turned"], 1)

            def project_h(ph, t, u, W, N, bank):
                s = LNS[ph]
                pe.wait_ge(s["hT"], t + 3)
                pe.wait_ge(s["used"], t + 1)
                for k in range(KT):
                    last = mm(bank[:, 0:N], hTs[:, u, k, :], W[:, k, :], start=(k == 0), stop=(k == KT - 1))
                last.then_inc(s["mm"], 1)

            def attention(L):
                s = AT[L]
                np_ = 5 if L == 0 else 4
                with pe.Fori(0, B) as b:
                    with pe.Fori(0, G) as g:
                        n = b * G + g
                        if L == 0:
                            pe.wait_ge(s["wq"], n * 16 + 16)
                        else:
                            pe.wait_ge(s["wqs"], n + 1)
                        pe.wait_ge(s["exp"], n * NS + 1)
                        for m in range(np_):
                            if m >= 2:
                                pe.wait_ge(s["ropem"], n * np_ + m)
                                if L == 1:
                                    pe.wait_ge(s["qlow"], n * np_ + (m - 1))
                            for half in range(2):
                                o = sco[m % 2][:, half * 512:(half + 1) * 512]
                                cols = bass.ds(b * T + half * 512, 512)
                                if L == 0:
                                    for k in range(KT):
                                        last = mm(o, WQ[:, k, m, :], hT[:, k, cols], start=(k == 0), stop=(k == KT - 1))
                                else:
                                    last = mm(o, WQ[0:QR, 0, m, :], qcT[:, cols], start=True, stop=True)
                            last.then_inc(s["proj"], 1)
                        for kind, i, j, c in STEPS:
                            if kind == "S":
                                if c == 0:
                                    pe.wait_ge(s["qk"], n * np_ + (np_ + 1))
                                if c >= 2:
                                    pe.wait_ge(s["exp"], n * NS + c)
                                o = sco[c % 2]
                                w = (i + 1) * P
                                for c0 in range(0, w, 512):
                                    c1 = min(w, c0 + 512)
                                    k_rhs = Krope[:, c0:c1] if L == 0 else KT1[:, bass.ds(b * T + c0, c1 - c0)]
                                    mm(o[:, c0:c1], QT[:, j, i * P:(i + 1) * P], k_rhs, start=True, stop=(c1 < w))
                                mm(o[:, i * P:w], identb[:], maskb[:], start=False, stop=True).then_inc(s["scores"], 1)
                            elif kind == "T":
                                if j == 0:
                                    pe.wait_ge(s["exp"], n * NS + (HG * i + HG + 1))
                                for h in range(HG):
                                    last = tr(ptp[c % 2][:, h * P:(h + 1) * P], Pr[:, i % 2, h, j * P:(j + 1) * P], ident[:])
                                last.then_inc(s["turn"], 1)
                            elif kind == "A":
                                if c == 0:
                                    pe.wait_ge(s["vs"], n + 1)
                                if c % 2 == 0:
                                    pe.wait_ge(s["ptA"], n * (TURNS // 2) + (c // 2 + 1))
                                else:
                                    pe.wait_ge(s["ptV"], n * (TURNS // 2) + (c // 2 + 1))
                                if L == 0:
                                    last = mm(OTp[:, :], Vs[:, j, :], PTs[:, c % 2, :], start=(j == 0), stop=(j == i))
                                else:
                                    pt = PTs[:, c % 2, :].rearrange("p (a s q) -> p s a q", s=2, q=P)
                                    for half in range(2):
                                        last = mm(OTp[half * 64:half * 64 + 64, 0:256], Vs[:, j, 0:KVR], pt[:, half],
                                                  start=(j == 0), stop=(j == i))
                                if j == i:
                                    last.then_inc(s["av"], 1)
                            elif kind == "R":
                                pe.wait_ge(s["rinv"], n * TT + (i + 1))
                                pe.wait_ge(s["xadd"], n * TT + (i + 1))
                                if L == 0:
                                    for h in range(HG):
                                        last = tr(mis[:, h * P:(h + 1) * P], rinv[:, i % 2, h:h + 1].to_broadcast([P, P]), ident[:])
                                else:
                                    for h in range(2):
                                        last = tr(mis[:, h * P:(h + 1) * P], rinv64[:, i % 2, h * P:(h + 1) * P], ident[:])
                                last.then_inc(s["rt"], 1)
                            else:
                                pe.wait_ge(s["ot"], n * TT + (i + 1))
                                if i == 0:
                                    pe.wait_ge(s["wos"], n + 2)
                                nh = HG if L == 0 else 2
                                for h in range(nh):
                                    last = mm(mis[:, 0:M], OTs[:, h * P:(h + 1) * P], WO[:, h, :], start=(h == 0), stop=(h == nh - 1))
                                last.then_inc(s["op"], 1)

            pe.wait_ge(s_mbc, 6)
            pe.wait_ge(s_mTc, 1)
            with pe.Fori(0, NT // 2) as it:
                for u in range(2):
                    turn_h("A", it * 2 + u, u)
                    if u == 0:
                        pe.wait_ge(s_sw, 16 * 7)
                    project_h("A", it * 2 + u, u, Wv, 512, ps[2 + u])
            pe.wait_ge(LNS["A"]["used"], NT + 2)
            pe.wait_ge(LNS["A"]["free"], NT + 2)
            pe.wait_ge(s_cwc, 3)
            attention(0)
            for ph, W, N in (("B", Wff, M), ("C", Wdown, RAW)):
                with pe.Fori(0, NT // 2) as it:
                    for u in range(2):
                        turn_h(ph, it * 2 + u, u)
                        project_h(ph, it * 2 + u, u, W, N, ps[2 + u])
            pe.wait_ge(LNS["C"]["used"], NT + 2)
            with pe.Fori(0, NT // 2) as it:
                for u in range(2):
                    t = it * 2 + u
                    pe.wait_ge(s_qk1, t + 1)
                    pe.wait_ge(s_qk1c, t + 1)
                    tr(ptp[u][0:QR, 0:P], sq[:, u, 0:QR], ident[:])
                    tr(ptp[u][:, P:2 * P], sq[:, u, P:2 * P], ident[:]).then_inc(s_qk1t, 1)
            pe.wait_ge(s_qk1c, NT + 2)
            attention(1)

            def shared_out(t, u):
                pe.wait_ge(s_shf, t + 3)
                pe.wait_ge(s_zf, t + 1)
                for c in range(3):
                    last = mm(OTp[:, 0:M], actT[:, u, c * P:(c + 1) * P], sw2[:, c, :], start=(c == 0), stop=(c == 2))
                last.then_inc(s_z, 1)

            def ffn_tile(t, u, first):
                turn_h("D", t, u)
                pe.wait_ge(LNS["D"]["hT"], t + 3)
                pe.wait_ge(s_lgc, t + 1)
                for k in range(KT):
                    last = mm(mis[:, 0:E], hTs[:, u, k, :], gateT[:, k, :], start=(k == 0), stop=(k == KT - 1))
                last.then_inc(s_lg, 1)
                pe.wait_ge(s_shf, t + 1)
                for w in range(2):
                    for c in range(3):
                        for k in range(KT):
                            last = mm(sco[u][:, w * 512 + c * P:w * 512 + (c + 1) * P], sw13[:, k, w, c * P:(c + 1) * P],
                                      hTs[:, u, k, :], start=(k == 0), stop=(k == KT - 1))
                last.then_inc(s_sh, 1)
                if not first:
                    shared_out(t - 1, 1 - u)

            pe.wait_ge(s_sws, 32)
            ffn_tile(0, 0, True)
            ffn_tile(1, 1, False)
            with pe.Fori(1, NT // 2) as it:
                for u in range(2):
                    ffn_tile(it * 2 + u, u, False)
            shared_out(NT - 1, 1)
            pe.wait_ge(s_mk, 1)
            for half in range(2):
                tiles = slice(half * 8, half * 8 + 8)
                o = sco[0][:, half * 512:(half + 1) * 512]
                mm(o, trib[:], maskt[:, tiles, :].rearrange("p t e -> p (t e)"), start=True, stop=False)
                if half == 0:
                    pe.wait_ge(s_seen, NT)
                last = mm(o, onesb[:], seen[:, tiles, :].rearrange("p t e -> p (t e)"), start=False, stop=True)
            last.then_inc(s_pos, 1)

            def turn_rows(e, v, half):
                pe.wait_ge(s_xe[v], half * 16 + 16)
                pe.wait_ge(s_xc, e + 1)
                for k in range(KT):
                    last = tr(ptp[v][:, k * P:(k + 1) * P], xe[:, v, k * P:(k + 1) * P], ident[:])
                last.then_inc(s_xt, 1)

            def up(e, v, u, r):
                pe.wait_ge(s_ew[u], r * 32 + 32)
                pe.wait_ge(s_xc, e + 3)
                pe.wait_ge(s_eh, e + 1)
                for k in range(KT):
                    last = mm(sco[v][:, 0:SI], xeT[:, v, k * P:(k + 1) * P], ring[:, u, k * SI:(k + 1) * SI],
                              start=(k == 0), stop=(k == KT - 1))
                last.then_inc(s_gu, 1)

            def turn_hidden(e, v):
                pe.wait_ge(s_eh, e + 3)
                pe.wait_ge(s_hc, e + 1)
                tr(OTp[:, v * 256:v * 256 + P], eh[:, v, 0:P], ident[:])
                tr(OTp[0:I2, v * 256 + P:v * 256 + 2 * P], eh[:, v, P:I], ident[:]).then_inc(s_ht, 1)

            def down(e, v, u):
                pe.wait_ge(s_hc, e + 3)
                pe.wait_ge(s_ys, e + 1)
                mm(mis[:, 0:M], ehT[:, v, 0:P], ring[:, u, 2 * SI:2 * SI + M], start=True, stop=False)
                mm(mis[:, 0:M], ehT[0:I2, v, P:2 * P], ring2[:, u, :], start=False, stop=True).then_inc(s_y, 1)

            def expert_group(r, first=False, last=False):
                for u in range(RING):
                    e = r * RING + u
                    up(e, u % 2, u, r)
                    if not (first and u == 0):
                        turn_hidden(e - 1, (u + 1) % 2)
                    if not (last and u == RING - 1):
                        turn_rows(e + 1, (u + 1) % 2, r * (RING // 2) + (u + 1) // 2)
                    if not (first and u == 0):
                        down(e - 1, (u + 1) % 2, (u - 1) % RING)

            turn_rows(0, 0, 0)
            pe.wait_ge(s_slot, 1)
            expert_group(0, first=True)
            with pe.Fori(1, E // RING - 1) as r:
                expert_group(r)
            expert_group(E // RING - 1, last=True)
            turn_hidden(E - 1, 1)
            down(E - 1, 1, RING - 1)

        @block.scalar
        def _(act):
            af = nc.scalar.activation

            def turned_copies(ph, shift, scale, layer):
                s = LNS[ph]
                with act.Fori(0, B) as b:
                    with act.Fori(0, TT // 2) as it:
                        for u in range(2):
                            t = b * TT + it * 2 + u
                            act.wait_ge(s["turned"], t + 3)
                            act.wait_ge(s["mm"], t + 1)
                            if ph == "A":
                                act.wait_ge(s["free"], t + 1)
                            settle(act, s_act)
                            for k in range(KT):
                                last = af(hTs[:, u, k, :], ptp[u][:, k * P:(k + 1) * P], ACT.Identity,
                                          bias=modT[:, layer, 2 * shift + k, bass.ds(b, 1)],
                                          scale=modT[:, layer, 2 * scale + k, bass.ds(b, 1)])
                            last.then_inc(s["hT"], 1)

            def root(ph):
                act.wait_ge(LNS[ph]["var"], 1)
                af(t16[:, 4, :], t16[:, 3, :], ACT.Sqrt).then_inc(LNS[ph]["std"], 1)

            def attention(L):
                s = AT[L]
                np_ = 5 if L == 0 else 4
                with act.Fori(0, B) as b:
                    with act.Fori(0, G) as g:
                        n = b * G + g
                        if L == 1:
                            for m in range(np_):
                                act.wait_ge(s["proj"], n * np_ + (m + 2))
                                af(QT[0:KVR, m, :], sco[m % 2][0:KVR, :], ACT.Copy).then_inc(s["qlow"], 1)
                        for kind, i, j, c in STEPS:
                            if kind == "S":
                                act.wait_ge(s["nmax"], n * NS + (c + 1))
                                af(Pr[:, i % 2, j, 0:(i + 1) * P], sco[c % 2][:, 0:(i + 1) * P], ACT.Exp,
                                   bias=nmax[:, c % 2:c % 2 + 1], accum_out=rsum[:, i % 2, j:j + 1]).then_inc(s["exp"], 1)
                            elif kind == "T" and c % 2 == 0:
                                act.wait_ge(s["turn"], n * TURNS + (c + 1))
                                af(PTs[:, 0, :], ptp[0][:, :], ACT.Copy).then_inc(s["ptA"], 1)
                            elif kind == "R":
                                act.wait_ge(s["rt"], n * TT + (i + 1))
                                w = HG * P if L == 0 else 2 * P
                                af(Rs[:, 0:w], mis[:, 0:w], ACT.Copy).then_inc(s["rs"], 1)

            act.wait_ge(s_c, 16 * 10)
            af(sg[:], cT[:], ACT.Exp, scale=-1.0).then_inc(s_ac, 1)
            act.wait_ge(s_mT, 1)
            af(modT[:].rearrange("p l c b -> p (l c b)"), mis[:, 0:48], ACT.Copy).then_inc(s_mTc, 1)
            root("A")
            act.wait_ge(s_mTc, 2)
            turned_copies("A", 0, 1, 0)
            attention(0)
            root("B")
            turned_copies("B", 3, 4, 0)
            with act.Fori(0, NT) as t:
                act.wait_ge(LNS["B"]["used"], t + 3)
                settle(act, s_act)
                af(vbig[:, t, M:2 * M], ffo[:, t, :], ACT.Square, accum_out=t16[:, 5, bass.ds(t, 1)]).then_inc(s_fss, 1)
            act.wait_ge(s_fss, NT)
            af(t16[:, 6, :], t16[:, 5, :], ACT.Sqrt).then_inc(s_ffv, 1)
            act.wait_ge(s_ffv, 2)
            af(t16[:, 8, :], t16[:, 7, :], ACT.Tanh).then_inc(s_fft, 1)
            root("C")
            turned_copies("C", 0, 1, 1)
            with act.Fori(0, NT) as t:
                act.wait_ge(LNS["C"]["used"], t + 3)
                settle(act, s_act)
                af(vbig[:, t, 256:256 + QR], raw[:, t, 0:QR], ACT.Square, accum_out=t16[:, 5, bass.ds(t, 1)]).then_inc(s_rss, 1)
                af(vbig[:, t, 384:384 + KVR], raw[:, t, QR:QR + KVR], ACT.Square, accum_out=t16[:, 6, bass.ds(t, 1)]).then_inc(s_rss, 1)
            act.wait_ge(s_rms, 1)
            af(t16[:, 7:9, :], t16[:, 5:7, :], ACT.Sqrt).then_inc(s_rmsd, 1)
            with act.Fori(0, NT // 2) as it:
                for u in range(2):
                    t = it * 2 + u
                    act.wait_ge(s_qk1t, t + 3)
                    settle(act, s_act)
                    af(hT[0:QR, 0, bass.ds(t * P, P)], ptp[u][0:QR, 0:P], ACT.Copy)
                    af(hT[:, 1, bass.ds(t * P, P)], ptp[u][:, P:2 * P], ACT.Copy).then_inc(s_qk1c, 1)
            attention(1)
            root("D")
            with act.Fori(0, NT // 2) as it:
                for u in range(2):
                    t = it * 2 + u
                    act.wait_ge(LNS["D"]["turned"], t + 3)
                    act.wait_ge(s_sh, t + 1)
                    af(hTs[:, u, :, :].rearrange("p k q -> p (k q)"), ptp[u][:, 0:M], ACT.Copy).then_inc(LNS["D"]["hT"], 1)
                    act.wait_ge(s_sh, t + 3)
                    act.wait_ge(s_shf, t + 1)
                    af(actA[:, u, :], sco[u][:, 0:384], ACT.Exp, scale=-1.0).then_inc(s_sact, 1)
            act.wait_ge(s_sub, 1)
            af(prob, lg, ACT.Exp).then_inc(s_ex, 1)

            def rows_copy(e, v):
                act.wait_ge(s_xt, e + 1)
                af(xeT[:, v, :], ptp[v][:, 0:M], ACT.Copy).then_inc(s_xc, 1)

            def expert(e, v, first=False, last=False):
                act.wait_ge(s_gu, e + 1)
                af(eg[:, v, :], sco[v][:, 0:I], ACT.Exp, scale=-1.0).then_inc(s_eg, 1)
                if not last:
                    rows_copy(e + 1, 1 - v)
                if not first:
                    scaled(e - 1, 1 - v)

            def scaled(e, v):
                act.wait_ge(s_y, e + 1)
                if not isinstance(e, int) or e >= 2:
                    act.wait_ge(s_add, e * 16 - 16)
                settle(act, s_act)
                gate = slots[:, e:e + 1, 1] if isinstance(e, int) else slots[:, bass.ds(e, 1), 1]
                af(ys[:, v, :], mis[:, 0:M], ACT.Copy, scale=gate).then_inc(s_ys, 1)

            rows_copy(0, 0)
            expert(0, 0, first=True)
            for e in range(1, 4):
                expert(e, e % 2)
            with act.Fori(2, E // 2 - 1) as it:
                for v in range(2):
                    expert(it * 2 + v, v)
            expert(E - 2, 0)
            expert(E - 1, 1, last=True)
            scaled(E - 1, 1)

        @block.vector
        def _(v):
            ve = nc.vector
            chain = [0]

            def link(ins):
                chain[0] += 1
                ins.then_inc(s_ch, 1)
                v.wait_ge(s_ch, chain[0])

            def statistics(ph):
                s = LNS[ph]
                with v.Fori(0, NT) as t:
                    ve.bn_stats(st[:, t, :], X[:, t, :]).then_inc(s["stats"], 1)
                v.wait_ge(s["stats"], NT)
                link(ve.tensor_tensor(t16[:, 0, :], st[:, :, 1], st[:, :, 4], ALU.add))
                link(ve.tensor_tensor(t16[:, 1, :], st[:, :, 1], st[:, :, 4], ALU.subtract))
                link(ve.tensor_tensor(t16[:, 2, :], st[:, :, 2], st[:, :, 5], ALU.add))
                link(ve.scalar_tensor_tensor(t16[:, 1, :], t16[:, 1, :], 0.25, t16[:, 1, :], ALU.mult, ALU.mult))
                link(ve.scalar_tensor_tensor(t16[:, 2, :], t16[:, 2, :], 1.0 / M, t16[:, 1, :], ALU.mult, ALU.add))
                ve.tensor_scalar(t16[:, 3, :], t16[:, 2, :], LN_EPS, None, ALU.add).then_inc(s["var"], 1)
                v.wait_ge(s["std"], 1)
                link(ve.reciprocal(t16[:, 2, :], t16[:, 4, :]))
                ve.scalar_tensor_tensor(t16[:, 1, :], t16[:, 0, :], -0.5, t16[:, 2, :], ALU.mult, ALU.mult).then_inc(s["ready"], 1)
                v.wait_ge(s["ready"], 1)

            def normalise(ph, t, u, o=None):
                s = LNS[ph]
                v.wait_ge(s["turned"], t + 1)
                ve.tensor_scalar(xn[:, u, :], X[:, t, :], t16[:, 2, bass.ds(t, 1)], t16[:, 1, bass.ds(t, 1)],
                                 ALU.mult, ALU.add).then_inc(s["xn"], 1)

            def attention(L):
                s = AT[L]
                np_ = 5 if L == 0 else 4
                with v.Fori(0, B) as b:
                    with v.Fori(0, G) as g:
                        n = b * G + g
                        for m in range(np_):
                            v.wait_ge(s["proj"], n * np_ + (m + 2))
                            if m >= 2:
                                v.wait_ge(s["qk"], n * np_ + m)
                            src, r = sco[m % 2], rt[:, m % 2]
                            if L == 0:
                                ve.tensor_tensor(r[:, 0, :], src[:, :], rope[:, 0, :], ALU.mult)
                                ve.tensor_tensor(r[0:64, 1, :], src[64:128, :], rope[64:128, 1, :], ALU.mult)
                                ve.tensor_tensor(r[64:128, 1, :], src[0:64, :], rope[0:64, 1, :], ALU.mult).then_inc(s["ropem"], 1)
                            else:
                                ve.tensor_tensor(r[64:128, 0, :], src[64:128, :], rope[64:128, 0, :], ALU.mult)
                                ve.tensor_tensor(r[64:96, 1, :], src[96:128, :], rope[96:128, 1, :], ALU.mult)
                                ve.tensor_tensor(r[96:128, 1, :], src[64:96, :], rope[64:96, 1, :], ALU.mult).then_inc(s["ropem"], 1)
                        for kind, i, j, c in STEPS:
                            if kind == "S":
                                v.wait_ge(s["scores"], n * NS + (c + 1))
                                ve.tensor_reduce(nmax[:, c % 2:c % 2 + 1], sco[c % 2][:, 0:(i + 1) * P], AX.X, ALU.max,
                                                 negate=True).then_inc(s["nmax"], 1)
                            elif kind == "T":
                                if j == 0:
                                    v.wait_ge(s["exp"], n * NS + (HG * i + HG + 1))
                                    if L == 0:
                                        ve.reciprocal(rinv[:, i % 2, :], rsum[:, i % 2, :]).then_inc(s["rinv"], 1)
                                    else:
                                        ve.reciprocal(rinv64[:, i % 2, :].rearrange("p (h d) -> p h d", h=HG),
                                                      rsum[:, i % 2, :].unsqueeze(2).to_broadcast([P, HG, 64])).then_inc(s["rinv"], 1)
                                if c % 2 == 1:
                                    v.wait_ge(s["turn"], n * TURNS + (c + 1))
                                    ve.tensor_copy(PTs[:, 1, :], ptp[1][:, :]).then_inc(s["ptV"], 1)
                            elif kind == "R":
                                v.wait_ge(s["av"], n * TT + (i + 1))
                                v.wait_ge(s["rs"], n * TT + (i + 1))
                                w = HG * P if L == 0 else 2 * P
                                ve.tensor_tensor(OTs[:, 0:w], OTp[:, 0:w], Rs[:, 0:w], ALU.mult).then_inc(s["ot"], 1)
                            elif kind == "O":
                                v.wait_ge(s["op"], n * TT + (i + 1))
                                xt = X[:, bass.ds(b * TT + i, 1), :].rearrange("p a m -> p (a m)")
                                ve.tensor_tensor(xt, mis[:, 0:M], xt, ALU.add).then_inc(s["xadd"], 1)

            v.wait_ge(s_ac, 1)
            v.wait_ge(s_c, 16 * 10)
            link(ve.tensor_scalar(sg[:], sg[:], 1.0, None, ALU.add))
            link(ve.reciprocal(sg[:], sg[:]))
            link(ve.tensor_tensor(sc[:], sg[:], cT[:], ALU.mult))
            ve.tensor_copy(scb, sc[:].unsqueeze(3).to_broadcast([P, KT, 4, P])).then_inc(s_sg, 1)
            v.wait_ge(s_x, 16)
            statistics("A")
            v.wait_ge(s_mTc, 1)
            for l in range(2):
                for c in (1, 4):
                    last = ve.tensor_scalar(modT[:, l, 2 * c:2 * c + 2, :], modT[:, l, 2 * c:2 * c + 2, :], 1.0, None, ALU.add)
            last.then_inc(s_mTc, 1)
            for n in range(6):
                v.wait_ge(s_mb, n + 1)
                src = ptp[n % 2][:, :].rearrange("p (b m) -> p b m", b=B)
                if n < 4:
                    ve.tensor_copy(gm[:, n], src).then_inc(s_mbc, 1)
                else:
                    ve.tensor_scalar(sm[:, n - 4], src, float(n - 4), None, ALU.add).then_inc(s_mbc, 1)
            v.wait_ge(s_mbc, 6)
            link(ve.tensor_scalar(gs, gm[:], 0.0, 2.0, ALU.is_ge, ALU.mult))
            gf = gm[:].rearrange("p a b m -> p (a b m)")
            link(ve.scalar_tensor_tensor(gf, gf, -1.0, gf, ALU.mult, ALU.max))
            link(ve.tensor_scalar(gf, gf, 0.25, None, ALU.max))
            ve.scalar_tensor_tensor(gm[:].rearrange("p a b m -> p (a b m)"), gs.rearrange("p a b m -> p (a b m)"), -1.0,
                                    gm[:].rearrange("p a b m -> p (a b m)"), ALU.add, ALU.mult).then_inc(s_gm, 1)
            v.wait_ge(s_cw, 1)
            ve.tensor_scalar(Wq1[:, :, 0:KVR], sco[0][0:QR, :].rearrange("p (h n) -> p h n", h=16), L1_SCALE, None,
                             ALU.mult).then_inc(s_cwc, 1)
            v.wait_ge(s_w1, 80)
            ve.tensor_scalar(Wq1[:, :, KVR:D], Wq1[:, :, KVR:D], L1_SCALE, None, ALU.mult).then_inc(s_q1, 1)
            for n in range(2):
                v.wait_ge(s_cw, n + 2)
                ve.tensor_copy(Wvo[:, 4 * n:4 * n + 4, :], sco[1][:, :].rearrange("p (h m) -> p h m", h=4)).then_inc(s_cwc, 1)

            with v.Fori(0, NT // 2) as it:
                for u in range(2):
                    t = it * 2 + u
                    normalise("A", t, u)
                    v.wait_ge(LNS["A"]["mm"], t + 3)
                    ve.tensor_copy(vbig[:, t, :], ps[2 + u][:, :]).then_inc(LNS["A"]["used"], 1)
            attention(0)
            v.wait_ge(AT[0]["xadd"], B * G * TT + 1)
            statistics("B")
            with v.Fori(0, NT // 2) as it:
                for u in range(2):
                    t = it * 2 + u
                    normalise("B", t, u)
                    v.wait_ge(LNS["B"]["mm"], t + 3)
                    ve.tensor_tensor(ffo[:, t, :], ps[2 + u][:, 0:M], sc_bc[:], ALU.mult).then_inc(LNS["B"]["used"], 1)
            v.wait_ge(s_ffv, 1)
            ve.tensor_scalar(t16[:, 7, :], t16[:, 6, :], HYP_EPS, None, ALU.max).then_inc(s_ffv, 1)
            v.wait_ge(s_ffv, 2)
            link(ve.tensor_scalar(t16[:, 9, :], t16[:, 7, :], HYP_EPS, None, ALU.add))
            link(ve.reciprocal(t16[:, 9, :], t16[:, 9, :]))
            v.wait_ge(s_fft, 1)
            link(ve.tensor_tensor(t16[:, 9, :], t16[:, 9, :], t16[:, 8, :], ALU.mult))
            link(ve.tensor_tensor(t16[:, 10, :], t16[:, 9, :], t16[:, 6, :], ALU.mult))
            link(ve.tensor_scalar(t16[:, 10, :], t16[:, 10, :], HYP_EPS, None, ALU.max))
            link(ve.reciprocal(t16[:, 10, :], t16[:, 10, :]))
            link(ve.tensor_scalar(t16[:, 10, :], t16[:, 10, :], MAX_NORM, 1.0, ALU.mult, ALU.min))
            link(ve.tensor_tensor(t16[:, 9, :], t16[:, 9, :], t16[:, 10, :], ALU.mult))
            v.wait_ge(s_fss, NT)
            with v.Fori(0, B) as b:
                with v.Fori(0, TT) as it:
                    t = b * TT + it
                    ft = ffo[:, bass.ds(t, 1), :].rearrange("p a m -> p (a m)")
                    gb = gm[:, 1, bass.ds(b, 1), :].rearrange("p a m -> p (a m)")
                    ve.scalar_tensor_tensor(ft, ft, t16[:, 9, bass.ds(t, 1)], gb, ALU.mult, ALU.mult).then_inc(s_fff, 1)
            v.wait_ge(s_fff, NT)
            link(ve.tensor_tensor(X[:], X[:], ffo, ALU.add))
            statistics("C")
            with v.Fori(0, NT // 2) as it:
                for u in range(2):
                    t = it * 2 + u
                    normalise("C", t, u)
                    v.wait_ge(LNS["C"]["mm"], t + 3)
                    ve.tensor_copy(raw[:, t, :], ps[2 + u][:, 0:RAW]).then_inc(LNS["C"]["used"], 1)
            v.wait_ge(s_rss, 2 * NT)
            link(ve.tensor_scalar(t16[:, 5, :], t16[:, 5, :], 1.0 / QR, RMS_EPS, ALU.mult, ALU.add))
            ve.tensor_scalar(t16[:, 6, :], t16[:, 6, :], 1.0 / KVR, RMS_EPS, ALU.mult, ALU.add).then_inc(s_rms, 1)
            v.wait_ge(s_rope1, 32)
            for b in range(B):
                tiles = slice(b * TT, (b + 1) * TT)
                x1, x2 = raw[:, tiles, QR + KVR:QR + KVR + 32], raw[:, tiles, QR + KVR + 32:RAW]
                ve.tensor_tensor(rope_a[:, tiles, :], raw[:, tiles, QR + KVR:RAW], kcs[:, 0], ALU.mult)
                ve.tensor_tensor(rope_b[:, tiles, 0:32], x2, kcs[:, 1, :, 0:32], ALU.mult)
                last = ve.tensor_tensor(rope_b[:, tiles, 32:64], x1, kcs[:, 1, :, 32:64], ALU.mult)
            link(last)
            v.wait_ge(s_rmsd, 1)
            link(ve.reciprocal(t16[:, 5:7, :], t16[:, 7:9, :]))
            with v.Fori(0, NT // 2) as it:
                for u in range(2):
                    t = it * 2 + u
                    v.wait_ge(s_qk1t, t + 1)
                    v.wait_ge(s_v1, t + 1)
                    ve.scalar_tensor_tensor(sq[:, u, 0:QR], raw[:, t, 0:QR], t16[:, 5, bass.ds(t, 1)], qw_bc[:],
                                            ALU.mult, ALU.mult)
                    ve.scalar_tensor_tensor(sq[:, u, P:P + KVR], raw[:, t, QR:QR + KVR], t16[:, 6, bass.ds(t, 1)], kvw_bc[:],
                                            ALU.mult, ALU.mult)
                    ve.tensor_tensor(sq[:, u, P + KVR:2 * P], rope_a[:, t, :], rope_b[:, t, :], ALU.add).then_inc(s_qk1, 1)
            attention(1)
            v.wait_ge(AT[1]["xadd"], B * G * TT + 1)
            statistics("D")
            ve.memset(actT, 0.0).then_inc(s_dv, 1)
            v.wait_ge(s_dv, 1)

            def ffn_tile(t, u, first):
                v.wait_ge(s_lg, t + 1)
                ve.tensor_copy(lg[:, bass.ds(t, 1), :].rearrange("p a e -> p (a e)"), mis[:, 0:E]).then_inc(s_lgc, 1)
                v.wait_ge(s_sact, t + 1)
                v.wait_ge(s_shf, t + 2)
                ve.tensor_scalar(actB, actA[:, u, :], 1.0, None, ALU.add).then_inc(s_dv, 1)
                v.wait_ge(s_dv, t * 3 + 2)
                ve.reciprocal(actA[:, u, :], actB).then_inc(s_dv, 1)
                v.wait_ge(s_dv, t * 3 + 3)
                ve.tensor_tensor(actB, actA[:, u, :], sco[u][:, 0:384], ALU.mult).then_inc(s_dv, 1)
                v.wait_ge(s_dv, t * 3 + 4)
                ve.tensor_tensor(actT[:, u, :], actB, sco[u][:, 512:896], ALU.mult).then_inc(s_shf, 1)
                if not first:
                    shared_copy(t - 1)

            def rows(t, u):
                v.wait_ge(s_hrow, t + 1)
                ve.tensor_scalar(xn[:, u, :], X[:, bass.ds(t, 1), :].rearrange("p a m -> p (a m)"), t16[:, 2, bass.ds(t, 1)],
                                 t16[:, 1, bass.ds(t, 1)], ALU.mult, ALU.add).then_inc(LNS["D"]["xn"], 1)

            def shared_copy(t):
                v.wait_ge(s_z, t + 1)
                ve.tensor_copy(zall[:, bass.ds(t, 1), :].rearrange("p a m -> p (a m)"), OTp[:, 0:M]).then_inc(s_zf, 1)

            rows(0, 0)
            rows(1, 1)
            ffn_tile(0, 0, True)
            rows(2, 0)
            ffn_tile(1, 1, False)
            with v.Fori(1, NT // 2 - 1) as it:
                for u in range(2):
                    rows(it * 2 + (u + 1), 1 - u)
                    ffn_tile(it * 2 + u, u, False)
            rows(NT - 1, 1)
            ffn_tile(NT - 2, 0, False)
            ffn_tile(NT - 1, 1, False)
            shared_copy(NT - 1)
            v.wait_ge(s_lgc, NT + 1)
            link(ve.tensor_reduce(t16[:, 5, :], lg, AX.X, ALU.max))
            ve.tensor_tensor(lg, lg, t16[:, 5, :].unsqueeze(2).to_broadcast([P, NT, E]), ALU.subtract).then_inc(s_sub, 1)
            v.wait_ge(s_ex, 1)
            link(ve.tensor_reduce(t16[:, 6, :], prob, AX.X, ALU.add))
            link(ve.reciprocal(t16[:, 7, :], t16[:, 6, :]))
            link(ve.tensor_tensor(prob, prob, t16[:, 7, :].unsqueeze(2).to_broadcast([P, NT, E]), ALU.mult))
            for t in range(NT):
                last = ve.max(top8[:, t, :], prob[:, t, :])
            link(last)
            for t in range(NT):
                last = ve.max_index(idx8[:, t, :], top8[:, t, :], prob[:, t, :])
            link(last)
            link(ve.tensor_copy(idxf, idx8))
            all_ = [P, NT, TOPK, E]
            link(ve.tensor_tensor(oh, iota[:].unsqueeze(1).unsqueeze(1).to_broadcast(all_),
                                  idxf[:, :, 0:TOPK].unsqueeze(3).to_broadcast(all_), ALU.is_equal))
            with nc.allow_low_precision("counts up to 16 are exact"):
                ve.tensor_reduce(maskt, oh.rearrange("p t k e -> p t e k"), AX.X, ALU.add).then_inc(s_mk, 1)
            ve.memset(seen[:, 0, :], 0.0).then_inc(s_seen, 1)
            v.wait_ge(s_mk, 1)
            for t in range(1, NT):
                v.wait_ge(s_seen, t)
                ve.tensor_tensor(seen[:, t, :], seen[:, t - 1, :], maskt[:, t - 1, :], ALU.add).then_inc(s_seen, 1)
            v.wait_ge(s_pos, 1)
            link(ve.tensor_tensor(ohm, oh, sco[0][:, :].rearrange("p (t e) -> p t e", t=NT).unsqueeze(2).to_broadcast(all_),
                                  ALU.mult))
            link(ve.tensor_reduce(posk, ohm, AX.X, ALU.add))
            link(ve.tensor_scalar(over, posk, float(CAP), None, ALU.is_ge))
            link(ve.scalar_tensor_tensor(slotf, posk, float(E), idxf[:, :, 0:TOPK], ALU.mult, ALU.add))
            link(ve.tensor_tensor(posk, dumps[:], slotf, ALU.subtract))
            link(ve.tensor_tensor(posk, posk, over, ALU.mult))
            link(ve.tensor_tensor(slotf, slotf, posk, ALU.add))
            ve.tensor_copy(slotu, slotf)
            ve.tensor_copy(pay[:, :, :, 0], tokid[:].unsqueeze(2).to_broadcast([P, NT, TOPK]))
            ve.tensor_copy(pay[:, :, :, 1], top8[:, :, 0:TOPK]).then_inc(s_slot, 1)
            v.wait_ge(s_zf, NT + 1)
            for b in range(B):
                tiles = slice(b * TT, (b + 1) * TT)
                link(ve.tensor_tensor(zall[:, tiles, :], zall[:, tiles, :],
                                      gm[:, 3, b, :].unsqueeze(1).to_broadcast([P, TT, M]), ALU.mult))
                link(ve.tensor_tensor(X[:, tiles, :], X[:, tiles, :], zall[:, tiles, :], ALU.add))
            v.wait_ge(s_tab, 16)
            ve.tensor_copy(toku[:], slots[:, :, 0]).then_inc(s_tok, 1)

            def hidden_copy(e, w):
                v.wait_ge(s_ht, e + 1)
                ve.tensor_copy(ehT[:, w, 0:P], OTp[:, w * 256:w * 256 + P])
                ve.tensor_copy(ehT[0:I2, w, P:2 * P], OTp[0:I2, w * 256 + P:w * 256 + 2 * P]).then_inc(s_hc, 1)

            def expert(e, w, first=False):
                if not first:
                    hidden_copy(e - 1, 1 - w)
                v.wait_ge(s_eg, e + 1)
                v.wait_ge(s_eh, e + 1)
                ve.tensor_scalar(eh[:, w, :], eg[:, w, :], 1.0, None, ALU.add).then_inc(s_ed, 1)
                v.wait_ge(s_ed, e * 3 + 1)
                ve.reciprocal(eg[:, w, :], eh[:, w, :]).then_inc(s_ed, 1)
                v.wait_ge(s_ed, e * 3 + 2)
                ve.tensor_tensor(eg[:, w, :], eg[:, w, :], sco[w][:, 0:I], ALU.mult).then_inc(s_ed, 1)
                v.wait_ge(s_ed, e * 3 + 3)
                ve.tensor_tensor(eh[:, w, :], eg[:, w, :], sco[w][:, I:2 * I], ALU.mult).then_inc(s_eh, 1)

            expert(0, 0, first=True)
            expert(1, 1)
            with v.Fori(1, E // 2) as it:
                for w in range(2):
                    expert(it * 2 + w, w)
            hidden_copy(E - 1, 1)
            for b in range(B):
                v.wait_ge(s_accl, 16 * (b + 1))
                tiles = slice(b * TT, (b + 1) * TT)
                link(ve.tensor_tensor(accs[:, tiles, :], accs[:, tiles, :], gm[:, 3, b, :].unsqueeze(1).to_broadcast([P, TT, M]), ALU.mult))
                ve.tensor_tensor(X[:, tiles, :], X[:, tiles, :], accs[:, tiles, :], ALU.add).then_inc(s_fin, 1)

        @block.gpsimd
        def _(pool):
            gp = nc.gpsimd
            for ph in "ABCD":
                s = LNS[ph]
                for k in ("turned", "mm", "used", "free", "hT"):
                    if k in s:
                        pool.sem_inc(s[k], 2)
            for L in (0, 1):
                s = AT[L]
                for k in ("proj", "exp", "ropem", "qk", "xadd", "wos"):
                    pool.sem_inc(s[k], 1)
            for s, k in ((s_qk1c, 2), (s_qk1t, 2), (s_v1, 2), (s_hrow, 2), (s_lgc, 1), (s_shf, 2), (s_zf, 1), (s_sh, 2), (s_hst[0], 16), (s_hst[1], 16),
                         (s_xc, 2), (s_eh, 2), (s_hc, 2), (s_ys, 1)):
                pool.sem_inc(s, k)

            def copies(ph, dst):
                s = LNS[ph]
                with pool.Fori(0, NT // 2) as it:
                    for u in range(2):
                        t = it * 2 + u
                        pool.wait_ge(s["hT"], t + 3)
                        gp.tensor_copy(hT[:, :, bass.ds(t * P, P)], hTs[:, u]).then_inc(s["free"], 1)

            def attention(L):
                s = AT[L]
                np_ = 5 if L == 0 else 4
                with pool.Fori(0, B) as b:
                    with pool.Fori(0, G) as g:
                        n = b * G + g
                        if L == 1:
                            pool.wait_ge(s["proj"], n * np_ + 1)
                            gp.tensor_copy(WQ[0:QR, 0, 0:HG, :], Wq1[:, bass.ds(g * HG, HG), :]).then_inc(s["wqs"], 1)
                        pool.wait_ge(s["proj"], n * np_ + 2)
                        if L == 0:
                            gp.tensor_copy(Vs, vbig[:, bass.ds(b * TT, TT), bass.ds(g * D, D)]).then_inc(s["vs"], 1)
                        else:
                            gp.tensor_copy(Vs[:, :, 0:KVR], V1[:, bass.ds(b * TT, TT), :]).then_inc(s["vs"], 1)
                        if L == 0:
                            for m in range(np_):
                                pool.wait_ge(s["ropem"], n * np_ + (m + 2))
                                r = rt[:, m % 2]
                                dst = QT[:, m, :] if m < HG else Krope
                                gp.tensor_tensor(dst, r[:, 0, :], r[:, 1, :], ALU.add).then_inc(s["qk"], 1)
                        else:
                            pool.wait_ge(s["vs"], n + 1)
                            for m in range(np_):
                                pool.wait_ge(s["ropem"], n * np_ + (m + 2))
                                pool.wait_ge(s["qlow"], n * np_ + (m + 1))
                                r = rt[:, m % 2]
                                gp.tensor_tensor(QT[64:128, m, :], r[64:128, 0, :], r[64:128, 1, :], ALU.add).then_inc(s["qk"], 1)
                        nh = HG if L == 0 else 2
                        if L == 0:
                            pool.wait_ge(s["wo"], n * 16 + 16)
                        else:
                            pool.wait_ge(s["qk"], n * np_ + (np_ + 1))
                        for h in range(nh):
                            src = WOr[:, h, :] if L == 0 else Wvo[:, bass.ds(g * 2 + h, 1), :].rearrange("p a m -> p (a m)")
                            ga = gm[:, 0 if L == 0 else 2, bass.ds(b, 1), :].rearrange("p a m -> p (a m)")
                            last = gp.tensor_tensor(WO[:, h, :], src, ga, ALU.mult)
                        last.then_inc(s["wos"], 1)

            copies("A", None)
            pool.wait_ge(s_gm, 1)
            attention(0)
            with pool.Fori(0, NT // 2) as it:
                for u in range(2):
                    t = it * 2 + u
                    pool.wait_ge(s_qk1, t + 1)
                    gp.tensor_copy(V1[:, t, :], sq[:, u, P:P + KVR]).then_inc(s_v1, 1)
            pool.wait_ge(s_v1, NT + 2)
            pool.wait_ge(s_cwc, 3)
            pool.wait_ge(s_q1, 1)
            attention(1)
            pool.wait_ge(AT[1]["xadd"], B * G * TT + 1)
            gp.memset(zero, 0.0).then_inc(s_zero, 1)
            with pool.Fori(0, B) as b:
                with pool.Fori(0, TT // 2) as it:
                    for u in range(2):
                        t = b * TT + it * 2 + u
                        one_cb = sm[:, 1, bass.ds(b, 1), :].rearrange("p a m -> p (a m)")
                        sb_row = sm[:, 0, bass.ds(b, 1), :].rearrange("p a m -> p (a m)")
                        pool.wait_ge(LNS["D"]["xn"], t + 1)
                        settle(pool, s_pool)
                        gp.tensor_tensor(xn[:, u, :], xn[:, u, :], one_cb, ALU.mult).then_inc(s_hp, 1)
                        pool.wait_ge(s_hp, t + 1)
                        pool.wait_ge(LNS["D"]["turned"], t + 1)
                        pool.wait_ge(s_hst[u], (b * (TT // 2) + it) * 16 + 16)
                        settle(pool, s_pool)
                        gp.tensor_tensor(hrow[:, u, :], xn[:, u, :], sb_row, ALU.add).then_inc(s_hrow, 1)
            pool.wait_ge(s_slot, 1)
            pool.wait_ge(s_pad, 48)

            def scatter(t, it, u, first=False):
                if not first:
                    pool.wait_ge(s_sct[u], it * (16 * TOPK))
                gp.tensor_copy(slotc[:, u, :], slotu[:, t, :])
                gp.tensor_copy(payc[:, u].rearrange("p k c -> p (k c)"), pay[:, t].rearrange("p k c -> p (k c)")).then_inc(s_stage, 1)
                pool.wait_ge(s_stage, t + 1)
                settle(pool, s_pool)
                for k in range(TOPK):
                    gp.indirect_dma_start(table, bass.IndirectOffsetOnAxis(slotc[:, u, k:k + 1], 0), payc[:, u, k, :], None)\
                      .then_inc(s_sct[u], 16)

            scatter(0, 0, 0, first=True)
            scatter(1, 0, 1, first=True)
            with pool.Fori(1, NT // 2) as it:
                for u in range(2):
                    scatter(it * 2 + u, it, u)
            pool.wait_ge(s_tok, 1)
            for u in range(2):
                pool.wait_ge(s_hst[u], 16 * (NT // 2) + 16)

            def gather(e, v, w):
                gp.tensor_copy(tokc[:, w:w + 1], toku[:, bass.ds(e, 1)]).then_inc(s_tc, 1)
                pool.wait_ge(s_tc, e + 1)
                settle(pool, s_pool)
                gp.indirect_dma_start(xe[:, v, :], None, hd, bass.IndirectOffsetOnAxis(tokc[:, w:w + 1], 0)).then_inc(s_xe[v], 16)

            def add(e, v, w, first=False):
                pool.wait_ge(s_ys, e + 2)
                if not first:
                    pool.wait_ge(s_add, e * 16)
                settle(pool, s_pool)
                gp.indirect_dma_start(acc, bass.IndirectOffsetOnAxis(tokc[:, w:w + 1], 0), ys[:, v, :], None,
                                      compute_op=ALU.add).then_inc(s_add, 16)

            gather(0, 0, 0)
            gather(1, 1, 1)

            def expert(e, w, first=False, last=False):
                if not last:
                    pool.wait_ge(s_xt, e + 1)
                    gather(e + 2, w % 2, (w + 2) % 4)
                add(e, w % 2, w, first)

            for w in range(4):
                expert(w, w, first=(w == 0))
            with pool.Fori(1, E // 4 - 1) as it:
                for w in range(4):
                    expert(it * 4 + w, w)
            for w in range(4):
                expert(E - 4 + w, w, last=(w >= 2))


def _layouts(np, z):
    f = lambda a: np.ascontiguousarray(a)
    kp = lambda w: f(w.reshape(w.shape[0] // 128, 128, -1).transpose(1, 0, 2))
    a = {"x": f(z["L0_attn_x"])}
    a["cT"] = f(np.concatenate([z["L0_c"], z["L1_c"]], 0).T.reshape(2, 128, 4).transpose(1, 0, 2))
    a["wmod"] = f(np.stack([z["L0_wmod"], z["L1_wmod"]]).reshape(2, 2, 128, 1536).transpose(2, 0, 1, 3))
    wq = z["L0_attn_w_aq"].reshape(4, 4, 2, 128, 128).transpose(0, 3, 2, 1, 4)
    wk = z["L0_attn_w_ak"].reshape(4, 1, 2, 128, 128).transpose(0, 3, 2, 1, 4)
    a["wq"] = f(np.concatenate([wq, wk], 3))
    a["wv"] = f(z["L0_attn_w_av"].transpose(1, 0, 2).reshape(2, 128, 512).transpose(1, 0, 2))
    a["wo0"] = f(z["L0_attn_w_ao"].transpose(0, 2, 1, 3))
    a["wff"] = kp(z["L0_ffn_weight"])
    a["ffs"] = f(z["L0_ffn_scale"].reshape(1, 256))
    halves = np.r_[0:64:2, 1:64:2]
    a["wdown"] = kp(np.concatenate([z["L1_attn_wq_down"], z["L1_attn_wkv_down"], z["L1_attn_wk_rope"][:, halves]], 1))
    a["qw"], a["kvw"] = f(z["L1_attn_q_norm_w"].reshape(1, 96)), f(z["L1_attn_kv_norm_w"].reshape(1, 64))
    a["wqu"] = f(z["L1_attn_wq_up"].reshape(96, 16, 128).transpose(2, 1, 0))
    kv = z["L1_attn_wkv_up"].reshape(64, 16, 256)
    a["wku"], a["wvu"] = f(kv[:, :, :128].transpose(2, 1, 0)), f(kv[:, :, 128:].transpose(2, 1, 0))
    a["wo1"] = f(z["L1_attn_wo"].reshape(16, 128, 256).transpose(1, 0, 2))
    a["wqr"] = f(z["L1_attn_wq_rope"].reshape(96, 16, 64)[:, :, halves])
    a["gateT"] = kp(z["L1_ffn_gate_w"].T)
    sw = np.zeros((128, 2, 2, 384), np.float32)
    for w, n in enumerate(("L1_ffn_sw1", "L1_ffn_sw3")):
        sw[:, :, w, :352] = kp(z[n].T)
    a["sw13"] = sw
    sw2 = np.zeros((384, 256), np.float32)
    sw2[:352] = z["L1_ffn_sw2"].T
    a["sw2"] = kp(sw2)
    w13 = np.concatenate([z["L1_ffn_w1"], z["L1_ffn_w3"]], 1).transpose(0, 2, 1).reshape(64, 2, 128, 352).transpose(0, 2, 1, 3)
    w2 = z["L1_ffn_w2"].transpose(0, 2, 1)
    a["we"] = f(np.concatenate([w13.reshape(64, 128, 704), w2[:, :128]], 2))
    a["we2"] = f(w2[:, 128:])
    return a


def _constants(np):
    bf = np.dtype("bfloat16")
    c = {"ident": np.eye(128, dtype=np.float32), "identb": np.eye(128).astype(bf)}
    c["maskb"] = np.where(np.arange(128)[:, None] < np.arange(128)[None, :], -1e30, 0.0).astype(bf)
    c["trib"] = np.triu(np.ones((128, 128)), 1).astype(bf)
    c["onesb"] = np.ones((128, 128)).astype(bf)
    c["iota"] = np.tile(np.arange(64, dtype=np.float32), (128, 1))
    p, t, k = np.ogrid[0:128, 0:16, 0:6]
    c["dumps"] = (8192 + (t * 6 + k) * 128 + p).astype(np.float32)
    c["tokid"] = (np.arange(16)[None, :] * 128 + np.arange(128)[:, None]).astype(np.float32)
    pads = np.zeros((128, 64, 2), np.float32)
    pads[:, :, 0] = 2048 + np.arange(128)[:, None]
    c["pads"] = pads.reshape(128, 128)
    pos = np.arange(1024, dtype=np.float32)
    f0 = np.power(np.float32(10000.0), -np.arange(64, dtype=np.float32) / np.float32(64))
    ang = (pos[:, None] * f0[None, :]).astype(np.float32).astype(np.float64).T
    q = 128 ** -0.25
    r0 = np.zeros((128, 2, 1024), np.float32)
    r0[:64, 0] = r0[64:, 0] = np.cos(ang) * q
    r0[:64, 1] = np.sin(ang) * q
    r0[64:, 1] = -np.sin(ang) * q
    c["rope0"] = r0
    f1 = (np.float32(1.0) / np.power(np.float32(10000.0), np.arange(0, 64, 2, dtype=np.float32) / np.float32(64))).astype(np.float32)
    ang = (pos[:, None] * f1[None, :]).astype(np.float32).astype(np.float64)
    cos, sin = np.cos(ang), np.sin(ang)
    r1 = np.zeros((128, 2, 1024), np.float32)
    r1[64:96, 0] = r1[96:, 0] = cos.T
    r1[64:96, 1], r1[96:, 1] = sin.T, -sin.T
    c["rope1"] = r1
    k = np.zeros((128, 2, 8, 64), np.float32)
    cs, sn = (m.reshape(8, 128, 32).transpose(1, 0, 2) for m in (cos, sin))
    k[:, 0, :, :32] = k[:, 0, :, 32:] = cs
    k[:, 1, :, :32], k[:, 1, :, 32:] = -sn, sn
    c["kcs"] = k
    return c


def kernel(**inputs):
    import numpy as np
    import concourse.bacc as bacc
    from concourse.bass_utils import run_bass_kernel_spmd

    nc = bacc.Bacc("TRN2", target_bir_lowering=False, num_devices=1)
    arrays = {**_layouts(np, {k: np.asarray(v) for k, v in inputs.items()}), **_constants(np)}
    aps = {k: nc.dram_tensor(f"in_{k}", v.shape, mybir.dt.from_np(v.dtype), kind="ExternalInput").ap() for k, v in arrays.items()}
    out = nc.dram_tensor("out_x", (B, T, M), F32, kind="ExternalOutput").ap()
    program(nc, aps, out)
    r = run_bass_kernel_spmd(nc, [{f"in_{k}": v for k, v in arrays.items()}], core_ids=[0])
    return r.results[0]["out_x"]
```

```python
from contextlib import ExitStack

import concourse.bass as bass
from concourse import mybir

F32 = mybir.dt.float32
BF16 = mybir.dt.bfloat16
U32 = mybir.dt.uint32
ALU = mybir.AluOpType
ACT = mybir.ActivationFunctionType
AX = mybir.AxisListType

P = 128
B, T, M = 2, 1024, 256
KT = M // P
TT = T // P
NT = B * TT
G, HG = 4, 4
D = 128
QR, KVR, DR, DV = 96, 64, 64, 128
RAW = QR + KVR + DR
E, I, TOPK, CAP = 64, 176, 6, 128
I2 = I - P
SI = 352
UP = 2 * P + 64 + I2
WE = KT * UP + M
RING = 8
LN_EPS, RMS_EPS, HYP_EPS, MAX_NORM = 1e-5, 1e-6, 1e-7, 0.99
L1_SCALE = float((128 + DR) ** -0.5)


def attention_steps():
    steps, turn = [], 0
    for i in range(TT + 1):
        work = []
        if i:
            for j in range(i):
                work.append(("T", i - 1, j, turn + j))
                if j:
                    work.append(("A", i - 1, j - 1, turn + j - 1))
            work.append(("A", i - 1, i - 1, turn + i - 1))
            work.append(("R", i - 1, 0, 0))
            turn += i
        done = 0
        for h in range(HG):
            if i < TT:
                steps.append(("S", i, h, HG * i + h))
            if h == 0 and i >= 2:
                steps.append(("O", i - 2, 0, 0))
            upto = len(work) * (h + 1) // HG
            steps += work[done:upto]
            done = upto
    steps.append(("O", TT - 1, 0, 0))
    return steps, turn


STEPS, TURNS = attention_steps()
NS = HG * TT


def settle(eng, passed):
    eng.sem_inc(passed, 1)


def program(nc, a, out):
    with ExitStack() as ctx:
        def sb(name, shape, dt=F32):
            return ctx.enter_context(nc.sbuf_tensor(name, shape, dt))

        def sem(name):
            return ctx.enter_context(nc.semaphore(name))

        hd = nc.dram_tensor("h_rows", (B * T + P, M), F32, kind="Internal").ap()
        accd = [nc.dram_tensor(f"routed_sum_{u}", (B * T + P, M), F32, kind="Internal").ap() for u in range(2)]

        X = sb("X", [P, NT, M])
        big = sb("big", [P, 13312])
        hT = sb("hT", [P, KT, B * T])
        vbig = sb("vbig", [P, NT, 512])
        ident = sb("ident", [P, P])
        identb = sb("identb", [P, P], BF16)
        maskb = sb("maskb", [P, P], BF16)
        trib = sb("trib", [P, P], BF16)
        onesb = sb("onesb", [P, P], BF16)
        iota = sb("iota", [P, CAP])
        padid = sb("padid", [P, 1])
        tokid = sb("tokid", [P, NT])
        att = sb("att", [P, 10496])
        rope = att[:, 0:2048].rearrange("p (w t) -> p w t", w=2)
        Wq1 = att[0:QR, 2048:4096].rearrange("p (h n) -> p h n", h=16)
        Wvo = att[:, 4096:6144].rearrange("p (h m) -> p h m", h=8)
        WQ = att[:, 6144:7424].rearrange("p (k h d) -> p k h d", k=KT, h=HG + 1)
        WOr = att[:, 7424:8448].rearrange("p (h m) -> p h m", h=HG)
        rinv64 = att[:, 7424:7936].rearrange("p (u n) -> p u n", u=2)
        WO = att[:, 8448:9472].rearrange("p (h m) -> p h m", h=HG)
        Vs = att[:, 9472:10496].rearrange("p (t d) -> p t d", t=TT)
        ring = att[:, 0:RING * WE].rearrange("p (u n) -> p u n", u=RING)
        ring2 = att[0:I2, RING * WE:RING * (WE + M)].rearrange("p (u n) -> p u n", u=RING)
        cT = sb("cT", [P, KT, 4])
        sg = sb("sg", [P, KT, 4])
        sc = sb("sc", [P, KT, 4])
        modT = sb("modT", [P, 2, 12, B])
        gm = sb("gm", [P, 4, B, M])
        sm = sb("sm", [P, 2, B, M])
        Wff = sb("Wff", [P, KT, M])
        sc_bc = sb("sc_bc", [P, M])
        Wdown = sb("Wdown", [P, KT, RAW])
        qw_bc = sb("qw_bc", [P, QR])
        kvw_bc = sb("kvw_bc", [P, KVR])
        gateT = sb("gateT", [P, KT, E])
        st = sb("st", [P, NT, 6])
        t16 = sb("t16", [P, 12, NT])
        rtv = sb("rtv", [P, 4 * T])
        rt = rtv[:, :].rearrange("p (u w t) -> p u w t", u=2, w=2)
        gs = rtv[:, 0:2048].rearrange("p (a b m) -> p a b m", a=4, b=B)
        scb = rtv[:, 2048:3072].rearrange("p (k c n) -> p k c n", k=KT, c=4)
        Wv = rtv[:, 3072:4096].rearrange("p (k n) -> p k n", k=KT)
        kcs = rtv[:, 0:1024].rearrange("p (w t r) -> p w t r", w=2, t=TT)
        sw13 = rtv[:, 0:1536].rearrange("p (k w n) -> p k w n", k=KT, w=2)
        sw2 = rtv[:, 1536:2304].rearrange("p (k m) -> p k m", k=3)
        nmax = sb("nmax", [P, 2])
        rsum = sb("rsum", [P, 2, HG])
        rinv = sb("rinv", [P, 2, HG])
        PTs = sb("PTs", [P, 2, HG * P])
        Rs = sb("Rs", [P, HG * P])
        OTs = sb("OTs", [P, HG * P])
        xn = Rs[:, :].rearrange("p (u m) -> p u m", u=2)
        hTs = PTs[:, 0, :].rearrange("p (u k q) -> p u k q", u=2, k=KT)
        sq = OTs[:, :].rearrange("p (u m) -> p u m", u=2)

        Pr = big[:, 0:8192].rearrange("p (u h k) -> p u h k", u=2, h=HG)
        QT = big[:, 8192:12288].rearrange("p (h t) -> p h t", h=HG)
        Krope = big[:, 12288:13312]
        wmod = big[:, 0:6144].rearrange("p (l k n) -> p l k n", l=2, k=KT)
        vflat = vbig[:, :, :].rearrange("p t n -> p (t n)")
        wqu = vflat[:, 0:1536].rearrange("p (h n) -> p h n", h=16)
        wku = vflat[:, 1536:2560].rearrange("p (h n) -> p h n", h=16)
        wvu = vflat[:, 2560:3584].rearrange("p (h n) -> p h n", h=16)
        wo1 = vflat[:, 3584:7680].rearrange("p (h n) -> p h n", h=16)
        ffo = vbig[:, :, 0:M]
        raw = vbig[:, :, 0:RAW]
        rope_a = vbig[:, :, 256:320]
        rope_b = vbig[:, :, 320:384]
        V1 = vbig[:, :, 384:448]
        qcT = hT[0:QR, 0, :]
        KT1 = hT[:, 1, :]
        qn = xn
        def two(lo, n):
            return big[:, lo:lo + 2 * n].rearrange("p (u n) -> p u n", u=2)

        hrow, zero = two(0, M), big[:, 512:768]
        actA, actB, actT = two(768, 384), two(1536, 384), two(2304, 384)
        PO = big[:, 3072:4608].rearrange("p (u k c) -> p u k c", u=2, k=TOPK)
        VAL = big[:, 4608:6144].rearrange("p (u k c e) -> p u k c e", u=2, k=TOPK, c=2)
        oh = big[:, 6144:6528].bitcast(BF16).rearrange("p (u k e) -> p u k e", u=2, k=TOPK)
        ohm = big[:, 6528:6912].rearrange("p (k e) -> p k e", k=TOPK)
        prob, top8 = two(6912, E), two(7040, 8)
        idx8 = big[:, 7056:7072].bitcast(U32).rearrange("p (u k) -> p u k", u=2)
        idxf, posk = two(7072, 8), two(7088, TOPK)
        lmax, lsum, lrec = big[:, 7100:7102], big[:, 7102:7104], big[:, 7104:7106]
        pv = big[:, 7106:7130].rearrange("p (u k c) -> p u k c", u=2, k=TOPK)
        mask = big[:, 7168:7232].bitcast(BF16).rearrange("p (u e) -> p u e", u=2)
        seen = big[:, 7232:7296].bitcast(BF16).rearrange("p (u e) -> p u e", u=2)
        slots = big[:, 7296:7424].rearrange("p (c e) -> p c e", c=2)
        empty = big[:, 7424:7488]
        xe = big[:, 7680:8704].rearrange("p (u n) -> p u n", u=4)
        xeT, eg, eh, ehT = two(8704, M), two(9216, M), two(9728, M), two(10240, M)
        ys = big[:, 10752:11776].rearrange("p (u n) -> p u n", u=4)
        toku = sb("toku", [P, E], U32)
        tokc = sb("tokc", [P, 8], U32)
        zall = vbig[:, :, 256:512]
        accs = vbig[:, :, 0:M]

        ps = [ctx.enter_context(nc.psum_tensor(f"ps{i}", [P, 512], F32)) for i in range(4)]
        sco = [ctx.enter_context(nc.psum_tensor(f"sco{i}", [P, 1024], F32)) for i in range(2)]
        ptp, OTp, mis = ps[0:2], ps[2], ps[3]
        shb, posb, sumb = sco[0], sco[1][:, 0:512], sco[1][:, 512:1024]

        s_passed = sem("waits_passed")
        s_x = sem("x_loaded")
        s_c = sem("consts_loaded")
        s_wm = sem("wmod_loaded")
        s_w1 = sem("l1_weights_loaded")
        s_sw = sem("small_weights_loaded")
        s_ch = sem("vector_chain")
        s_ac = sem("scalar_chain")
        s_sg = sem("c_silu")
        s_mT = sem("modT_matmuls")
        s_mTc = sem("modT_copied")
        s_mb = sem("mod_rows_matmuls")
        s_mbc = sem("mod_rows_copied")
        s_gm = sem("gates_ready")
        s_cw = sem("joined_weight_matmuls")
        s_cwc = sem("joined_weights_copied")
        s_rope1 = sem("l1_rope_loaded")
        s_sws = sem("shared_weights_loaded")

        LNS = {}
        for ph in "ABCD":
            names = ["stats", "var", "std", "ready", "turned", "hT"]
            names += ["xn"]
            names += ["mm", "used"] if ph != "D" else []
            names += ["free"] if ph == "A" else []
            LNS[ph] = {k: sem(f"{k}_{ph}") for k in names}
        s_fss, s_ffv, s_fft, s_fff = sem("ffn_squares"), sem("ffn_norm"), sem("ffn_tanh"), sem("ffn_done")
        s_rss, s_rms, s_rmsd = sem("raw_squares"), sem("rms_root_in"), sem("rms_root")
        s_qk1, s_qk1t, s_qk1c, s_v1 = sem("l1_rows"), sem("l1_turned"), sem("l1_turned_copied"), sem("l1_values_copied")
        AT = {}
        for L in (0, 1):
            names = ["wos", "vs", "proj", "ropem", "qk", "scores", "nmax", "exp", "turn", "ptA", "ptV", "av", "rinv", "rt",
                     "rs", "ot", "op", "xadd"]
            names += ["wq", "wo"] if L == 0 else ["wqs", "qlow"]
            AT[L] = {k: sem(f"{k}_L{L}") for k in names}
        s_hrow, s_hp = sem("h_rows_made"), sem("h_row_parts")
        s_hst = [sem(f"h_rows_stored_{u}") for u in range(2)]
        s_xe = [sem(f"expert_rows_{u}") for u in range(4)]
        s_lg, s_sh, s_sact, s_dv, s_shf, s_z, s_zf = (
            sem("logits"), sem("shared_products"), sem("shared_tanh"), sem("shared_chain"),
            sem("shared_hidden"), sem("shared_out"), sem("shared_out_copied"))
        s_lm, s_ex, s_rc, s_oh, s_mk, s_seen, s_pos, s_po, s_val, s_tbl, s_slot = (
            sem("logit_maxima"), sem("router_exps"), sem("router_chain"), sem("choices_one_hot"), sem("choice_mask"),
            sem("choices_seen"), sem("positions"), sem("positions_one_hot"), sem("choice_values"), sem("slot_products"),
            sem("slots_summed"))
        s_place = sem("place_chain")
        s_pad, s_zero, s_tok = sem("dram_set"), sem("zero_tile"), sem("token_ids")
        s_ew = [sem(f"expert_weights_{u}") for u in range(RING)]
        s_tc, s_xt, s_xc, s_gu, s_eg, s_ed, s_eh, s_y, s_ys = (
            sem("expert_ids"), sem("expert_turned"), sem("expert_turned_copied"), sem("expert_up"),
            sem("expert_tanh"), sem("expert_chain"), sem("expert_hidden"), sem("expert_down"), sem("expert_scaled"))
        s_add = [sem(f"expert_added_{u}") for u in range(2)]
        s_accl = [sem(f"sums_loaded_{b}") for b in range(B)]
        s_fin, s_out = sem("out_ready"), sem("out_stored")

        block = ctx.enter_context(nc.Block())
        xv = a["x"].rearrange("b (t p) m -> p (b t) m", p=P)
        ov = out.rearrange("b (t p) m -> p (b t) m", p=P)

        @block.sync
        def _(sp):
            sp.dma_start(cT[:], a["cT"]).then_inc(s_c, 16)
            sp.dma_start(ident[:], a["ident"]).then_inc(s_c, 16)
            for t, n in ((identb, "identb"), (maskb, "maskb"), (trib, "trib"), (onesb, "onesb"), (iota, "iota"),
                         (padid, "padid"), (tokid, "tokid"), (rope, "rope0")):
                sp.dma_start(t[:], a[n]).then_inc(s_c, 16)
            sp.dma_start(X[:], xv).then_inc(s_x, 16)
            sp.dma_start(wmod, a["wmod"]).then_inc(s_wm, 16)
            sp.dma_start(Wv, a["wv"]).then_inc(s_sw, 16)
            sp.dma_start(wqu, a["wqu"]).then_inc(s_w1, 16)
            sp.dma_start(wku, a["wku"]).then_inc(s_w1, 16)
            sp.dma_start(wvu, a["wvu"]).then_inc(s_w1, 16)
            sp.dma_start(wo1, a["wo1"]).then_inc(s_w1, 16)
            sp.dma_start(Wq1[:, :, KVR:D], a["wqr"]).then_inc(s_w1, 16)
            for t, n in ((Wff, "wff"), (Wdown, "wdown"), (gateT, "gateT")):
                sp.dma_start(t[:], a[n]).then_inc(s_sw, 16)
            sp.dma_start(sc_bc[:], a["ffs"].to_broadcast([P, M])).then_inc(s_sw, 16)
            sp.dma_start(qw_bc[:], a["qw"].to_broadcast([P, QR])).then_inc(s_sw, 16)
            sp.dma_start(kvw_bc[:], a["kvw"].to_broadcast([P, KVR])).then_inc(s_sw, 16)
            s = AT[0]
            with sp.Fori(0, B) as b:
                with sp.Fori(0, G) as g:
                    n = b * G + g
                    sp.wait_ge(s["proj"], n * 5 + 1)
                    sp.dma_start(WQ, a["wq"][g]).then_inc(s["wq"], 16)
                    sp.wait_ge(s["wos"], n + 1)
                    sp.dma_start(WOr, a["wo0"][g]).then_inc(s["wo"], 16)
            sp.wait_ge(s["ropem"], 5 * B * G + 1)
            sp.dma_start(rope, a["rope1"]).then_inc(s_rope1, 16)
            sp.wait_ge(s["qk"], 5 * B * G + 1)
            sp.dma_start(kcs, a["kcs"]).then_inc(s_rope1, 16)
            sp.wait_ge(AT[1]["qk"], 4 * B * G + 1)
            sp.dma_start(sw13, a["sw13"]).then_inc(s_sws, 16)
            sp.dma_start(sw2, a["sw2"]).then_inc(s_sws, 16)
            sp.wait_ge(AT[1]["xadd"], B * G * TT + 1)
            for u in range(RING):
                sp.dma_start(ring[:, u, :], a["we"][u]).then_inc(s_ew[u], 16)
                sp.dma_start(ring2[:, u, :], a["we2"][u]).then_inc(s_ew[u], 16)
            sp.wait_ge(s_zero, 1)
            sp.dma_start(hd[B * T:B * T + P, :], zero).then_inc(s_pad, 16)
            for u in range(2):
                sp.dma_start(accd[u].rearrange("(t p) m -> p t m", p=P), zero.unsqueeze(1).to_broadcast([P, NT + 1, M])).then_inc(s_pad, 16)
            with sp.Fori(0, NT // 2) as it:
                for u in range(2):
                    sp.wait_ge(s_hrow, it * 2 + (u + 3))
                    sp.dma_start(hd[bass.ds((it * 2 + u) * P, P), :], hrow[:, u, :]).then_inc(s_hst[u], 16)
            with sp.Fori(1, E // RING) as r:
                for u in range(RING):
                    sp.wait_ge(s_y, (r - 1) * RING + (u + 1))
                    sp.dma_start(ring[:, u, :], a["we"][r * RING + u]).then_inc(s_ew[u], 16)
                    sp.dma_start(ring2[:, u, :], a["we2"][r * RING + u]).then_inc(s_ew[u], 16)
            for u in range(2):
                sp.wait_ge(s_add[u], 16 * (E // 2))
            for b in range(B):
                for u, dst in enumerate((accs, zall)):
                    sp.dma_start(dst[:, b * TT:(b + 1) * TT, :],
                                 accd[u][b * T:(b + 1) * T, :].rearrange("(t p) m -> p t m", p=P)).then_inc(s_accl[b], 16)
            for b in range(B):
                sp.wait_ge(s_fin, b + 1)
                sp.dma_start(ov[:, b * TT:(b + 1) * TT, :], X[:, b * TT:(b + 1) * TT, :]).then_inc(s_out, 16)
            sp.wait_ge(s_out, 32)
            for u in range(2):
                sp.wait_ge(s_hst[u], 16 * (NT // 2) + 16)
            sp.wait_ge(s_pad, 48)

        @block.tensor
        def _(pe):
            mm, tr = nc.tensor.matmul, nc.tensor.transpose
            pe.wait_ge(s_sg, 1)
            pe.wait_ge(s_wm, 16)
            for l in range(2):
                for c in range(12):
                    for k in range(KT):
                        last = mm(mis[:, 24 * l + 2 * c:24 * l + 2 * c + 2], wmod[:, l, k, c * P:(c + 1) * P],
                                  sc[:, k, 2 * l:2 * l + 2], start=(k == 0), stop=(k == KT - 1))
            last.then_inc(s_mT, 1)
            for n, (l, c) in enumerate(((0, 2), (0, 5), (1, 2), (1, 5), (1, 3), (1, 4))):
                if n >= 2:
                    pe.wait_ge(s_mbc, n - 1)
                for b in range(B):
                    for k in range(KT):
                        last = mm(ptp[n % 2][:, b * M:(b + 1) * M], scb[:, k, 2 * l + b, :],
                                  wmod[:, l, k, c * M:(c + 1) * M], start=(k == 0), stop=(k == KT - 1))
                last.then_inc(s_mb, 1)
            pe.wait_ge(s_w1, 80)
            for h in range(16):
                last = mm(sco[0][0:QR, h * KVR:(h + 1) * KVR], wqu[:, h, :], wku[:, h, :], start=True, stop=True)
            last.then_inc(s_cw, 1)
            for h in range(16):
                half = KVR * (h % 2)
                if h % 8 == 0 and h:
                    pe.wait_ge(s_cwc, h // 8 + 1)
                last = mm(sco[1][half:half + KVR, (h // 2) % 4 * M:(h // 2) % 4 * M + M], wvu[:, h, :], wo1[:, h, :],
                          start=True, stop=True)
                if h % 8 == 7:
                    last.then_inc(s_cw, 1)

            def turn_h(ph, t, u):
                s = LNS[ph]
                pe.wait_ge(s["xn"], t + 1)
                pe.wait_ge(s["hT"], t + 1)
                for k in range(KT):
                    last = tr(ptp[u][:, k * P:(k + 1) * P], xn[:, u, k * P:(k + 1) * P], ident[:])
                last.then_inc(s["turned"], 1)

            def project_h(ph, t, u, W, N, bank):
                s = LNS[ph]
                pe.wait_ge(s["hT"], t + 3)
                pe.wait_ge(s["used"], t + 1)
                for k in range(KT):
                    last = mm(bank[:, 0:N], hTs[:, u, k, :], W[:, k, :], start=(k == 0), stop=(k == KT - 1))
                last.then_inc(s["mm"], 1)

            def layer_norm_products(ph, W, N):
                turn_h(ph, 0, 0)
                with pe.Fori(0, NT // 2 - 1) as it:
                    for u in range(2):
                        turn_h(ph, it * 2 + (u + 1), 1 - u)
                        project_h(ph, it * 2 + u, u, W, N, ps[2 + u])
                turn_h(ph, NT - 1, 1)
                for u in range(2):
                    project_h(ph, NT - 2 + u, u, W, N, ps[2 + u])

            def attention(L):
                s = AT[L]
                np_ = 5 if L == 0 else 4
                with pe.Fori(0, B) as b:
                    with pe.Fori(0, G) as g:
                        n = b * G + g
                        if L == 0:
                            pe.wait_ge(s["wq"], n * 16 + 16)
                        else:
                            pe.wait_ge(s["wqs"], n + 1)
                        pe.wait_ge(s["exp"], n * NS + 1)
                        for m in range(np_):
                            if m >= 2:
                                pe.wait_ge(s["ropem"], n * np_ + m)
                                if L == 1:
                                    pe.wait_ge(s["qlow"], n * np_ + (m - 1))
                            for half in range(2):
                                o = sco[m % 2][:, half * 512:(half + 1) * 512]
                                cols = bass.ds(b * T + half * 512, 512)
                                if L == 0:
                                    for k in range(KT):
                                        last = mm(o, WQ[:, k, m, :], hT[:, k, cols], start=(k == 0), stop=(k == KT - 1))
                                else:
                                    last = mm(o, WQ[0:QR, 0, m, :], qcT[:, cols], start=True, stop=True)
                            last.then_inc(s["proj"], 1)
                        for kind, i, j, c in STEPS:
                            if kind == "S":
                                if c == 0:
                                    pe.wait_ge(s["qk"], n * np_ + (np_ + 1))
                                if c >= 2:
                                    pe.wait_ge(s["exp"], n * NS + c)
                                o = sco[c % 2]
                                w = (i + 1) * P
                                for c0 in range(0, w, 512):
                                    c1 = min(w, c0 + 512)
                                    k_rhs = Krope[:, c0:c1] if L == 0 else KT1[:, bass.ds(b * T + c0, c1 - c0)]
                                    mm(o[:, c0:c1], QT[:, j, i * P:(i + 1) * P], k_rhs, start=True, stop=(c1 < w))
                                mm(o[:, i * P:w], identb[:], maskb[:], start=False, stop=True).then_inc(s["scores"], 1)
                            elif kind == "T":
                                if j == 0:
                                    pe.wait_ge(s["exp"], n * NS + (HG * i + HG + 1))
                                for h in range(HG):
                                    last = tr(ptp[c % 2][:, h * P:(h + 1) * P], Pr[:, i % 2, h, j * P:(j + 1) * P], ident[:])
                                last.then_inc(s["turn"], 1)
                            elif kind == "A":
                                if c == 0:
                                    pe.wait_ge(s["vs"], n + 1)
                                if c % 2 == 0:
                                    pe.wait_ge(s["ptA"], n * (TURNS // 2) + (c // 2 + 1))
                                else:
                                    pe.wait_ge(s["ptV"], n * (TURNS // 2) + (c // 2 + 1))
                                if L == 0:
                                    last = mm(OTp[:, :], Vs[:, j, :], PTs[:, c % 2, :], start=(j == 0), stop=(j == i))
                                else:
                                    pt = PTs[:, c % 2, :].rearrange("p (a s q) -> p s a q", s=2, q=P)
                                    for half in range(2):
                                        last = mm(OTp[half * 64:half * 64 + 64, 0:256], Vs[:, j, 0:KVR], pt[:, half],
                                                  start=(j == 0), stop=(j == i))
                                if j == i:
                                    last.then_inc(s["av"], 1)
                            elif kind == "R":
                                pe.wait_ge(s["rinv"], n * TT + (i + 1))
                                pe.wait_ge(s["xadd"], n * TT + (i + 1))
                                if L == 0:
                                    for h in range(HG):
                                        last = tr(mis[:, h * P:(h + 1) * P], rinv[:, i % 2, h:h + 1].to_broadcast([P, P]), ident[:])
                                else:
                                    for h in range(2):
                                        last = tr(mis[:, h * P:(h + 1) * P], rinv64[:, i % 2, h * P:(h + 1) * P], ident[:])
                                last.then_inc(s["rt"], 1)
                            else:
                                pe.wait_ge(s["ot"], n * TT + (i + 1))
                                if i == 0:
                                    pe.wait_ge(s["wos"], n + 2)
                                nh = HG if L == 0 else 2
                                for h in range(nh):
                                    last = mm(mis[:, 0:M], OTs[:, h * P:(h + 1) * P], WO[:, h, :], start=(h == 0), stop=(h == nh - 1))
                                last.then_inc(s["op"], 1)

            pe.wait_ge(s_mbc, 6)
            pe.wait_ge(s_mTc, 1)
            pe.wait_ge(s_sw, 16 * 7)
            layer_norm_products("A", Wv, 512)
            pe.wait_ge(LNS["A"]["used"], NT + 2)
            pe.wait_ge(LNS["A"]["free"], NT + 2)
            pe.wait_ge(s_cwc, 3)
            attention(0)
            for ph, W, N in (("B", Wff, M), ("C", Wdown, RAW)):
                layer_norm_products(ph, W, N)
            pe.wait_ge(LNS["C"]["used"], NT + 2)
            with pe.Fori(0, NT // 2) as it:
                for u in range(2):
                    t = it * 2 + u
                    pe.wait_ge(s_qk1, t + 1)
                    pe.wait_ge(s_qk1c, t + 1)
                    tr(ptp[u][0:QR, 0:P], sq[:, u, 0:QR], ident[:])
                    tr(ptp[u][:, P:2 * P], sq[:, u, P:2 * P], ident[:]).then_inc(s_qk1t, 1)
            pe.wait_ge(s_qk1c, NT + 2)
            attention(1)

            def shared_out(t, u):
                pe.wait_ge(s_shf, t + 3)
                pe.wait_ge(s_zf, t + 1)
                for c in range(3):
                    last = mm(OTp[:, 0:M], actT[:, u, c * P:(c + 1) * P], sw2[:, c, :], start=(c == 0), stop=(c == 2))
                last.then_inc(s_z, 1)

            def positions(t, u):
                pe.wait_ge(s_mk, t + 1)
                pe.wait_ge(s_seen, t + 1)
                pe.wait_ge(s_po, t + 1)
                mm(posb[:, 0:E], trib[:], mask[:, u, :], start=True, stop=False)
                mm(posb[:, 0:E], onesb[:], seen[:, u, :], start=False, stop=True).then_inc(s_pos, 1)

            def slot_sums(t, u):
                pe.wait_ge(s_po, t + 2)
                pe.wait_ge(s_val, t + 3)
                pe.wait_ge(s_slot, t + 1)
                for k in range(TOPK):
                    last = mm(sumb[:, 0:2 * E], PO[:, u, k, :], VAL[:, u, k, :, :].rearrange("p c e -> p (c e)"),
                              start=(k == 0), stop=(k == TOPK - 1))
                last.then_inc(s_tbl, 1)

            def ffn_tile(t, u, behind):
                pe.wait_ge(LNS["D"]["hT"], t + 3)
                pe.wait_ge(s_ex, t + 1)
                for k in range(KT):
                    last = mm(mis[:, 0:E], hTs[:, u, k, :], gateT[:, k, :], start=(k == 0), stop=(k == KT - 1))
                last.then_inc(s_lg, 1)
                pe.wait_ge(s_shf, t + 2)
                for w in range(2):
                    for c in range(3):
                        for k in range(KT):
                            last = mm(shb[:, w * 512 + c * P:w * 512 + (c + 1) * P], sw13[:, k, w, c * P:(c + 1) * P],
                                      hTs[:, u, k, :], start=(k == 0), stop=(k == KT - 1))
                last.then_inc(s_sh, 1)
                if behind >= 1:
                    positions(t - 1, 1 - u)
                if behind >= 2:
                    slot_sums(t - 2, u)
                if behind >= 1:
                    shared_out(t - 1, 1 - u)

            pe.wait_ge(s_sws, 32)
            turn_h("D", 0, 0)
            for t in range(2):
                turn_h("D", t + 1, 1 - t)
                ffn_tile(t, t, t)
            with pe.Fori(1, NT // 2 - 1) as it:
                for u in range(2):
                    turn_h("D", it * 2 + (u + 1), 1 - u)
                    ffn_tile(it * 2 + u, u, 2)
            turn_h("D", NT - 1, 1)
            ffn_tile(NT - 2, 0, 2)
            ffn_tile(NT - 1, 1, 2)
            positions(NT - 1, 1)
            slot_sums(NT - 2, 0)
            shared_out(NT - 1, 1)
            slot_sums(NT - 1, 1)

            outs = (OTp, mis)

            def turn_rows(e, w, gathers):
                v = w % 2
                pe.wait_ge(s_xe[w % 4], gathers * 16)
                pe.wait_ge(s_xc, e + 1)
                for k in range(KT):
                    last = tr(ptp[v][:, k * P:(k + 1) * P], xe[:, w % 4, k * P:(k + 1) * P], ident[:])
                last.then_inc(s_xt, 1)

            def up(e, v, u, r):
                pe.wait_ge(s_ew[u], r * 32 + 32)
                pe.wait_ge(s_xc, e + 3)
                pe.wait_ge(s_eh, e + 1)
                for c, o in ((2, sco[v][0:64 + I2, P:2 * P]), (0, sco[v][:, 0:P]), (1, sco[v][:, 2 * P:3 * P])):
                    for k in range(KT):
                        last = mm(o, ring[:, u, k * UP + c * P:k * UP + min(c * P + P, UP)], xeT[:, v, k * P:(k + 1) * P],
                                  start=(k == 0), stop=(k == KT - 1))
                last.then_inc(s_gu, 1)

            def down(e, v, u):
                pe.wait_ge(s_eh, e + 3)
                pe.wait_ge(s_ys, e + 1)
                mm(outs[v][:, 0:M], ehT[:, v, 0:P], ring[:, u, KT * UP:WE], start=True, stop=False)
                mm(outs[v][:, 0:M], ehT[0:I2, v, P:2 * P], ring2[:, u, :], start=False, stop=True).then_inc(s_y, 1)

            def expert_group(r, first=False, last=False):
                for u in range(RING):
                    e = r * RING + u
                    up(e, u % 2, u, r)
                    if not (last and u == RING - 1):
                        turn_rows(e + 1, u + 1, r * (RING // 4) + (u + 1) // 4 + 1)
                    if not (first and u == 0):
                        down(e - 1, (u + 1) % 2, (u - 1) % RING)

            pe.wait_ge(s_zf, NT + 1)
            pe.wait_ge(s_shf, NT + 2)
            pe.wait_ge(s_slot, NT + 1)
            turn_rows(0, 0, 1)
            expert_group(0, first=True)
            with pe.Fori(1, E // RING - 1) as r:
                expert_group(r)
            expert_group(E // RING - 1, last=True)
            down(E - 1, 1, RING - 1)

        @block.scalar
        def _(act):
            af = nc.scalar.activation

            def turned_copies(ph, shift, scale, layer, squares=None):
                s = LNS[ph]
                with act.Fori(0, B) as b:
                    with act.Fori(0, TT // 2) as it:
                        for u in range(2):
                            t = b * TT + it * 2 + u
                            act.wait_ge(s["turned"], t + 3)
                            act.wait_ge(s["mm"], t + 1)
                            if ph == "A":
                                act.wait_ge(s["free"], t + 1)
                            settle(act, s_passed)
                            for k in range(KT):
                                last = af(hTs[:, u, k, :], ptp[u][:, k * P:(k + 1) * P], ACT.Identity,
                                          bias=modT[:, layer, 2 * shift + k, bass.ds(b, 1)],
                                          scale=modT[:, layer, 2 * scale + k, bass.ds(b, 1)])
                            last.then_inc(s["hT"], 1)
                    if squares:
                        with act.Fori(0, TT) as it:
                            t = b * TT + it
                            act.wait_ge(s["used"], t + 3)
                            settle(act, s_passed)
                            squares(t)

            def root(ph):
                act.wait_ge(LNS[ph]["var"], 1)
                af(t16[:, 4, :], t16[:, 3, :], ACT.Sqrt).then_inc(LNS[ph]["std"], 1)

            def attention(L):
                s = AT[L]
                np_ = 5 if L == 0 else 4
                with act.Fori(0, B) as b:
                    with act.Fori(0, G) as g:
                        n = b * G + g
                        if L == 1:
                            for m in range(np_):
                                act.wait_ge(s["proj"], n * np_ + (m + 2))
                                af(QT[0:KVR, m, :], sco[m % 2][0:KVR, :], ACT.Copy).then_inc(s["qlow"], 1)
                        for kind, i, j, c in STEPS:
                            if kind == "S":
                                act.wait_ge(s["nmax"], n * NS + (c + 1))
                                af(Pr[:, i % 2, j, 0:(i + 1) * P], sco[c % 2][:, 0:(i + 1) * P], ACT.Exp,
                                   bias=nmax[:, c % 2:c % 2 + 1], accum_out=rsum[:, i % 2, j:j + 1]).then_inc(s["exp"], 1)
                            elif kind == "T" and c % 2 == 0:
                                act.wait_ge(s["turn"], n * TURNS + (c + 1))
                                af(PTs[:, 0, :], ptp[0][:, :], ACT.Copy).then_inc(s["ptA"], 1)
                            elif kind == "R":
                                act.wait_ge(s["rt"], n * TT + (i + 1))
                                w = HG * P if L == 0 else 2 * P
                                af(Rs[:, 0:w], mis[:, 0:w], ACT.Copy).then_inc(s["rs"], 1)

            act.wait_ge(s_c, 16 * 10)
            af(sg[:], cT[:], ACT.Exp, scale=-1.0).then_inc(s_ac, 1)
            act.wait_ge(s_mT, 1)
            af(modT[:].rearrange("p l c b -> p (l c b)"), mis[:, 0:48], ACT.Copy).then_inc(s_mTc, 1)
            root("A")
            act.wait_ge(s_mTc, 2)
            turned_copies("A", 0, 1, 0)
            attention(0)
            root("B")
            turned_copies("B", 3, 4, 0, lambda t: af(vbig[:, t, M:2 * M], ffo[:, t, :], ACT.Square,
                                                     accum_out=t16[:, 5, bass.ds(t, 1)]).then_inc(s_fss, 1))
            act.wait_ge(s_fss, NT)
            af(t16[:, 6, :], t16[:, 5, :], ACT.Sqrt).then_inc(s_ffv, 1)
            act.wait_ge(s_ffv, 2)
            af(t16[:, 8, :], t16[:, 7, :], ACT.Tanh).then_inc(s_fft, 1)
            root("C")

            def raw_squares(t):
                af(vbig[:, t, 256:256 + QR], raw[:, t, 0:QR], ACT.Square, accum_out=t16[:, 5, bass.ds(t, 1)]).then_inc(s_rss, 1)
                af(vbig[:, t, 384:384 + KVR], raw[:, t, QR:QR + KVR], ACT.Square, accum_out=t16[:, 6, bass.ds(t, 1)]).then_inc(s_rss, 1)

            turned_copies("C", 0, 1, 1, raw_squares)
            act.wait_ge(s_rms, 1)
            af(t16[:, 7:9, :], t16[:, 5:7, :], ACT.Sqrt).then_inc(s_rmsd, 1)
            with act.Fori(0, NT // 2) as it:
                for u in range(2):
                    t = it * 2 + u
                    act.wait_ge(s_qk1t, t + 3)
                    settle(act, s_passed)
                    af(hT[0:QR, 0, bass.ds(t * P, P)], ptp[u][0:QR, 0:P], ACT.Copy)
                    af(hT[:, 1, bass.ds(t * P, P)], ptp[u][:, P:2 * P], ACT.Copy).then_inc(s_qk1c, 1)
            attention(1)
            root("D")
            with act.Fori(0, B) as b:
                with act.Fori(0, TT // 2) as it:
                    for u in range(2):
                        t = b * TT + it * 2 + u
                        act.wait_ge(LNS["D"]["turned"], t + 3)
                        act.wait_ge(s_sh, t + 1)
                        settle(act, s_passed)
                        for k in range(KT):
                            last = af(hTs[:, u, k, :], ptp[u][:, k * P:(k + 1) * P], ACT.Identity,
                                      bias=modT[:, 1, 6 + k, bass.ds(b, 1)], scale=modT[:, 1, 8 + k, bass.ds(b, 1)])
                        last.then_inc(LNS["D"]["hT"], 1)
                        act.wait_ge(s_lm, t + 1)
                        af(prob[:, u, :], mis[:, 0:E], ACT.Exp, bias=lmax[:, u:u + 1], accum_out=lsum[:, u:u + 1]).then_inc(s_ex, 1)
                        act.wait_ge(s_sh, t + 3)
                        act.wait_ge(s_shf, t + 1)
                        af(actA[:, u, :], shb[:, 0:384], ACT.Tanh, scale=0.5).then_inc(s_sact, 1)

            def rows_copy(e, v):
                act.wait_ge(s_xt, e + 1)
                af(xeT[:, v, :], ptp[v][:, 0:M], ACT.Copy).then_inc(s_xc, 1)

            def expert(e, w, first=False, last=False):
                v = w % 2
                act.wait_ge(s_gu, e + 1)
                af(eg[0:I2, v, P:2 * P], sco[v][0:I2, P:2 * P], ACT.Tanh, scale=0.5)
                af(eg[:, v, 0:P], sco[v][:, 0:P], ACT.Tanh, scale=0.5).then_inc(s_eg, 1)
                if not last:
                    rows_copy(e + 1, 1 - v)
                if not first:
                    scaled(e - 1, (w - 1) % 4)

            def scaled(e, w):
                act.wait_ge(s_y, e + 1)
                if isinstance(e, int):
                    if e >= 4:
                        act.wait_ge(s_add[w % 2], 16 * (e // 2 - 1))
                    gate = slots[:, 1, e:e + 1]
                else:
                    act.wait_ge(s_add[w % 2], e * 8 - (16 + 8 * (w % 2)))
                    gate = slots[:, 1, bass.ds(e, 1)]
                settle(act, s_passed)
                af(ys[:, w, :], (OTp, mis)[w % 2][:, 0:M], ACT.Copy, scale=gate).then_inc(s_ys, 1)

            rows_copy(0, 0)
            for e in range(8):
                expert(e, e % 4, first=(e == 0))
            with act.Fori(2, E // 4 - 1) as it:
                for w in range(4):
                    expert(it * 4 + w, w)
            for e in range(E - 4, E):
                expert(e, e % 4, last=(e == E - 1))
            scaled(E - 1, 3)

        @block.vector
        def _(v):
            ve = nc.vector
            chain = [0]

            def link(ins):
                chain[0] += 1
                ins.then_inc(s_ch, 1)
                v.wait_ge(s_ch, chain[0])

            def statistics(ph):
                s = LNS[ph]
                with v.Fori(0, NT) as t:
                    ve.bn_stats(st[:, t, :], X[:, t, :]).then_inc(s["stats"], 1)
                v.wait_ge(s["stats"], NT)
                link(ve.tensor_tensor(t16[:, 0, :], st[:, :, 1], st[:, :, 4], ALU.add))
                link(ve.tensor_tensor(t16[:, 1, :], st[:, :, 1], st[:, :, 4], ALU.subtract))
                link(ve.tensor_tensor(t16[:, 2, :], st[:, :, 2], st[:, :, 5], ALU.add))
                link(ve.scalar_tensor_tensor(t16[:, 1, :], t16[:, 1, :], 0.25, t16[:, 1, :], ALU.mult, ALU.mult))
                link(ve.scalar_tensor_tensor(t16[:, 2, :], t16[:, 2, :], 1.0 / M, t16[:, 1, :], ALU.mult, ALU.add))
                ve.tensor_scalar(t16[:, 3, :], t16[:, 2, :], LN_EPS, None, ALU.add).then_inc(s["var"], 1)
                v.wait_ge(s["std"], 1)
                link(ve.reciprocal(t16[:, 2, :], t16[:, 4, :]))
                ve.scalar_tensor_tensor(t16[:, 1, :], t16[:, 0, :], -0.5, t16[:, 2, :], ALU.mult, ALU.mult).then_inc(s["ready"], 1)
                v.wait_ge(s["ready"], 1)

            def normalise(ph, t, u):
                s = LNS[ph]
                v.wait_ge(s["turned"], t + 1)
                ve.tensor_scalar(xn[:, u, :], X[:, bass.ds(t, 1), :].rearrange("p a m -> p (a m)"), t16[:, 2, bass.ds(t, 1)],
                                 t16[:, 1, bass.ds(t, 1)], ALU.mult, ALU.add).then_inc(s["xn"], 1)

            def layer_norm(ph, keep):
                s = LNS[ph]

                def kept(t, u):
                    v.wait_ge(s["mm"], t + 3)
                    keep(t, u).then_inc(s["used"], 1)

                normalise(ph, 0, 0)
                with v.Fori(0, NT // 2 - 1) as it:
                    for u in range(2):
                        normalise(ph, it * 2 + (u + 1), 1 - u)
                        kept(it * 2 + u, u)
                normalise(ph, NT - 1, 1)
                kept(NT - 2, 0)
                kept(NT - 1, 1)

            def attention(L):
                s = AT[L]
                np_ = 5 if L == 0 else 4
                with v.Fori(0, B) as b:
                    with v.Fori(0, G) as g:
                        n = b * G + g
                        for m in range(np_):
                            v.wait_ge(s["proj"], n * np_ + (m + 2))
                            if m >= 2:
                                v.wait_ge(s["qk"], n * np_ + m)
                            src, r = sco[m % 2], rt[:, m % 2]
                            if L == 0:
                                ve.tensor_tensor(r[:, 0, :], src[:, :], rope[:, 0, :], ALU.mult)
                                ve.tensor_tensor(r[0:64, 1, :], src[64:128, :], rope[64:128, 1, :], ALU.mult)
                                ve.tensor_tensor(r[64:128, 1, :], src[0:64, :], rope[0:64, 1, :], ALU.mult).then_inc(s["ropem"], 1)
                            else:
                                ve.tensor_tensor(r[64:128, 0, :], src[64:128, :], rope[64:128, 0, :], ALU.mult)
                                ve.tensor_tensor(r[64:96, 1, :], src[96:128, :], rope[96:128, 1, :], ALU.mult)
                                ve.tensor_tensor(r[96:128, 1, :], src[64:96, :], rope[64:96, 1, :], ALU.mult).then_inc(s["ropem"], 1)
                        for kind, i, j, c in STEPS:
                            if kind == "S":
                                v.wait_ge(s["scores"], n * NS + (c + 1))
                                ve.tensor_reduce(nmax[:, c % 2:c % 2 + 1], sco[c % 2][:, 0:(i + 1) * P], AX.X, ALU.max,
                                                 negate=True).then_inc(s["nmax"], 1)
                            elif kind == "T":
                                if j == 0:
                                    v.wait_ge(s["exp"], n * NS + (HG * i + HG + 1))
                                    if L == 0:
                                        ve.reciprocal(rinv[:, i % 2, :], rsum[:, i % 2, :]).then_inc(s["rinv"], 1)
                                    else:
                                        ve.reciprocal(rinv64[:, i % 2, :].rearrange("p (h d) -> p h d", h=HG),
                                                      rsum[:, i % 2, :].unsqueeze(2).to_broadcast([P, HG, 64])).then_inc(s["rinv"], 1)
                                if c % 2 == 1:
                                    v.wait_ge(s["turn"], n * TURNS + (c + 1))
                                    ve.tensor_copy(PTs[:, 1, :], ptp[1][:, :]).then_inc(s["ptV"], 1)
                            elif kind == "R":
                                v.wait_ge(s["av"], n * TT + (i + 1))
                                v.wait_ge(s["rs"], n * TT + (i + 1))
                                w = HG * P if L == 0 else 2 * P
                                ve.tensor_tensor(OTs[:, 0:w], OTp[:, 0:w], Rs[:, 0:w], ALU.mult).then_inc(s["ot"], 1)
                            elif kind == "O":
                                v.wait_ge(s["op"], n * TT + (i + 1))
                                xt = X[:, bass.ds(b * TT + i, 1), :].rearrange("p a m -> p (a m)")
                                ve.tensor_tensor(xt, mis[:, 0:M], xt, ALU.add).then_inc(s["xadd"], 1)

            v.wait_ge(s_ac, 1)
            v.wait_ge(s_c, 16 * 10)
            link(ve.tensor_scalar(sg[:], sg[:], 1.0, None, ALU.add))
            link(ve.reciprocal(sg[:], sg[:]))
            link(ve.tensor_tensor(sc[:], sg[:], cT[:], ALU.mult))
            ve.tensor_copy(scb, sc[:].unsqueeze(3).to_broadcast([P, KT, 4, P])).then_inc(s_sg, 1)
            v.wait_ge(s_x, 16)
            statistics("A")
            v.wait_ge(s_mTc, 1)
            for l in range(2):
                for c in (1, 4):
                    last = ve.tensor_scalar(modT[:, l, 2 * c:2 * c + 2, :], modT[:, l, 2 * c:2 * c + 2, :], 1.0, None, ALU.add)
            last.then_inc(s_mTc, 1)
            for n in range(6):
                v.wait_ge(s_mb, n + 1)
                src = ptp[n % 2][:, :].rearrange("p (b m) -> p b m", b=B)
                if n < 4:
                    ve.tensor_copy(gm[:, n], src).then_inc(s_mbc, 1)
                else:
                    ve.tensor_scalar(sm[:, n - 4], src, float(n - 4), None, ALU.add).then_inc(s_mbc, 1)
            v.wait_ge(s_mbc, 6)
            link(ve.tensor_scalar(gs, gm[:], 0.0, 2.0, ALU.is_ge, ALU.mult))
            gf = gm[:].rearrange("p a b m -> p (a b m)")
            link(ve.scalar_tensor_tensor(gf, gf, -1.0, gf, ALU.mult, ALU.max))
            link(ve.tensor_scalar(gf, gf, 0.25, None, ALU.max))
            ve.scalar_tensor_tensor(gm[:].rearrange("p a b m -> p (a b m)"), gs.rearrange("p a b m -> p (a b m)"), -1.0,
                                    gm[:].rearrange("p a b m -> p (a b m)"), ALU.add, ALU.mult).then_inc(s_gm, 1)
            v.wait_ge(s_cw, 1)
            ve.tensor_scalar(Wq1[:, :, 0:KVR], sco[0][0:QR, :].rearrange("p (h n) -> p h n", h=16), L1_SCALE, None,
                             ALU.mult).then_inc(s_cwc, 1)
            for n in range(2):
                v.wait_ge(s_cw, n + 2)
                ve.tensor_copy(Wvo[:, 4 * n:4 * n + 4, :], sco[1][:, :].rearrange("p (h m) -> p h m", h=4)).then_inc(s_cwc, 1)
            v.wait_ge(s_w1, 80)
            ve.tensor_scalar(Wq1[:, :, KVR:D], Wq1[:, :, KVR:D], L1_SCALE, None, ALU.mult).then_inc(s_cwc, 1)

            layer_norm("A", lambda t, u: ve.tensor_copy(vbig[:, t, :], ps[2 + u][:, :]))
            attention(0)
            v.wait_ge(AT[0]["xadd"], B * G * TT + 1)
            statistics("B")
            layer_norm("B", lambda t, u: ve.tensor_tensor(ffo[:, t, :], ps[2 + u][:, 0:M], sc_bc[:], ALU.mult))
            v.wait_ge(s_ffv, 1)
            ve.tensor_scalar(t16[:, 7, :], t16[:, 6, :], HYP_EPS, None, ALU.max).then_inc(s_ffv, 1)
            v.wait_ge(s_ffv, 2)
            link(ve.tensor_scalar(t16[:, 9, :], t16[:, 7, :], HYP_EPS, None, ALU.add))
            link(ve.reciprocal(t16[:, 9, :], t16[:, 9, :]))
            v.wait_ge(s_fft, 1)
            link(ve.tensor_tensor(t16[:, 9, :], t16[:, 9, :], t16[:, 8, :], ALU.mult))
            link(ve.tensor_tensor(t16[:, 10, :], t16[:, 9, :], t16[:, 6, :], ALU.mult))
            link(ve.tensor_scalar(t16[:, 10, :], t16[:, 10, :], HYP_EPS, None, ALU.max))
            link(ve.reciprocal(t16[:, 10, :], t16[:, 10, :]))
            link(ve.tensor_scalar(t16[:, 10, :], t16[:, 10, :], MAX_NORM, 1.0, ALU.mult, ALU.min))
            link(ve.tensor_tensor(t16[:, 9, :], t16[:, 9, :], t16[:, 10, :], ALU.mult))
            v.wait_ge(s_fss, NT)
            with v.Fori(0, B) as b:
                with v.Fori(0, TT) as it:
                    t = b * TT + it
                    ft = ffo[:, bass.ds(t, 1), :].rearrange("p a m -> p (a m)")
                    gb = gm[:, 1, bass.ds(b, 1), :].rearrange("p a m -> p (a m)")
                    ve.scalar_tensor_tensor(ft, ft, t16[:, 9, bass.ds(t, 1)], gb, ALU.mult, ALU.mult).then_inc(s_fff, 1)
            v.wait_ge(s_fff, NT)
            link(ve.tensor_tensor(X[:], X[:], ffo, ALU.add))
            statistics("C")
            layer_norm("C", lambda t, u: ve.tensor_copy(raw[:, t, :], ps[2 + u][:, 0:RAW]))
            v.wait_ge(s_rss, 2 * NT)
            link(ve.tensor_scalar(t16[:, 5, :], t16[:, 5, :], 1.0 / QR, RMS_EPS, ALU.mult, ALU.add))
            ve.tensor_scalar(t16[:, 6, :], t16[:, 6, :], 1.0 / KVR, RMS_EPS, ALU.mult, ALU.add).then_inc(s_rms, 1)
            v.wait_ge(s_rope1, 32)
            for b in range(B):
                tiles = slice(b * TT, (b + 1) * TT)
                x1, x2 = raw[:, tiles, QR + KVR:QR + KVR + 32], raw[:, tiles, QR + KVR + 32:RAW]
                ve.tensor_tensor(rope_a[:, tiles, :], raw[:, tiles, QR + KVR:RAW], kcs[:, 0], ALU.mult)
                ve.tensor_tensor(rope_b[:, tiles, 0:32], x2, kcs[:, 1, :, 0:32], ALU.mult)
                last = ve.tensor_tensor(rope_b[:, tiles, 32:64], x1, kcs[:, 1, :, 32:64], ALU.mult)
            link(last)
            v.wait_ge(s_rmsd, 1)
            link(ve.reciprocal(t16[:, 5:7, :], t16[:, 7:9, :]))
            with v.Fori(0, NT // 2) as it:
                for u in range(2):
                    t = it * 2 + u
                    v.wait_ge(s_qk1t, t + 1)
                    v.wait_ge(s_v1, t + 1)
                    ve.scalar_tensor_tensor(sq[:, u, 0:QR], raw[:, t, 0:QR], t16[:, 5, bass.ds(t, 1)], qw_bc[:],
                                            ALU.mult, ALU.mult)
                    ve.scalar_tensor_tensor(sq[:, u, P:P + KVR], raw[:, t, QR:QR + KVR], t16[:, 6, bass.ds(t, 1)], kvw_bc[:],
                                            ALU.mult, ALU.mult)
                    ve.tensor_tensor(sq[:, u, P + KVR:2 * P], rope_a[:, t, :], rope_b[:, t, :], ALU.add).then_inc(s_qk1, 1)
            attention(1)
            v.wait_ge(AT[1]["xadd"], B * G * TT + 1)
            statistics("D")
            ve.memset(seen[:, 0, :], 0.0).then_inc(s_seen, 1)
            ve.memset(slots, 0.0).then_inc(s_slot, 1)
            choices = [P, TOPK, E]

            def route(t, u):
                def link(n):
                    v.wait_ge(s_rc, t * 6 + n)
                v.wait_ge(s_lg, t + 1)
                ve.tensor_reduce(lmax[:, u:u + 1], mis[:, 0:E], AX.X, ALU.max, negate=True).then_inc(s_lm, 1)
                v.wait_ge(s_ex, t + 2)
                ve.reciprocal(lrec[:, u:u + 1], lsum[:, u:u + 1]).then_inc(s_rc, 1)
                link(1)
                ve.tensor_scalar(prob[:, u, :], prob[:, u, :], lrec[:, u:u + 1], None, ALU.mult).then_inc(s_rc, 1)
                link(2)
                settle(v, s_passed)
                ve.max(top8[:, u, :], prob[:, u, :]).then_inc(s_rc, 1)
                link(3)
                settle(v, s_passed)
                ve.max_index(idx8[:, u, :], top8[:, u, :], prob[:, u, :]).then_inc(s_rc, 1)
                v.wait_ge(s_val, t + 1)
                ve.tensor_copy(pv[:, u, :, 1], top8[:, u, 0:TOPK])
                ve.tensor_scalar(pv[:, u, :, 0], tokid[:, bass.ds(t, 1)].to_broadcast([P, TOPK]), 1.0, None, ALU.add).then_inc(s_rc, 1)
                link(4)
                ve.tensor_copy(idxf[:, u, :], idx8[:, u, :]).then_inc(s_rc, 1)
                link(6)
                ve.tensor_tensor(oh[:, u], iota[:, 0:E].unsqueeze(1).to_broadcast(choices),
                                 idxf[:, u, 0:TOPK].unsqueeze(2).to_broadcast(choices), ALU.is_equal).then_inc(s_oh, 1)
                v.wait_ge(s_oh, t + 1)
                with nc.allow_low_precision("counts up to 16 are exact"):
                    ve.tensor_reduce(mask[:, u, :], oh[:, u].rearrange("p k e -> p e k"), AX.X, ALU.add).then_inc(s_mk, 1)

            def shared_hidden(t, u):
                v.wait_ge(s_sact, t + 1)
                v.wait_ge(s_shf, t + 1)
                v.wait_ge(s_z, t + 1)
                ve.scalar_tensor_tensor(actB[:, u, :], actA[:, u, :], 1.0, shb[:, 0:384], ALU.add, ALU.mult).then_inc(s_dv, 1)
                v.wait_ge(s_dv, t + 1)
                ve.scalar_tensor_tensor(actT[:, u, :], actB[:, u, :], 0.5, shb[:, 512:896], ALU.mult, ALU.mult).then_inc(s_shf, 1)

            def place(t, u):
                v.wait_ge(s_pos, t + 1)
                ve.tensor_tensor(ohm, oh[:, u], posb[:, 0:E].unsqueeze(1).to_broadcast(choices), ALU.mult).then_inc(s_place, 1)
                v.wait_ge(s_place, t * 2 + 1)
                ve.tensor_reduce(posk[:, u, :], ohm, AX.X, ALU.add).then_inc(s_place, 1)
                v.wait_ge(s_place, t * 2 + 2)
                wide = [P, TOPK, CAP]
                ve.tensor_tensor(PO[:, u], iota[:].unsqueeze(1).to_broadcast(wide),
                                 posk[:, u, :].unsqueeze(2).to_broadcast(wide), ALU.is_equal).then_inc(s_po, 1)

            def sum_slots(t):
                v.wait_ge(s_tbl, t + 3)
                v.wait_ge(s_slot, t + 1)
                sf = slots.rearrange("p c e -> p (c e)")
                ve.tensor_tensor(sf, sf, sumb[:, 0:2 * E], ALU.add).then_inc(s_slot, 1)

            def count(t, u):
                v.wait_ge(s_mk, t + 1)
                v.wait_ge(s_seen, t + 1)
                ve.tensor_tensor(seen[:, 1 - u, :], seen[:, u, :], mask[:, u, :], ALU.add).then_inc(s_seen, 1)

            def shared_copy(t):
                v.wait_ge(s_z, t + 3)
                ve.tensor_copy(zall[:, bass.ds(t, 1), :].rearrange("p a m -> p (a m)"), OTp[:, 0:M]).then_inc(s_zf, 1)

            def rows(t, u):
                v.wait_ge(s_hrow, t + 1)
                normalise("D", t, u)

            def ffn_tile(t, u, behind):
                route(t, u)
                shared_hidden(t, u)
                if behind >= 1:
                    place(t - 1, 1 - u)
                count(t, u)
                if behind >= 2:
                    sum_slots(t - 2)
                if behind >= 1:
                    shared_copy(t - 1)

            rows(0, 0)
            for t in range(2):
                rows(t + 1, 1 - t)
                ffn_tile(t, t, t)
            with v.Fori(1, NT // 2 - 1) as it:
                for u in range(2):
                    rows(it * 2 + (u + 1), 1 - u)
                    ffn_tile(it * 2 + u, u, 2)
            rows(NT - 1, 1)
            ffn_tile(NT - 2, 0, 2)
            ffn_tile(NT - 1, 1, 2)
            place(NT - 1, 1)
            sum_slots(NT - 2)
            shared_copy(NT - 1)
            sum_slots(NT - 1)
            v.wait_ge(s_slot, NT + 1)
            link(ve.tensor_scalar(empty, slots[:, 0, :], 0.0, padid[:, 0:1], ALU.is_equal, ALU.mult))
            ve.scalar_tensor_tensor(toku[:], slots[:, 0, :], -1.0, empty, ALU.add, ALU.add).then_inc(s_tok, 1)
            v.wait_ge(s_zf, NT + 1)
            for b in range(B):
                tiles = slice(b * TT, (b + 1) * TT)
                link(ve.tensor_tensor(zall[:, tiles, :], zall[:, tiles, :],
                                      gm[:, 3, b, :].unsqueeze(1).to_broadcast([P, TT, M]), ALU.mult))
                link(ve.tensor_tensor(X[:, tiles, :], X[:, tiles, :], zall[:, tiles, :], ALU.add))
            v.sem_inc(s_tok, 1)

            def expert(e, w):
                v.wait_ge(s_eg, e + 1)
                v.wait_ge(s_eh, e + 1)
                ve.scalar_tensor_tensor(eh[64:64 + I2, w, P:2 * P], eg[0:I2, w, P:2 * P], 1.0, sco[w][0:I2, P:2 * P],
                                        ALU.add, ALU.mult)
                ve.scalar_tensor_tensor(eh[:, w, 0:P], eg[:, w, 0:P], 1.0, sco[w][:, 0:P], ALU.add, ALU.mult).then_inc(s_ed, 1)
                v.wait_ge(s_ed, e + 1)
                if not isinstance(e, int) or e >= 2:
                    v.wait_ge(s_y, e - 1)
                ve.scalar_tensor_tensor(ehT[0:I2, w, P:2 * P], eh[64:64 + I2, w, P:2 * P], 0.5,
                                        sco[w][64:64 + I2, P:2 * P], ALU.mult, ALU.mult)
                ve.scalar_tensor_tensor(ehT[:, w, 0:P], eh[:, w, 0:P], 0.5, sco[w][:, 2 * P:3 * P],
                                        ALU.mult, ALU.mult).then_inc(s_eh, 1)

            expert(0, 0)
            expert(1, 1)
            with v.Fori(1, E // 2) as it:
                for w in range(2):
                    expert(it * 2 + w, w)
            for b in range(B):
                v.wait_ge(s_accl[b], 32)
                tiles = slice(b * TT, (b + 1) * TT)
                link(ve.tensor_tensor(accs[:, tiles, :], accs[:, tiles, :], zall[:, tiles, :], ALU.add))
                link(ve.tensor_tensor(accs[:, tiles, :], accs[:, tiles, :], gm[:, 3, b, :].unsqueeze(1).to_broadcast([P, TT, M]), ALU.mult))
                ve.tensor_tensor(X[:, tiles, :], X[:, tiles, :], accs[:, tiles, :], ALU.add).then_inc(s_fin, 1)

        @block.gpsimd
        def _(pool):
            gp = nc.gpsimd
            for ph in "ABCD":
                s = LNS[ph]
                for k in ("turned", "mm", "used", "free", "hT"):
                    if k in s:
                        pool.sem_inc(s[k], 2)
            for L in (0, 1):
                s = AT[L]
                for k in ("proj", "exp", "ropem", "qk", "xadd", "wos"):
                    pool.sem_inc(s[k], 1)
            for s, k in ((s_qk1c, 2), (s_qk1t, 2), (s_v1, 2), (s_hrow, 2), (s_shf, 2), (s_zf, 1), (s_sh, 2), (s_hst[0], 16), (s_hst[1], 16), (s_ex, 1),
                         (s_po, 1), (s_val, 2), (s_tbl, 2), (s_z, 2), (s_xc, 2), (s_eh, 2), (s_ys, 2)):
                pool.sem_inc(s, k)

            def copies(ph):
                s = LNS[ph]
                with pool.Fori(0, NT // 2) as it:
                    for u in range(2):
                        t = it * 2 + u
                        pool.wait_ge(s["hT"], t + 3)
                        gp.tensor_copy(hT[:, :, bass.ds(t * P, P)], hTs[:, u]).then_inc(s["free"], 1)

            def attention(L):
                s = AT[L]
                np_ = 5 if L == 0 else 4
                with pool.Fori(0, B) as b:
                    with pool.Fori(0, G) as g:
                        n = b * G + g
                        if L == 1:
                            pool.wait_ge(s["proj"], n * np_ + 1)
                            gp.tensor_copy(WQ[0:QR, 0, 0:HG, :], Wq1[:, bass.ds(g * HG, HG), :]).then_inc(s["wqs"], 1)
                        pool.wait_ge(s["proj"], n * np_ + 2)
                        if L == 0:
                            gp.tensor_copy(Vs, vbig[:, bass.ds(b * TT, TT), bass.ds(g * D, D)]).then_inc(s["vs"], 1)
                        else:
                            gp.tensor_copy(Vs[:, :, 0:KVR], V1[:, bass.ds(b * TT, TT), :]).then_inc(s["vs"], 1)
                        if L == 0:
                            for m in range(np_):
                                pool.wait_ge(s["ropem"], n * np_ + (m + 2))
                                r = rt[:, m % 2]
                                dst = QT[:, m, :] if m < HG else Krope
                                gp.tensor_tensor(dst, r[:, 0, :], r[:, 1, :], ALU.add).then_inc(s["qk"], 1)
                        else:
                            pool.wait_ge(s["vs"], n + 1)
                            for m in range(np_):
                                pool.wait_ge(s["ropem"], n * np_ + (m + 2))
                                pool.wait_ge(s["qlow"], n * np_ + (m + 1))
                                r = rt[:, m % 2]
                                gp.tensor_tensor(QT[64:128, m, :], r[64:128, 0, :], r[64:128, 1, :], ALU.add).then_inc(s["qk"], 1)
                        nh = HG if L == 0 else 2
                        if L == 0:
                            pool.wait_ge(s["wo"], n * 16 + 16)
                        else:
                            pool.wait_ge(s["qk"], n * np_ + (np_ + 1))
                        for h in range(nh):
                            src = WOr[:, h, :] if L == 0 else Wvo[:, bass.ds(g * 2 + h, 1), :].rearrange("p a m -> p (a m)")
                            ga = gm[:, 0 if L == 0 else 2, bass.ds(b, 1), :].rearrange("p a m -> p (a m)")
                            last = gp.tensor_tensor(WO[:, h, :], src, ga, ALU.mult)
                        last.then_inc(s["wos"], 1)

            copies("A")
            pool.wait_ge(s_gm, 1)
            attention(0)
            with pool.Fori(0, NT // 2) as it:
                for u in range(2):
                    t = it * 2 + u
                    pool.wait_ge(s_qk1, t + 1)
                    gp.tensor_copy(V1[:, t, :], sq[:, u, P:P + KVR]).then_inc(s_v1, 1)
            pool.wait_ge(s_v1, NT + 2)
            pool.wait_ge(s_cwc, 4)
            attention(1)
            pool.wait_ge(AT[1]["xadd"], B * G * TT + 1)
            gp.memset(zero, 0.0).then_inc(s_zero, 1)
            with pool.Fori(0, B) as b:
                with pool.Fori(0, TT // 2) as it:
                    for u in range(2):
                        t = b * TT + it * 2 + u
                        one_cb = sm[:, 1, bass.ds(b, 1), :].rearrange("p a m -> p (a m)")
                        sb_row = sm[:, 0, bass.ds(b, 1), :].rearrange("p a m -> p (a m)")
                        pool.wait_ge(LNS["D"]["xn"], t + 1)
                        pool.wait_ge(s_hst[u], (b * (TT // 2) + it) * 16 + 16)
                        settle(pool, s_passed)
                        gp.tensor_tensor(hrow[:, u, :], xn[:, u, :], one_cb, ALU.mult).then_inc(s_hp, 1)
                        pool.wait_ge(s_hp, t + 1)
                        settle(pool, s_passed)
                        gp.tensor_tensor(hrow[:, u, :], hrow[:, u, :], sb_row, ALU.add).then_inc(s_hrow, 1)
                        wide = [P, TOPK, 2, E]
                        pool.wait_ge(s_oh, t + 1)
                        pool.wait_ge(s_tbl, t + 1)
                        settle(pool, s_passed)
                        gp.tensor_tensor(VAL[:, u], oh[:, u].unsqueeze(2).to_broadcast(wide),
                                         pv[:, u].unsqueeze(3).to_broadcast(wide), ALU.mult).then_inc(s_val, 1)
            pool.wait_ge(s_tok, 1)
            pool.wait_ge(s_pad, 48)
            for u in range(2):
                pool.wait_ge(s_hst[u], 16 * (NT // 2) + 16)

            def gather(e, w):
                gp.tensor_copy(tokc[:, w:w + 1], toku[:, bass.ds(e, 1)]).then_inc(s_tc, 1)
                pool.wait_ge(s_tc, e + 1)
                settle(pool, s_passed)
                gp.indirect_dma_start(xe[:, w % 4, :], None, hd, bass.IndirectOffsetOnAxis(tokc[:, w:w + 1], 0)).then_inc(s_xe[w % 4], 16)

            def expert(r, w, first=False, last=False):
                e = r * 8 + w
                if not (last and w >= 4):
                    pool.wait_ge(s_xt, e + 1)
                    gather(e + 4, (w + 4) % 8)
                pool.wait_ge(s_ys, e + 3)
                if not (first and w < 2):
                    pool.wait_ge(s_add[w % 2], r * 64 + 16 * (w // 2))
                settle(pool, s_passed)
                gp.indirect_dma_start(accd[w % 2], bass.IndirectOffsetOnAxis(tokc[:, w:w + 1], 0), ys[:, w % 4, :], None,
                                      compute_op=ALU.add).then_inc(s_add[w % 2], 16)

            for e in range(4):
                gather(e, e)
            for w in range(8):
                expert(0, w, first=True)
            with pool.Fori(1, E // 8 - 1) as r:
                for w in range(8):
                    expert(r, w)
            for w in range(8):
                expert(E // 8 - 1, w, last=True)


def _layouts(np, z):
    f = lambda a: np.ascontiguousarray(a)
    kp = lambda w: f(w.reshape(w.shape[0] // 128, 128, -1).transpose(1, 0, 2))
    a = {"x": f(z["L0_attn_x"])}
    a["cT"] = f(np.concatenate([z["L0_c"], z["L1_c"]], 0).T.reshape(2, 128, 4).transpose(1, 0, 2))
    a["wmod"] = f(np.stack([z["L0_wmod"], z["L1_wmod"]]).reshape(2, 2, 128, 1536).transpose(2, 0, 1, 3))
    wq = z["L0_attn_w_aq"].reshape(4, 4, 2, 128, 128).transpose(0, 3, 2, 1, 4)
    wk = z["L0_attn_w_ak"].reshape(4, 1, 2, 128, 128).transpose(0, 3, 2, 1, 4)
    a["wq"] = f(np.concatenate([wq, wk], 3))
    a["wv"] = f(z["L0_attn_w_av"].transpose(1, 0, 2).reshape(2, 128, 512).transpose(1, 0, 2))
    a["wo0"] = f(z["L0_attn_w_ao"].transpose(0, 2, 1, 3))
    a["wff"] = kp(z["L0_ffn_weight"])
    a["ffs"] = f(z["L0_ffn_scale"].reshape(1, 256))
    halves = np.r_[0:64:2, 1:64:2]
    a["wdown"] = kp(np.concatenate([z["L1_attn_wq_down"], z["L1_attn_wkv_down"], z["L1_attn_wk_rope"][:, halves]], 1))
    a["qw"], a["kvw"] = f(z["L1_attn_q_norm_w"].reshape(1, 96)), f(z["L1_attn_kv_norm_w"].reshape(1, 64))
    a["wqu"] = f(z["L1_attn_wq_up"].reshape(96, 16, 128).transpose(2, 1, 0))
    kv = z["L1_attn_wkv_up"].reshape(64, 16, 256)
    a["wku"], a["wvu"] = f(kv[:, :, :128].transpose(2, 1, 0)), f(kv[:, :, 128:].transpose(2, 1, 0))
    a["wo1"] = f(z["L1_attn_wo"].reshape(16, 128, 256).transpose(1, 0, 2))
    a["wqr"] = f(z["L1_attn_wq_rope"].reshape(96, 16, 64)[:, :, halves])
    a["gateT"] = kp(z["L1_ffn_gate_w"].T)
    sw = np.zeros((128, 2, 2, 384), np.float32)
    for w, n in enumerate(("L1_ffn_sw1", "L1_ffn_sw3")):
        sw[:, :, w, :352] = kp(z[n].T)
    a["sw13"] = sw
    sw2 = np.zeros((384, 256), np.float32)
    sw2[:352] = z["L1_ffn_sw2"].T
    a["sw2"] = kp(sw2)
    w1, w3 = (z[n].transpose(0, 2, 1).reshape(64, 2, 128, 176).transpose(0, 2, 1, 3) for n in ("L1_ffn_w1", "L1_ffn_w3"))
    gap = np.zeros((64, 128, 2, 16), np.float32)
    up = np.concatenate([w1[..., :128], w3[..., :128], w1[..., 128:], gap, w3[..., 128:]], 3)
    w2 = z["L1_ffn_w2"].transpose(0, 2, 1)
    a["we"] = f(np.concatenate([up.reshape(64, 128, 736), w2[:, :128]], 2))
    a["we2"] = f(w2[:, 128:])
    return a


def _constants(np):
    bf = np.dtype("bfloat16")
    c = {"ident": np.eye(128, dtype=np.float32), "identb": np.eye(128).astype(bf)}
    c["maskb"] = np.where(np.arange(128)[:, None] < np.arange(128)[None, :], -1e30, 0.0).astype(bf)
    c["trib"] = np.triu(np.ones((128, 128)), 1).astype(bf)
    c["onesb"] = np.ones((128, 128)).astype(bf)
    c["iota"] = np.tile(np.arange(128, dtype=np.float32), (128, 1))
    c["padid"] = (2049 + np.arange(128, dtype=np.float32))[:, None]
    c["tokid"] = (np.arange(16)[None, :] * 128 + np.arange(128)[:, None]).astype(np.float32)
    pos = np.arange(1024, dtype=np.float32)
    f0 = np.power(np.float32(10000.0), -np.arange(64, dtype=np.float32) / np.float32(64))
    ang = (pos[:, None] * f0[None, :]).astype(np.float32).astype(np.float64).T
    q = 128 ** -0.25
    r0 = np.zeros((128, 2, 1024), np.float32)
    r0[:64, 0] = r0[64:, 0] = np.cos(ang) * q
    r0[:64, 1] = np.sin(ang) * q
    r0[64:, 1] = -np.sin(ang) * q
    c["rope0"] = r0
    f1 = (np.float32(1.0) / np.power(np.float32(10000.0), np.arange(0, 64, 2, dtype=np.float32) / np.float32(64))).astype(np.float32)
    ang = (pos[:, None] * f1[None, :]).astype(np.float32).astype(np.float64)
    cos, sin = np.cos(ang), np.sin(ang)
    r1 = np.zeros((128, 2, 1024), np.float32)
    r1[64:96, 0] = r1[96:, 0] = cos.T
    r1[64:96, 1], r1[96:, 1] = sin.T, -sin.T
    c["rope1"] = r1
    k = np.zeros((128, 2, 8, 64), np.float32)
    cs, sn = (m.reshape(8, 128, 32).transpose(1, 0, 2) for m in (cos, sin))
    k[:, 0, :, :32] = k[:, 0, :, 32:] = cs
    k[:, 1, :, :32], k[:, 1, :, 32:] = -sn, sn
    c["kcs"] = k
    return c


def kernel(**inputs):
    import numpy as np
    import concourse.bacc as bacc
    from concourse.bass_utils import run_bass_kernel_spmd

    nc = bacc.Bacc("TRN2", target_bir_lowering=False, num_devices=1)
    arrays = {**_layouts(np, {k: np.asarray(v) for k, v in inputs.items()}), **_constants(np)}
    aps = {k: nc.dram_tensor(f"in_{k}", v.shape, mybir.dt.from_np(v.dtype), kind="ExternalInput").ap() for k, v in arrays.items()}
    out = nc.dram_tensor("out_x", (B, T, M), F32, kind="ExternalOutput").ap()
    program(nc, aps, out)
    r = run_bass_kernel_spmd(nc, [{f"in_{k}": v for k, v in arrays.items()}], core_ids=[0])
    return r.results[0]["out_x"]
```

```python
from contextlib import ExitStack

import concourse.bass as bass
from concourse import mybir

F32 = mybir.dt.float32
BF16 = mybir.dt.bfloat16
U32 = mybir.dt.uint32
ALU = mybir.AluOpType
ACT = mybir.ActivationFunctionType
AX = mybir.AxisListType

P = 128
B, T, M = 2, 1024, 256
KT = M // P
TT = T // P
NT = B * TT
G, HG = 4, 4
D = 128
QR, KVR, DR, DV = 96, 64, 64, 128
RAW = QR + KVR + DR
E, I, TOPK, CAP = 64, 176, 6, 128
I2 = I - P
UP = 2 * P + 64 + I2
WE = KT * UP + M
OUT_PARTS = 4
OUT_TILES = NT // OUT_PARTS
RING = 8
LN_EPS, RMS_EPS, HYP_EPS, MAX_NORM = 1e-5, 1e-6, 1e-7, 0.99
L1_SCALE = float((128 + DR) ** -0.5)
MOD_ROWS = ((0, 2), (0, 5), (1, 2), (1, 5), (1, 3), (1, 4))
AHEAD = 2
PLACES5 = ((1, 2), (2, 1), (2, 2), (5, 1), (5, 2), (6, 1), (6, 2), (7, 1), (TT, 0), (TT, 1))
PLACES4 = ((1, 2), (2, 1), (5, 1), (5, 2), (6, 1), (6, 2), (TT, 0), (TT, 1))


def attention_steps(np_):
    steps, turn, idx = [], 0, AHEAD
    heads = ([HG] if np_ > HG else []) + list(range(HG))
    for i in range(TT + 1):
        work = []
        if i:
            for j in range(i):
                work.append(("T", i - 1, j, turn + j))
                if j:
                    work.append(("A", i - 1, j - 1, turn + j - 1))
            work.append(("R", i - 1, 0, 0))
            work.append(("A", i - 1, i - 1, turn + i - 1))
            turn += i
        done, output = 0, False
        for h in range(HG):
            if i == TT:
                steps.append(("N", 0, h, h))
            elif i:
                steps.append(("S", i, h, HG * i + h))
            upto = len(work) * (h + 1) // HG
            for step in work[done:upto]:
                if step[0] == "A" and step[2] == 0 and i >= 2 and not output:
                    steps.append(("O", i - 2, 0, 0))
                    output = True
                steps.append(step)
            done = upto
            if h == 0 and i >= 2 and not output:
                steps.append(("O", i - 2, 0, 0))
                output = True
            if (i, h) in (PLACES4 if np_ == HG else PLACES5):
                steps.append(("P", int(not np_ <= idx < 2 * np_), heads[idx % np_], idx))
                idx += 1
    steps.append(("O", TT - 1, 0, 0))
    return steps, turn, heads


def copies_first(steps, odd):
    order, held = [], None
    for step in steps:
        if held and (step[0] in "SN" or odd and step[0] in "RO" or step[1] == held[1] and step[0] in "TAR"):
            order.append(held)
            held = None
        if step[0] in "SN":
            held = step
            continue
        order.append(step)
        if held and step[0] == "T" and step[3] % 2 == odd:
            order.append(held)
            held = None
    return order + ([held] if held else [])


NPROJ = (HG + 1, HG)
HALF = T // 2
(STEPS0, TURNS, HEADS0), (STEPS1, _, HEADS1) = (attention_steps(n) for n in NPROJ)
START_DVE = (4, 2)
ACT_STEPS, DVE_STEPS = ([copies_first(s, odd) for s in (STEPS0, STEPS1)] for odd in (0, 1))
STEPS, HEADS = (STEPS0, STEPS1), (HEADS0, HEADS1)
NS = HG * TT


def settle(eng, passed):
    eng.sem_inc(passed, 1)


def program(nc, a, out):
    with ExitStack() as ctx:
        def sb(name, shape, dt=F32):
            return ctx.enter_context(nc.sbuf_tensor(name, shape, dt))

        def sem(name):
            return ctx.enter_context(nc.semaphore(name))

        hd = nc.dram_tensor("h_rows", (B * T + P, M), F32, kind="Internal").ap()
        accd = [nc.dram_tensor(f"routed_sum_{u}", (B * T + P, M), F32, kind="Internal").ap() for u in range(2)]

        X = sb("X", [P, NT, M])
        big = sb("big", [P, 13312])
        hT = sb("hT", [P, KT, B * T])
        vbig = sb("vbig", [P, NT, 512])
        ident = sb("ident", [P, P])
        identb = sb("identb", [P, P], BF16)
        maskb = sb("maskb", [P, P], BF16)
        trib = sb("trib", [P, P], BF16)
        onesb = sb("onesb", [P, P], BF16)
        iota = sb("iota", [P, CAP])
        padid = sb("padid", [P, 1])
        tokid = sb("tokid", [P, NT])
        att = sb("att", [P, 10496])
        rope = att[:, 0:2048].rearrange("p (w t) -> p w t", w=2)
        Wq1 = att[0:QR, 2048:4096].rearrange("p (h n) -> p h n", h=16)
        Wvo = att[:, 4096:6144].rearrange("p (h m) -> p h m", h=8)
        WQ = att[:, 6144:7424].rearrange("p (k h d) -> p k h d", k=KT, h=HG + 1)
        WOr = att[:, 7424:8448].rearrange("p (h m) -> p h m", h=HG)
        WO = att[:, 8448:9472].rearrange("p (h m) -> p h m", h=HG)
        Vs = att[:, 9472:10496].rearrange("p (t d) -> p t d", t=TT)
        ring = att[:, 0:RING * WE].rearrange("p (u n) -> p u n", u=RING)
        ring2 = att[0:I2, RING * WE:RING * (WE + M)].rearrange("p (u n) -> p u n", u=RING)
        cT = sb("cT", [P, KT, 4])
        sg = sb("sg", [P, KT, 4])
        sc = sb("sc", [P, KT, 4])
        modT = sb("modT", [P, 2, 12, B])
        gm = sb("gm", [P, 4, B, M])
        sm = sb("sm", [P, 2, B, M])
        Wff = sb("Wff", [P, KT, M])
        sc_bc = sb("sc_bc", [P, M])
        Wdown = sb("Wdown", [P, KT, RAW])
        qw_bc = sb("qw_bc", [P, QR])
        kvw_bc = sb("kvw_bc", [P, KVR])
        gateT = sb("gateT", [P, KT, E])
        st = sb("st", [P, NT, 6])
        t16 = sb("t16", [P, 12, NT])
        rtv = sb("rtv", [P, 4 * T])
        rt = rtv[:, 0:4 * HALF].rearrange("p (u w t) -> p u w t", u=2, w=2)
        gs = rtv[:, 0:2048].rearrange("p (a b m) -> p a b m", a=4, b=B)
        scb = rtv[:, 2048:3072].rearrange("p (k c n) -> p k c n", k=KT, c=4)
        Wv = rtv[:, 3072:4096].rearrange("p (k n) -> p k n", k=KT)
        kcs = rtv[:, 0:1024].rearrange("p (w t r) -> p w t r", w=2, t=TT)
        sw13 = rtv[:, 0:1536].rearrange("p (k w n) -> p k w n", k=KT, w=2)
        sw2 = rtv[:, 1536:2304].rearrange("p (k m) -> p k m", k=3)
        nmax = sb("nmax", [P, 2])
        rsum = sb("rsum", [P, 2, HG])
        rinv = sb("rinv", [P, 2, HG])
        PTs = sb("PTs", [P, 2, HG * P])
        Rs = sb("Rs", [P, HG * P])
        OTs = sb("OTs", [P, HG * P])
        xn = Rs[:, :].rearrange("p (u m) -> p u m", u=2)
        hTs = PTs[:, 0, :].rearrange("p (u k q) -> p u k q", u=2, k=KT)

        Pr = big[:, 0:8192].rearrange("p (u h k) -> p u h k", u=2, h=HG)
        QT = big[:, 8192:12288].rearrange("p (h t) -> p h t", h=HG)
        rope_v = Pr[:, 0, 0:2, :].rearrange("p u (w t) -> p u w t", w=2)
        K0 = big[:, 12288:12800], rtv[:, 3072:3584]
        K1 = big[:, 12800:13312]
        wmod = big[:, 0:6144].rearrange("p (l k n) -> p l k n", l=2, k=KT)
        wqu = att[:, 7424:8960].rearrange("p (h n) -> p h n", h=16)
        wku = att[:, 8960:9984].rearrange("p (h n) -> p h n", h=16)
        wvu = big[:, 6144:7168].rearrange("p (h n) -> p h n", h=16)
        wo1 = big[:, 7168:11264].rearrange("p (h n) -> p h n", h=16)
        ffo = vbig[:, :, 0:M]
        raw = vbig[:, :, 0:RAW]
        V1 = vbig[:, :, 384:448]
        krows = vbig[:, :, 384:512]
        rope_b = rtv[:, 2048:3072].rearrange("p (t r) -> p t r", t=NT)
        gffo = big[:, 0:NT * M].rearrange("p (t m) -> p t m", t=NT)
        qcT = hT[0:QR, 0, :]
        KT1 = hT[:, 1, :]
        def two(lo, n):
            return big[:, lo:lo + 2 * n].rearrange("p (u n) -> p u n", u=2)

        hrow, zero = two(0, M), big[:, 512:768]
        actA, actB, actT = two(768, 384), two(1536, 384), two(2304, 384)
        PO = big[:, 3072:4608].rearrange("p (u k c) -> p u k c", u=2, k=TOPK)
        VAL = big[:, 4608:6144].rearrange("p (u k c e) -> p u k c e", u=2, k=TOPK, c=2)
        oh = big[:, 6144:6528].bitcast(BF16).rearrange("p (u k e) -> p u k e", u=2, k=TOPK)
        ohm = big[:, 6528:6912].rearrange("p (k e) -> p k e", k=TOPK)
        prob, top8 = two(6912, E), two(7040, 8)
        idx8 = big[:, 7056:7072].bitcast(U32).rearrange("p (u k) -> p u k", u=2)
        idxf, posk = two(7072, 8), two(7088, TOPK)
        lmax, lsum, lrec = big[:, 7100:7102], big[:, 7102:7104], big[:, 7104:7106]
        pv = big[:, 7106:7130].rearrange("p (u k c) -> p u k c", u=2, k=TOPK)
        mask = big[:, 7168:7232].bitcast(BF16).rearrange("p (u e) -> p u e", u=2)
        seen = big[:, 7232:7296].bitcast(BF16).rearrange("p (u e) -> p u e", u=2)
        slots = big[:, 7296:7424].rearrange("p (c e) -> p c e", c=2)
        empty = big[:, 7424:7488]
        xe = big[:, 7680:8704].rearrange("p (u n) -> p u n", u=4)
        xeT, eg, eh, ehT = two(8704, M), two(9216, M), two(9728, M), two(10240, M)
        ys = big[:, 10752:11776].rearrange("p (u n) -> p u n", u=4)
        toku = sb("toku", [P, E], U32)
        tokc = sb("tokc", [P, 8], U32)
        zall = vbig[:, :, 256:512]
        accs = vbig[:, :, 0:M]

        ps = [ctx.enter_context(nc.psum_tensor(f"ps{i}", [P, 512], F32)) for i in range(4)]
        sco = [ctx.enter_context(nc.psum_tensor(f"sco{i}", [P, 1024], F32)) for i in range(2)]
        ptp, OTp, mis = ps[0:2], ps[2], ps[3]
        START_BANKS = mis[:, :], sco[0][:, 0:HALF]
        shb, posb, sumb = sco[0], sco[1][:, 0:512], sco[1][:, 512:1024]

        s_passed = sem("waits_passed")
        s_x = sem("x_loaded")
        s_c = sem("consts_loaded")
        s_wm = sem("wmod_loaded")
        s_w1 = sem("l1_weights_loaded")
        s_sw = sem("small_weights_loaded")
        s_ch = sem("vector_chain")
        s_ac = sem("scalar_chain")
        s_sg = sem("silu_then_gates")
        s_mT = sem("modT_matmuls")
        s_mTc = sem("modT_copied")
        s_mb = sem("mod_rows_matmuls")
        s_mbc = sem("mod_rows_copied")
        s_cw = sem("joined_weight_matmuls")
        s_cwc = sem("joined_weights_copied")
        s_rope1 = sem("l1_rope_loaded")
        s_sws = sem("shared_weights_loaded")

        LNS = {}
        for ph in "ABCD":
            names = ["stats", "var", "std", "ready", "turned", "hT"]
            names += ["xn"]
            names += ["mm", "used"] if ph != "D" else []
            names += ["free"] if ph == "A" else []
            LNS[ph] = {k: sem(f"{k}_{ph}") for k in names}
        s_fss, s_ffv, s_fft, s_fff = sem("ffn_squares"), sem("ffn_norm"), sem("ffn_tanh"), sem("ffn_done")
        s_rss, s_rms, s_rmsd = sem("raw_squares"), sem("rms_root_in"), sem("rms_root")
        s_qk1, s_qk1t, s_qk1c, s_v1 = sem("l1_rows"), sem("l1_turned"), sem("l1_turned_copied"), sem("l1_key_ropes")
        AT = {}
        for L in (0, 1):
            names = ["wos", "vs", "proj", "pc", "ropem", "qk", "scores", "nmax", "exp", "turn", "ptA", "ptV", "av", "rinv", "rt",
                     "rs", "ot", "op", "xadd"]
            names += ["wq", "wo"] if L == 0 else ["wqs"]
            AT[L] = {k: sem(f"{k}_L{L}") for k in names}
        s_hrow, s_hp = sem("h_rows_made"), sem("h_row_parts")
        s_hst = [sem(f"h_rows_stored_{u}") for u in range(2)]
        s_xe = [sem(f"expert_rows_{u}") for u in range(4)]
        s_lg, s_sh, s_sact, s_dv, s_shf, s_z, s_zf = (
            sem("logits"), sem("shared_products"), sem("shared_tanh"), sem("shared_chain"),
            sem("shared_hidden"), sem("shared_out"), sem("shared_out_copied"))
        s_lm, s_ex, s_rc, s_oh, s_mk, s_seen, s_pos, s_po, s_val, s_tbl, s_slot = (
            sem("logit_maxima"), sem("router_exps"), sem("router_chain"), sem("choices_one_hot"), sem("choice_mask"),
            sem("choices_seen"), sem("positions"), sem("positions_one_hot"), sem("choice_values"), sem("slot_products"),
            sem("slots_summed"))
        s_place = sem("place_chain")
        s_pad, s_zero, s_tok = sem("dram_set"), sem("zero_tile"), sem("token_ids")
        s_ew = [sem(f"expert_weights_{u}") for u in range(RING)]
        s_tc, s_xt, s_xc, s_gu, s_eg, s_ed, s_eh, s_y, s_ys = (
            sem("expert_ids"), sem("expert_turned"), sem("expert_turned_copied"), sem("expert_up"),
            sem("expert_tanh"), sem("expert_chain"), sem("expert_hidden"), sem("expert_down"), sem("expert_scaled"))
        s_add = [sem(f"expert_added_{u}") for u in range(2)]
        s_fin, s_out = sem("out_ready"), sem("out_stored")

        block = ctx.enter_context(nc.Block())
        xv = a["x"].rearrange("b (t p) m -> p (b t) m", p=P)
        ov = out.rearrange("b (t p) m -> p (b t) m", p=P)

        @block.sync
        def _(sp):
            sp.dma_start(cT[:], a["cT"]).then_inc(s_wm, 16)
            sp.dma_start(wmod[:, 0], a["wmod"][:, 0]).then_inc(s_wm, 16)
            sp.dma_start(X[:], xv).then_inc(s_x, 16)
            for t, n in ((ident, "ident"), (identb, "identb"), (maskb, "maskb"), (trib, "trib"), (onesb, "onesb"), (iota, "iota"),
                         (padid, "padid"), (tokid, "tokid"), (rope, "rope0"), (Wv, "wv")):
                sp.dma_start(t[:], a[n]).then_inc(s_c, 16)
            sp.dma_start(wmod[:, 1], a["wmod"][:, 1]).then_inc(s_w1, 16)
            sp.dma_start(wqu, a["wqu"]).then_inc(s_w1, 16)
            sp.dma_start(wku, a["wku"]).then_inc(s_w1, 16)
            sp.dma_start(wvu, a["wvu"]).then_inc(s_w1, 16)
            sp.dma_start(wo1, a["wo1"]).then_inc(s_w1, 16)
            sp.dma_start(Wq1[:, :, KVR:D], a["wqr"]).then_inc(s_w1, 16)
            for t, n in ((Wff, "wff"), (Wdown, "wdown"), (gateT, "gateT")):
                sp.dma_start(t[:], a[n]).then_inc(s_sw, 16)
            sp.dma_start(sc_bc[:], a["ffs"].to_broadcast([P, M])).then_inc(s_sw, 16)
            sp.dma_start(qw_bc[:], a["qw"].to_broadcast([P, QR])).then_inc(s_sw, 16)
            sp.dma_start(kvw_bc[:], a["kvw"].to_broadcast([P, KVR])).then_inc(s_sw, 16)
            s = AT[0]
            np_ = NPROJ[0]
            sp.dma_start(WQ, a["wq"][0]).then_inc(s["wq"], 16)
            sp.wait_ge(s_cw, 1)
            sp.dma_start(WOr, a["wo0"][0]).then_inc(s["wo"], 16)
            with sp.Fori(1, G) as g:
                sp.wait_ge(s["proj"], g * (2 * B * np_))
                sp.dma_start(WQ, a["wq"][g]).then_inc(s["wq"], 16)
                sp.wait_ge(s["wos"], g * B)
                sp.dma_start(WOr, a["wo0"][g]).then_inc(s["wo"], 16)
            sp.wait_ge(s["qk"], 2 * np_ * B * G)
            sp.dma_start(rope, a["rope1"]).then_inc(s_rope1, 16)
            sp.dma_start(kcs, a["kcs"]).then_inc(s_rope1, 16)
            sp.wait_ge(AT[1]["qk"], 2 * NPROJ[1] * B * G)
            sp.dma_start(sw13, a["sw13"]).then_inc(s_sws, 16)
            sp.dma_start(sw2, a["sw2"]).then_inc(s_sws, 16)
            sp.wait_ge(AT[1]["xadd"], B * G * TT + 1)
            for u in range(RING):
                sp.dma_start(ring[:, u, :], a["we"][u]).then_inc(s_ew[u], 16)
                sp.dma_start(ring2[:, u, :], a["we2"][u]).then_inc(s_ew[u], 16)
            sp.wait_ge(s_zero, 1)
            sp.dma_start(hd[B * T:B * T + P, :], zero).then_inc(s_pad, 16)
            for u in range(2):
                sp.dma_start(accd[u].rearrange("(t p) m -> p t m", p=P), zero.unsqueeze(1).to_broadcast([P, NT + 1, M])).then_inc(s_pad, 16)
            with sp.Fori(0, NT // 2) as it:
                for u in range(2):
                    sp.wait_ge(s_hrow, it * 2 + (u + 3))
                    sp.dma_start(hd[bass.ds((it * 2 + u) * P, P), :], hrow[:, u, :]).then_inc(s_hst[u], 16)
            with sp.Fori(1, E // RING) as r:
                for u in range(RING):
                    sp.wait_ge(s_y, (r - 1) * RING + (u + 1))
                    sp.dma_start(ring[:, u, :], a["we"][r * RING + u]).then_inc(s_ew[u], 16)
                    sp.dma_start(ring2[:, u, :], a["we2"][r * RING + u]).then_inc(s_ew[u], 16)
            for u in range(2):
                sp.wait_ge(s_add[u], 16 * (E // 2))
            for c in range(OUT_PARTS):
                w = slice(c * OUT_TILES, (c + 1) * OUT_TILES)
                for u, dst in enumerate((accs, zall)):
                    sp.dma_start(dst[:, w, :], accd[u][w.start * P:w.stop * P, :].rearrange("(t p) m -> p t m", p=P))\
                      .then_inc(s_ew[c], 16)
            for c in range(OUT_PARTS):
                w = slice(c * OUT_TILES, (c + 1) * OUT_TILES)
                sp.wait_ge(s_fin, c + 1)
                sp.dma_start(ov[:, w, :], X[:, w, :]).then_inc(s_out, 16)
            sp.wait_ge(s_out, 16 * OUT_PARTS)
            for u in range(2):
                sp.wait_ge(s_hst[u], 16 * (NT // 2) + 16)
            sp.wait_ge(s_pad, 48)

        @block.tensor
        def _(pe):
            mm, tr = nc.tensor.matmul, nc.tensor.transpose

            def modulation(l):
                for c in range(12):
                    for k in range(KT):
                        last = mm(mis[:, 2 * c:2 * c + 2], wmod[:, l, k, c * P:(c + 1) * P], sc[:, k, 2 * l:2 * l + 2],
                                  start=(k == 0), stop=(k == KT - 1))
                last.then_inc(s_mT, 1)

            def modulation_rows(n):
                l, c = MOD_ROWS[n]
                if n >= 2:
                    pe.wait_ge(s_mbc, n - 1)
                for b in range(B):
                    for k in range(KT):
                        last = mm(ptp[n % 2][:, b * M:(b + 1) * M], scb[:, k, 2 * l + b, :],
                                  wmod[:, l, k, c * M:(c + 1) * M], start=(k == 0), stop=(k == KT - 1))
                last.then_inc(s_mb, 1)

            def joined_weights():
                for h in range(16):
                    last = mm(sco[0][0:QR, h * KVR:(h + 1) * KVR], wqu[:, h, :], wku[:, h, :], start=True, stop=True)
                last.then_inc(s_cw, 1)
                for h in range(16):
                    half = KVR * (h % 2)
                    if h % 8 == 0 and h:
                        pe.wait_ge(s_cwc, h // 8 + 1)
                    last = mm(sco[1][half:half + KVR, (h // 2) % 4 * M:(h // 2) % 4 * M + M], wvu[:, h, :], wo1[:, h, :],
                              start=True, stop=True)
                    if h % 8 == 7:
                        last.then_inc(s_cw, 1)

            def turn_h(ph, t, u):
                s = LNS[ph]
                pe.wait_ge(s["xn"], t + 1)
                pe.wait_ge(s["hT"], t + 1)
                for k in range(KT):
                    last = tr(ptp[u][:, k * P:(k + 1) * P], xn[:, u, k * P:(k + 1) * P], ident[:])
                last.then_inc(s["turned"], 1)

            def project_h(ph, t, u, W, N, bank):
                s = LNS[ph]
                pe.wait_ge(s["hT"], t + 3)
                pe.wait_ge(s["used"], t + 1)
                for k in range(KT):
                    last = mm(bank[:, 0:N], hTs[:, u, k, :], W[:, k, :], start=(k == 0), stop=(k == KT - 1))
                last.then_inc(s["mm"], 1)

            def layer_norm_products(ph, W, N):
                turn_h(ph, 0, 0)
                with pe.Fori(0, NT // 2 - 1) as it:
                    for u in range(2):
                        turn_h(ph, it * 2 + (u + 1), 1 - u)
                        project_h(ph, it * 2 + u, u, W, N, ps[2 + u])
                turn_h(ph, NT - 1, 1)
                for u in range(2):
                    project_h(ph, NT - 2 + u, u, W, N, ps[2 + u])

            def attention(L):
                s, np_ = AT[L], NPROJ[L]

                def project(b, half, m, done, o=mis[:, :], open_=0):
                    if not isinstance(done, int) or done > open_:
                        pe.wait_ge(s["pc"], done - open_)
                    cols = slice(b * T + half * HALF, b * T + (half + 1) * HALF)
                    if L == 0:
                        for k in range(KT):
                            last = mm(o, WQ[:, k, m, :], hT[:, k, cols], start=(k == 0), stop=(k == KT - 1))
                    else:
                        last = mm(o, WQ[0:QR, 0, m, :], qcT[:, cols], start=True, stop=True)
                    last.then_inc(s["proj"], 1)

                def score(n, b, i, j, c):
                    pe.wait_ge(s["exp"], n * NS + (c + 1))
                    o = sco[c % 2]
                    w = (i + 1) * P
                    for c0 in range(0, w, 512):
                        c1 = min(w, c0 + 512)
                        if L == 0:
                            k_rhs = (K0[b] if c0 == 0 else K1)[:, 0:c1 - c0]
                        else:
                            k_rhs = KT1[:, b * T + c0:b * T + c1]
                        mm(o[:, c0:c1], QT[:, j, i * P:(i + 1) * P], k_rhs, start=True, stop=(c1 < w))
                    mm(o[:, i * P:w], identb[:], maskb[:], start=False, stop=True).then_inc(s["scores"], 1)

                def group(g, b, last):
                    n = g * B + b
                    before = n * (2 * np_) + np_
                    user = ("O", TT - 1, -1)
                    for kind, i, j, c in STEPS[L]:
                        if kind == "P" and c >= np_ and last:
                            continue
                        if kind in "ROP":
                            if user[0] == "O":
                                pe.wait_ge(s["xadd"], (n + user[2]) * TT + (user[1] + 2))
                            elif user[0] == "R":
                                pe.wait_ge(s["rs"], n * TT + (user[1] + 1))
                            else:
                                pe.wait_ge(s["pc"], before + (user[1] + 1))
                            user = (kind, c if kind == "P" else i, 0)
                        if kind == "P":
                            if i == 0 and b == B - 1 and c == np_:
                                if L == 0:
                                    pe.wait_ge(s["wq"], g * 16 + 32)
                                else:
                                    pe.wait_ge(s["wqs"], g + 2)
                            project(b if c < np_ else 1 - b, i, j, before + c)
                        elif kind == "S":
                            if c == NS // 2:
                                pe.wait_ge(s["qk"], before + np_)
                            score(n, b, i, j, c)
                        elif kind == "N":
                            if not last:
                                if c == 0:
                                    pe.wait_ge(s["qk"], before + 2 * np_)
                                score(n + 1, 1 - b, i, j, c)
                        elif kind == "T":
                            if j == 0:
                                pe.wait_ge(s["exp"], n * NS + (HG * i + HG + 2))
                            for h in range(HG):
                                last_ = tr(ptp[c % 2][:, h * P:(h + 1) * P], Pr[:, i % 2, h, j * P:(j + 1) * P], ident[:])
                            last_.then_inc(s["turn"], 1)
                        elif kind == "A":
                            if c == 0:
                                pe.wait_ge(s["vs"], n + 1)
                            if c % 2 == 0:
                                pe.wait_ge(s["ptA"], n * (TURNS // 2) + (c // 2 + 1))
                            else:
                                pe.wait_ge(s["ptV"], n * (TURNS // 2) + (c // 2 + 1))
                            if L == 0:
                                last_ = mm(OTp[:, :], Vs[:, j, :], PTs[:, c % 2, :], start=(j == 0), stop=(j == i))
                            else:
                                pt = PTs[:, c % 2, :].rearrange("p (a s q) -> p s a q", s=2, q=P)
                                for half in range(2):
                                    last_ = mm(OTp[half * 64:half * 64 + 64, 0:256], Vs[:, j, 0:KVR], pt[:, half],
                                               start=(j == 0), stop=(j == i))
                            if j == i:
                                last_.then_inc(s["av"], 1)
                        elif kind == "R":
                            pe.wait_ge(s["rinv"], n * TT + (i + 1))
                            if L == 0:
                                for h in range(HG):
                                    last_ = tr(mis[:, h * P:(h + 1) * P], rinv[:, i % 2, h:h + 1].to_broadcast([P, P]), ident[:])
                            else:
                                for h in range(HG):
                                    last_ = mm(mis[h % 2 * 64:h % 2 * 64 + 64, h // 2 * P:(h // 2 + 1) * P],
                                               rinv[:, i % 2, h:h + 1].to_broadcast([P, 64]), ident[:], start=True, stop=True)
                            last_.then_inc(s["rt"], 1)
                        else:
                            pe.wait_ge(s["ot"], n * TT + (i + 1))
                            if i == 0:
                                pe.wait_ge(s["wos"], n + 1)
                            nh = HG if L == 0 else 2
                            for h in range(nh):
                                last_ = mm(mis[:, 0:M], OTs[:, h * P:(h + 1) * P], WO[:, h, :], start=(h == 0), stop=(h == nh - 1))
                            last_.then_inc(s["op"], 1)

                if L == 0:
                    pe.wait_ge(s["wq"], 16)
                else:
                    pe.wait_ge(s["wqs"], 1)
                for c, m in enumerate(HEADS[L]):
                    project(0, 0, m, c, START_BANKS[c % 2], 1)
                for c in range(AHEAD):
                    project(0, 1, HEADS[L][c], np_ + c, START_BANKS[(np_ + c) % 2], 1)
                pe.wait_ge(s["pc"], np_ + AHEAD)
                pe.wait_ge(s["qk"], np_)
                for h in range(HG):
                    score(0, 0, 0, h, h)
                with pe.Fori(0, G - 1) as g:
                    for b in range(B):
                        group(g, b, False)
                for b in range(B):
                    group(G - 1, b, b == B - 1)

            pe.wait_ge(s_sg, 1)
            pe.wait_ge(s_wm, 32)
            modulation(0)
            modulation_rows(0)
            modulation_rows(1)
            pe.wait_ge(s_c, 16 * 10)
            pe.wait_ge(s_mbc, 2)
            pe.wait_ge(s_mTc, 1)
            layer_norm_products("A", Wv, 512)
            pe.wait_ge(LNS["A"]["used"], NT + 2)
            pe.wait_ge(LNS["A"]["free"], NT + 2)
            pe.wait_ge(s_w1, 96)
            modulation(1)
            for n in range(2, 6):
                modulation_rows(n)
            joined_weights()
            pe.wait_ge(s_mbc, 6)
            pe.wait_ge(s_mTc, 3)
            pe.wait_ge(s_cwc, 3)
            attention(0)
            pe.wait_ge(s_sw, 16 * 6)
            for ph, W, N in (("B", Wff, M), ("C", Wdown, RAW)):
                layer_norm_products(ph, W, N)
            pe.wait_ge(LNS["C"]["used"], NT + 2)
            pe.wait_ge(s_v1, 8)
            for t in range(NT):
                u = t % 2
                pe.wait_ge(s_qk1, t + 1)
                pe.wait_ge(s_qk1c, t + 1)
                tr(ptp[u][0:QR, 0:P], raw[:, t, 0:QR], ident[:])
                tr(ptp[u][:, P:2 * P], krows[:, t, :], ident[:]).then_inc(s_qk1t, 1)
            pe.wait_ge(s_qk1c, NT + 2)
            attention(1)

            def shared_out(t, u):
                pe.wait_ge(s_shf, t + 3)
                pe.wait_ge(s_zf, t + 1)
                for c in range(3):
                    last = mm(OTp[:, 0:M], actT[:, u, c * P:(c + 1) * P], sw2[:, c, :], start=(c == 0), stop=(c == 2))
                last.then_inc(s_z, 1)

            def positions(t, u):
                pe.wait_ge(s_mk, t + 1)
                pe.wait_ge(s_seen, t + 1)
                pe.wait_ge(s_po, t + 1)
                mm(posb[:, 0:E], trib[:], mask[:, u, :], start=True, stop=False)
                mm(posb[:, 0:E], onesb[:], seen[:, u, :], start=False, stop=True).then_inc(s_pos, 1)

            def slot_sums(t, u):
                pe.wait_ge(s_po, t + 2)
                pe.wait_ge(s_val, t + 3)
                pe.wait_ge(s_slot, t + 1)
                for k in range(TOPK):
                    last = mm(sumb[:, 0:2 * E], PO[:, u, k, :], VAL[:, u, k, :, :].rearrange("p c e -> p (c e)"),
                              start=(k == 0), stop=(k == TOPK - 1))
                last.then_inc(s_tbl, 1)

            def ffn_tile(t, u, behind):
                pe.wait_ge(LNS["D"]["hT"], t + 3)
                pe.wait_ge(s_ex, t + 1)
                for k in range(KT):
                    last = mm(mis[:, 0:E], hTs[:, u, k, :], gateT[:, k, :], start=(k == 0), stop=(k == KT - 1))
                last.then_inc(s_lg, 1)
                pe.wait_ge(s_shf, t + 2)
                for w in range(2):
                    for c in range(3):
                        for k in range(KT):
                            last = mm(shb[:, w * 512 + c * P:w * 512 + (c + 1) * P], sw13[:, k, w, c * P:(c + 1) * P],
                                      hTs[:, u, k, :], start=(k == 0), stop=(k == KT - 1))
                last.then_inc(s_sh, 1)
                if behind >= 1:
                    positions(t - 1, 1 - u)
                if behind >= 2:
                    slot_sums(t - 2, u)
                if behind >= 1:
                    shared_out(t - 1, 1 - u)

            pe.wait_ge(s_sws, 32)
            turn_h("D", 0, 0)
            for t in range(2):
                turn_h("D", t + 1, 1 - t)
                ffn_tile(t, t, t)
            with pe.Fori(1, NT // 2 - 1) as it:
                for u in range(2):
                    turn_h("D", it * 2 + (u + 1), 1 - u)
                    ffn_tile(it * 2 + u, u, 2)
            turn_h("D", NT - 1, 1)
            ffn_tile(NT - 2, 0, 2)
            ffn_tile(NT - 1, 1, 2)
            positions(NT - 1, 1)
            slot_sums(NT - 2, 0)
            shared_out(NT - 1, 1)
            slot_sums(NT - 1, 1)

            outs = (OTp, mis)

            def turn_rows(e, w, gathers):
                v = w % 2
                pe.wait_ge(s_xe[w % 4], gathers * 16)
                pe.wait_ge(s_xc, e + 1)
                for k in range(KT):
                    last = tr(ptp[v][:, k * P:(k + 1) * P], xe[:, w % 4, k * P:(k + 1) * P], ident[:])
                last.then_inc(s_xt, 1)

            def up(e, v, u, r):
                pe.wait_ge(s_ew[u], r * 32 + 32)
                pe.wait_ge(s_xc, e + 3)
                pe.wait_ge(s_eh, e + 1)
                for c, o in ((2, sco[v][0:64 + I2, P:2 * P]), (0, sco[v][:, 0:P]), (1, sco[v][:, 2 * P:3 * P])):
                    for k in range(KT):
                        last = mm(o, ring[:, u, k * UP + c * P:k * UP + min(c * P + P, UP)], xeT[:, v, k * P:(k + 1) * P],
                                  start=(k == 0), stop=(k == KT - 1))
                last.then_inc(s_gu, 1)

            def down(e, v, u):
                pe.wait_ge(s_eh, e + 3)
                pe.wait_ge(s_ys, e + 1)
                mm(outs[v][:, 0:M], ehT[:, v, 0:P], ring[:, u, KT * UP:WE], start=True, stop=False)
                mm(outs[v][:, 0:M], ehT[0:I2, v, P:2 * P], ring2[:, u, :], start=False, stop=True).then_inc(s_y, 1)

            def expert_group(r, first=False, last=False):
                for u in range(RING):
                    e = r * RING + u
                    up(e, u % 2, u, r)
                    if not (last and u == RING - 1):
                        turn_rows(e + 1, u + 1, r * (RING // 4) + (u + 1) // 4 + 1)
                    if not (first and u == 0):
                        down(e - 1, (u + 1) % 2, (u - 1) % RING)

            pe.wait_ge(s_zf, NT + 1)
            pe.wait_ge(s_shf, NT + 2)
            pe.wait_ge(s_slot, NT + 1)
            turn_rows(0, 0, 1)
            expert_group(0, first=True)
            with pe.Fori(1, E // RING - 1) as r:
                expert_group(r)
            expert_group(E // RING - 1, last=True)
            down(E - 1, 1, RING - 1)

        @block.scalar
        def _(act):
            af = nc.scalar.activation

            def turned_copies(ph, shift, scale, layer, squares=None):
                s = LNS[ph]
                for t in range(NT + 2):
                    if t < NT:
                        act.wait_ge(s["turned"], t + 3)
                        act.wait_ge(s["mm"], t + 1)
                        if ph == "A":
                            act.wait_ge(s["free"], t + 1)
                        u, b = t % 2, t // TT
                        for k in range(KT):
                            last = af(hTs[:, u, k, :], ptp[u][:, k * P:(k + 1) * P], ACT.Identity,
                                      bias=modT[:, layer, 2 * shift + k, b:b + 1], scale=modT[:, layer, 2 * scale + k, b:b + 1])
                        last.then_inc(s["hT"], 1)
                    if squares and t >= 2:
                        act.wait_ge(s["used"], t + 1)
                        squares(t - 2)

            def root(ph):
                act.wait_ge(LNS[ph]["var"], 1)
                af(t16[:, 4, :], t16[:, 3, :], ACT.Sqrt).then_inc(LNS[ph]["std"], 1)

            def attention(L):
                s, np_ = AT[L], NPROJ[L]

                def exponent(n, i, j, c):
                    act.wait_ge(s["nmax"], n * NS + (c + 1))
                    af(Pr[:, i % 2, j, 0:(i + 1) * P], sco[c % 2][:, 0:(i + 1) * P], ACT.Exp,
                       bias=nmax[:, c % 2:c % 2 + 1], accum_out=rsum[:, i % 2, j:j + 1]).then_inc(s["exp"], 1)

                def projected(b, half, m, done, o=mis[:, :]):
                    act.wait_ge(s["proj"], done + 1)
                    dst = QT[:, m, half * HALF:(half + 1) * HALF] if m < HG else K1 if half else K0[b]
                    af(dst, o, ACT.Copy).then_inc(s["pc"], 1)

                def group(g, b, last):
                    n = g * B + b
                    before = n * (2 * np_) + np_
                    for kind, i, j, c in ACT_STEPS[L]:
                        if kind == "P" and not (c >= np_ and last):
                            projected(b if c < np_ else 1 - b, i, j, before + c)
                        elif kind == "S" or kind == "N" and not last:
                            exponent(n + (kind == "N"), i, j, c)
                        elif kind == "T" and c % 2 == 0:
                            act.wait_ge(s["turn"], n * TURNS + (c + 1))
                            af(PTs[:, 0, :], ptp[0][:, :], ACT.Copy).then_inc(s["ptA"], 1)
                        elif kind == "R":
                            act.wait_ge(s["rt"], n * TT + (i + 1))
                            w = HG * P if L == 0 else 2 * P
                            af(Rs[:, 0:w], mis[:, 0:w], ACT.Copy).then_inc(s["rs"], 1)

                for c, m in enumerate(HEADS[L]):
                    projected(0, 0, m, c, START_BANKS[c % 2])
                for c in range(AHEAD):
                    projected(0, 1, HEADS[L][c], np_ + c, START_BANKS[(np_ + c) % 2])
                for h in range(HG):
                    exponent(0, 0, h, h)
                with act.Fori(0, G - 1) as g:
                    for b in range(B):
                        group(g, b, False)
                for b in range(B):
                    group(G - 1, b, b == B - 1)

            act.wait_ge(s_wm, 32)
            af(sg[:], cT[:], ACT.Exp, scale=-1.0).then_inc(s_ac, 1)
            root("A")

            def modulation_copy(l):
                act.wait_ge(s_mT, l + 1)
                af(modT[:, l].rearrange("p c b -> p (c b)"), mis[:, 0:24], ACT.Copy).then_inc(s_mTc, 1)

            modulation_copy(0)
            act.wait_ge(s_mTc, 2)
            turned_copies("A", 0, 1, 0)
            modulation_copy(1)
            attention(0)
            root("B")
            turned_copies("B", 3, 4, 0, lambda t: af(vbig[:, t, M:2 * M], ffo[:, t, :], ACT.Square,
                                                     accum_out=t16[:, 5, t:t + 1]).then_inc(s_fss, 1))
            act.wait_ge(s_fss, NT)
            af(t16[:, 6, :], t16[:, 5, :], ACT.Sqrt).then_inc(s_ffv, 1)
            act.wait_ge(s_ffv, 2)
            af(t16[:, 8, :], t16[:, 7, :], ACT.Tanh).then_inc(s_fft, 1)
            root("C")

            def raw_squares(t):
                af(vbig[:, t, RAW:RAW + QR], raw[:, t, 0:QR], ACT.Square, accum_out=t16[:, 5, t:t + 1]).then_inc(s_rss, 1)
                af(vbig[:, t, RAW + QR:RAW + QR + KVR], raw[:, t, QR:QR + KVR], ACT.Square, accum_out=t16[:, 6, t:t + 1]).then_inc(s_rss, 1)

            turned_copies("C", 0, 1, 1, raw_squares)
            act.wait_ge(s_rms, 1)
            af(t16[:, 7:9, :], t16[:, 5:7, :], ACT.Sqrt).then_inc(s_rmsd, 1)
            for t in range(NT):
                act.wait_ge(s_qk1t, t + 1)
                af(hT[0:QR, 0, t * P:(t + 1) * P], ptp[t % 2][0:QR, 0:P], ACT.Copy)
                af(hT[:, 1, t * P:(t + 1) * P], ptp[t % 2][:, P:2 * P], ACT.Copy).then_inc(s_qk1c, 1)
            attention(1)
            root("D")

            def turned_copy(t):
                u, b = t % 2, t // TT
                act.wait_ge(LNS["D"]["turned"], t + 3)
                act.wait_ge(s_sh, t + 1)
                for k in range(KT):
                    last = af(hTs[:, u, k, :], ptp[u][:, k * P:(k + 1) * P], ACT.Identity,
                              bias=modT[:, 1, 6 + k, b:b + 1], scale=modT[:, 1, 8 + k, b:b + 1])
                last.then_inc(LNS["D"]["hT"], 1)

            def shared_copy(t):
                act.wait_ge(s_z, t + 3)
                af(zall[:, t, :], OTp[:, 0:M], ACT.Copy).then_inc(s_zf, 1)

            turned_copy(0)
            for t in range(NT):
                u = t % 2
                act.wait_ge(s_lm, t + 1)
                af(prob[:, u, :], mis[:, 0:E], ACT.Exp, bias=lmax[:, u:u + 1], accum_out=lsum[:, u:u + 1]).then_inc(s_ex, 1)
                act.wait_ge(s_sh, t + 3)
                act.wait_ge(s_shf, t + 1)
                af(actA[:, u, :], shb[:, 0:384], ACT.Tanh, scale=0.5).then_inc(s_sact, 1)
                if t + 1 < NT:
                    turned_copy(t + 1)
                if t:
                    shared_copy(t - 1)
            shared_copy(NT - 1)

            def rows_copy(e, v):
                act.wait_ge(s_xt, e + 1)
                af(xeT[:, v, :], ptp[v][:, 0:M], ACT.Copy).then_inc(s_xc, 1)

            def expert(e, w, first=False, last=False):
                v = w % 2
                act.wait_ge(s_gu, e + 1)
                af(eg[0:I2, v, P:2 * P], sco[v][0:I2, P:2 * P], ACT.Tanh, scale=0.5)
                af(eg[:, v, 0:P], sco[v][:, 0:P], ACT.Tanh, scale=0.5).then_inc(s_eg, 1)
                if not last:
                    rows_copy(e + 1, 1 - v)
                if not first:
                    scaled(e - 1, (w - 1) % 4)

            def scaled(e, w):
                act.wait_ge(s_y, e + 1)
                if isinstance(e, int):
                    if e >= 4:
                        act.wait_ge(s_add[w % 2], 16 * (e // 2 - 1))
                    gate = slots[:, 1, e:e + 1]
                else:
                    act.wait_ge(s_add[w % 2], e * 8 - (16 + 8 * (w % 2)))
                    gate = slots[:, 1, bass.ds(e, 1)]
                settle(act, s_passed)
                af(ys[:, w, :], (OTp, mis)[w % 2][:, 0:M], ACT.Copy, scale=gate).then_inc(s_ys, 1)

            rows_copy(0, 0)
            for e in range(8):
                expert(e, e % 4, first=(e == 0))
            with act.Fori(2, E // 4 - 1) as it:
                for w in range(4):
                    expert(it * 4 + w, w)
            for e in range(E - 4, E):
                expert(e, e % 4, last=(e == E - 1))
            scaled(E - 1, 3)

        @block.vector
        def _(v):
            ve = nc.vector
            chain = [0]

            def link(ins):
                chain[0] += 1
                ins.then_inc(s_ch, 1)
                v.wait_ge(s_ch, chain[0])

            def statistics(ph, rows_made=False):
                s = LNS[ph]
                if not rows_made:
                    for t in range(NT):
                        ve.bn_stats(st[:, t, :], X[:, t, :]).then_inc(s["stats"], 1)
                v.wait_ge(s["stats"], NT)
                link(ve.tensor_tensor(t16[:, 0, :], st[:, :, 1], st[:, :, 4], ALU.add))
                link(ve.tensor_tensor(t16[:, 1, :], st[:, :, 1], st[:, :, 4], ALU.subtract))
                link(ve.tensor_tensor(t16[:, 2, :], st[:, :, 2], st[:, :, 5], ALU.add))
                link(ve.scalar_tensor_tensor(t16[:, 1, :], t16[:, 1, :], 0.25, t16[:, 1, :], ALU.mult, ALU.mult))
                link(ve.scalar_tensor_tensor(t16[:, 2, :], t16[:, 2, :], 1.0 / M, t16[:, 1, :], ALU.mult, ALU.add))
                ve.tensor_scalar(t16[:, 3, :], t16[:, 2, :], LN_EPS, None, ALU.add).then_inc(s["var"], 1)
                v.wait_ge(s["std"], 1)
                link(ve.reciprocal(t16[:, 2, :], t16[:, 4, :]))
                ve.scalar_tensor_tensor(t16[:, 1, :], t16[:, 0, :], -0.5, t16[:, 2, :], ALU.mult, ALU.mult).then_inc(s["ready"], 1)
                v.wait_ge(s["ready"], 1)

            def normalise(ph, t, u):
                s = LNS[ph]
                v.wait_ge(s["turned"], t + 1)
                ve.tensor_scalar(xn[:, u, :], X[:, bass.ds(t, 1), :].rearrange("p a m -> p (a m)"), t16[:, 2, bass.ds(t, 1)],
                                 t16[:, 1, bass.ds(t, 1)], ALU.mult, ALU.add).then_inc(s["xn"], 1)

            def layer_norm(ph, keep):
                s = LNS[ph]

                def kept(t, u):
                    v.wait_ge(s["mm"], t + 3)
                    keep(t, u).then_inc(s["used"], 1)

                normalise(ph, 0, 0)
                normalise(ph, 1, 1)
                with v.Fori(0, NT // 2 - 1) as it:
                    for u in range(2):
                        normalise(ph, it * 2 + (u + 2), u)
                        kept(it * 2 + u, u)
                kept(NT - 2, 0)
                kept(NT - 1, 1)

            def attention(L):
                s = AT[L]

                def maximum(n, i, c):
                    v.wait_ge(s["scores"], n * NS + (c + 1))
                    ve.tensor_reduce(nmax[:, c % 2:c % 2 + 1], sco[c % 2][:, 0:(i + 1) * P], AX.X, ALU.max,
                                     negate=True).then_inc(s["nmax"], 1)

                def row_statistics(n, t):
                    v.wait_ge(s["xadd"], n * TT + (t % TT + 2))
                    ve.bn_stats(st[:, t, :], X[:, t, :]).then_inc(LNS["BD"[L]]["stats"], 1)

                def group(g, b, last=False):
                    n = g * B + b
                    for kind, i, j, c in DVE_STEPS[L]:
                        if kind == "O" and last and i:
                            row_statistics(n, b * TT + i - 1)
                        if kind == "S" or kind == "N" and not (last and b == B - 1):
                            maximum(n + (kind == "N"), i, c)
                        elif kind == "T":
                            if j == 0:
                                v.wait_ge(s["exp"], n * NS + (HG * i + HG + 2))
                                ve.reciprocal(rinv[:, i % 2, :], rsum[:, i % 2, :]).then_inc(s["rinv"], 1)
                            if c % 2 == 1:
                                v.wait_ge(s["turn"], n * TURNS + (c + 1))
                                ve.tensor_copy(PTs[:, 1, :], ptp[1][:, :]).then_inc(s["ptV"], 1)
                        elif kind == "R":
                            v.wait_ge(s["av"], n * TT + (i + 1))
                            v.wait_ge(s["rs"], n * TT + (i + 1))
                            w = HG * P if L == 0 else 2 * P
                            ve.tensor_tensor(OTs[:, 0:w], OTp[:, 0:w], Rs[:, 0:w], ALU.mult).then_inc(s["ot"], 1)
                        elif kind == "O":
                            v.wait_ge(s["op"], n * TT + (i + 1))
                            xt = X[:, b * TT + i, :]
                            ve.tensor_tensor(xt, mis[:, 0:M], xt, ALU.add).then_inc(s["xadd"], 1)

                    if last:
                        row_statistics(n, b * TT + TT - 1)

                lo, mid = (0, 64) if L == 0 else (64, 96)
                mine = range(NPROJ[L] - START_DVE[L], NPROJ[L])
                for c in mine:
                    v.wait_ge(s["pc"], c + 1)
                    q, r = QT[:, HEADS[L][c], 0:HALF], rope_v[:, c % 2]
                    link(ve.tensor_tensor(r[lo:P, 0, :], q[lo:P], rope[lo:P, 0, 0:HALF], ALU.mult))
                    link(ve.tensor_tensor(r[lo:mid, 1, :], q[mid:P], rope[mid:P, 1, 0:HALF], ALU.mult))
                    link(ve.tensor_tensor(r[mid:P, 1, :], q[lo:mid], rope[lo:mid, 1, 0:HALF], ALU.mult))
                    link(ve.tensor_tensor(q[lo:P], r[lo:P, 0, :], r[lo:P, 1, :], ALU.add))
                v.wait_ge(s["qk"], mine[0])
                v.sem_inc(s["qk"], len(mine))
                for h in range(HG):
                    maximum(0, 0, h)

                with v.Fori(0, G - 1) as g:
                    for b in range(B):
                        group(g, b)
                for b in range(B):
                    group(G - 1, b, last=True)

            v.wait_ge(s_ac, 1)
            v.wait_ge(s_wm, 32)
            link(ve.tensor_scalar(sg[:], sg[:], 1.0, None, ALU.add))
            link(ve.reciprocal(sg[:], sg[:]))
            link(ve.tensor_tensor(sc[:], sg[:], cT[:], ALU.mult))
            ve.tensor_copy(scb, sc[:].unsqueeze(3).to_broadcast([P, KT, 4, P])).then_inc(s_sg, 1)
            v.wait_ge(s_x, 16)
            statistics("A")

            def modulation(l):
                v.wait_ge(s_mTc, 2 * l + 1)
                for c in (1, 4):
                    last = ve.tensor_scalar(modT[:, l, 2 * c:2 * c + 2, :], modT[:, l, 2 * c:2 * c + 2, :], 1.0, None, ALU.add)
                last.then_inc(s_mTc, 1)

            def modulation_rows(n):
                v.wait_ge(s_mb, n + 1)
                src = ptp[n % 2][:, :].rearrange("p (b m) -> p b m", b=B)
                if n < 4:
                    ve.tensor_copy(gm[:, n], src).then_inc(s_mbc, 1)
                else:
                    ve.tensor_scalar(sm[:, n - 4], src, float(n - 4), None, ALU.add).then_inc(s_mbc, 1)

            def gates(l):
                gf = gm[:, 2 * l:2 * l + 2].rearrange("p a b m -> p (a b m)")
                sf = gs[:, 2 * l:2 * l + 2].rearrange("p a b m -> p (a b m)")
                link(ve.tensor_scalar(sf, gf, 0.0, 2.0, ALU.is_ge, ALU.mult))
                link(ve.scalar_tensor_tensor(gf, gf, -1.0, gf, ALU.mult, ALU.max))
                link(ve.tensor_scalar(gf, gf, 0.25, None, ALU.max))
                ve.scalar_tensor_tensor(gf, sf, -1.0, gf, ALU.add, ALU.mult).then_inc(s_sg, 1)

            modulation(0)
            modulation_rows(0)
            modulation_rows(1)
            layer_norm("A", lambda t, u: ve.tensor_copy(vbig[:, t, :], ps[2 + u][:, :]))
            v.wait_ge(s_mbc, 2)
            gates(0)
            modulation(1)
            for n in range(2, 6):
                modulation_rows(n)
            v.wait_ge(s_mbc, 6)
            gates(1)
            v.wait_ge(s_cw, 1)
            ve.tensor_scalar(Wq1[:, :, 0:KVR], sco[0][0:QR, :].rearrange("p (h n) -> p h n", h=16), L1_SCALE, None,
                             ALU.mult).then_inc(s_cwc, 1)
            for n in range(2):
                v.wait_ge(s_cw, n + 2)
                ve.tensor_copy(Wvo[:, 4 * n:4 * n + 4, :], sco[1][:, :].rearrange("p (h m) -> p h m", h=4)).then_inc(s_cwc, 1)
            v.wait_ge(s_w1, 96)
            ve.tensor_scalar(Wq1[:, :, KVR:D], Wq1[:, :, KVR:D], L1_SCALE, None, ALU.mult).then_inc(s_cwc, 1)
            attention(0)
            v.wait_ge(AT[0]["xadd"], B * G * TT + 1)
            statistics("B", rows_made=True)
            layer_norm("B", lambda t, u: ve.tensor_tensor(ffo[:, t, :], ps[2 + u][:, 0:M], sc_bc[:], ALU.mult))
            v.wait_ge(s_ffv, 1)
            ve.tensor_scalar(t16[:, 7, :], t16[:, 6, :], HYP_EPS, None, ALU.max).then_inc(s_ffv, 1)
            v.wait_ge(s_ffv, 2)
            link(ve.tensor_scalar(t16[:, 9, :], t16[:, 7, :], HYP_EPS, None, ALU.add))
            link(ve.reciprocal(t16[:, 9, :], t16[:, 9, :]))
            v.wait_ge(s_fft, 1)
            link(ve.tensor_tensor(t16[:, 9, :], t16[:, 9, :], t16[:, 8, :], ALU.mult))
            link(ve.tensor_tensor(t16[:, 10, :], t16[:, 9, :], t16[:, 6, :], ALU.mult))
            link(ve.tensor_scalar(t16[:, 10, :], t16[:, 10, :], HYP_EPS, None, ALU.max))
            link(ve.reciprocal(t16[:, 10, :], t16[:, 10, :]))
            link(ve.tensor_scalar(t16[:, 10, :], t16[:, 10, :], MAX_NORM, 1.0, ALU.mult, ALU.min))
            link(ve.tensor_tensor(t16[:, 9, :], t16[:, 9, :], t16[:, 10, :], ALU.mult))
            v.wait_ge(s_fss, NT)
            for t in range(NT):
                v.wait_ge(s_fff, max(t + 1, NT))
                ve.scalar_tensor_tensor(X[:, t, :], gffo[:, t, :], t16[:, 9, t:t + 1], X[:, t, :],
                                        ALU.mult, ALU.add).then_inc(s_fff, 1)
            for t in range(NT):
                v.wait_ge(s_fff, NT + t + 1)
                ve.bn_stats(st[:, t, :], X[:, t, :]).then_inc(LNS["C"]["stats"], 1)
            statistics("C", rows_made=True)
            layer_norm("C", lambda t, u: ve.tensor_copy(raw[:, t, :], ps[2 + u][:, 0:RAW]))
            v.wait_ge(s_rss, 2 * NT)
            link(ve.tensor_scalar(t16[:, 5, :], t16[:, 5, :], 1.0 / QR, RMS_EPS, ALU.mult, ALU.add))
            ve.tensor_scalar(t16[:, 6, :], t16[:, 6, :], 1.0 / KVR, RMS_EPS, ALU.mult, ALU.add).then_inc(s_rms, 1)
            v.wait_ge(s_rmsd, 1)
            link(ve.reciprocal(t16[:, 5:7, :], t16[:, 7:9, :]))
            for t in range(NT):
                ve.scalar_tensor_tensor(raw[:, t, 0:QR], raw[:, t, 0:QR], t16[:, 5, t:t + 1], qw_bc[:], ALU.mult, ALU.mult)
                ve.scalar_tensor_tensor(V1[:, t, :], raw[:, t, QR:QR + KVR], t16[:, 6, t:t + 1], kvw_bc[:],
                                        ALU.mult, ALU.mult).then_inc(s_qk1, 1)
            attention(1)
            v.wait_ge(AT[1]["xadd"], B * G * TT + 1)
            statistics("D", rows_made=True)
            ve.memset(seen[:, 0, :], 0.0).then_inc(s_seen, 1)
            ve.memset(slots, 0.0).then_inc(s_slot, 1)
            choices = [P, TOPK, E]

            def route(t, u):
                def link(n):
                    v.wait_ge(s_rc, t * 6 + n)
                v.wait_ge(s_lg, t + 1)
                ve.tensor_reduce(lmax[:, u:u + 1], mis[:, 0:E], AX.X, ALU.max, negate=True).then_inc(s_lm, 1)
                v.wait_ge(s_ex, t + 2)
                ve.reciprocal(lrec[:, u:u + 1], lsum[:, u:u + 1]).then_inc(s_rc, 1)
                link(1)
                ve.tensor_scalar(prob[:, u, :], prob[:, u, :], lrec[:, u:u + 1], None, ALU.mult).then_inc(s_rc, 1)
                link(2)
                settle(v, s_passed)
                ve.max(top8[:, u, :], prob[:, u, :]).then_inc(s_rc, 1)
                link(3)
                settle(v, s_passed)
                ve.max_index(idx8[:, u, :], top8[:, u, :], prob[:, u, :]).then_inc(s_rc, 1)
                v.wait_ge(s_val, t + 1)
                ve.tensor_copy(pv[:, u, :, 1], top8[:, u, 0:TOPK])
                ve.tensor_scalar(pv[:, u, :, 0], tokid[:, bass.ds(t, 1)].to_broadcast([P, TOPK]), 1.0, None, ALU.add).then_inc(s_rc, 1)
                link(4)
                ve.tensor_copy(idxf[:, u, :], idx8[:, u, :]).then_inc(s_rc, 1)
                link(6)
                ve.tensor_tensor(oh[:, u], iota[:, 0:E].unsqueeze(1).to_broadcast(choices),
                                 idxf[:, u, 0:TOPK].unsqueeze(2).to_broadcast(choices), ALU.is_equal).then_inc(s_oh, 1)
                v.wait_ge(s_oh, t + 1)
                with nc.allow_low_precision("counts up to 16 are exact"):
                    ve.tensor_reduce(mask[:, u, :], oh[:, u].rearrange("p k e -> p e k"), AX.X, ALU.add).then_inc(s_mk, 1)

            def shared_hidden(t, u):
                v.wait_ge(s_sact, t + 1)
                v.wait_ge(s_shf, t + 1)
                v.wait_ge(s_z, t + 1)
                ve.scalar_tensor_tensor(actB[:, u, :], actA[:, u, :], 1.0, shb[:, 0:384], ALU.add, ALU.mult).then_inc(s_dv, 1)
                v.wait_ge(s_dv, t + 1)
                ve.scalar_tensor_tensor(actT[:, u, :], actB[:, u, :], 0.5, shb[:, 512:896], ALU.mult, ALU.mult).then_inc(s_shf, 1)

            def place(t, u):
                v.wait_ge(s_pos, t + 1)
                ve.tensor_tensor(ohm, oh[:, u], posb[:, 0:E].unsqueeze(1).to_broadcast(choices), ALU.mult).then_inc(s_place, 1)
                v.wait_ge(s_place, t * 2 + 1)
                ve.tensor_reduce(posk[:, u, :], ohm, AX.X, ALU.add).then_inc(s_place, 1)
                v.wait_ge(s_place, t * 2 + 2)
                wide = [P, TOPK, CAP]
                ve.tensor_tensor(PO[:, u], iota[:].unsqueeze(1).to_broadcast(wide),
                                 posk[:, u, :].unsqueeze(2).to_broadcast(wide), ALU.is_equal).then_inc(s_po, 1)

            def sum_slots(t):
                v.wait_ge(s_tbl, t + 3)
                v.wait_ge(s_slot, t + 1)
                sf = slots.rearrange("p c e -> p (c e)")
                ve.tensor_tensor(sf, sf, sumb[:, 0:2 * E], ALU.add).then_inc(s_slot, 1)

            def count(t, u):
                v.wait_ge(s_mk, t + 1)
                v.wait_ge(s_seen, t + 1)
                ve.tensor_tensor(seen[:, 1 - u, :], seen[:, u, :], mask[:, u, :], ALU.add).then_inc(s_seen, 1)

            def rows(t, u):
                v.wait_ge(s_hrow, t + 1)
                normalise("D", t, u)

            def ffn_tile(t, u, behind):
                route(t, u)
                shared_hidden(t, u)
                if behind >= 1:
                    place(t - 1, 1 - u)
                count(t, u)
                if behind >= 2:
                    sum_slots(t - 2)

            rows(0, 0)
            rows(1, 1)
            for t in range(2):
                rows(t + 2, t)
                ffn_tile(t, t, t)
            with v.Fori(1, NT // 2 - 1) as it:
                for u in range(2):
                    rows(it * 2 + (u + 2), u)
                    ffn_tile(it * 2 + u, u, 2)
            ffn_tile(NT - 2, 0, 2)
            ffn_tile(NT - 1, 1, 2)
            place(NT - 1, 1)
            sum_slots(NT - 2)
            sum_slots(NT - 1)
            v.wait_ge(s_slot, NT + 1)
            link(ve.tensor_scalar(empty, slots[:, 0, :], 0.0, padid[:, 0:1], ALU.is_equal, ALU.mult))
            ve.scalar_tensor_tensor(toku[:], slots[:, 0, :], -1.0, empty, ALU.add, ALU.add).then_inc(s_tok, 1)
            v.wait_ge(s_zf, NT + 1)
            for b in range(B):
                tiles = slice(b * TT, (b + 1) * TT)
                link(ve.tensor_tensor(zall[:, tiles, :], zall[:, tiles, :],
                                      gm[:, 3, b, :].unsqueeze(1).to_broadcast([P, TT, M]), ALU.mult))
                link(ve.tensor_tensor(X[:, tiles, :], X[:, tiles, :], zall[:, tiles, :], ALU.add))
            v.sem_inc(s_tok, 1)

            def expert(e, w):
                v.wait_ge(s_eg, e + 1)
                v.wait_ge(s_eh, e + 1)
                ve.scalar_tensor_tensor(eh[64:64 + I2, w, P:2 * P], eg[0:I2, w, P:2 * P], 1.0, sco[w][0:I2, P:2 * P],
                                        ALU.add, ALU.mult)
                ve.scalar_tensor_tensor(eh[:, w, 0:P], eg[:, w, 0:P], 1.0, sco[w][:, 0:P], ALU.add, ALU.mult).then_inc(s_ed, 1)
                v.wait_ge(s_ed, e + 1)
                if not isinstance(e, int) or e >= 2:
                    v.wait_ge(s_y, e - 1)
                ve.scalar_tensor_tensor(ehT[0:I2, w, P:2 * P], eh[64:64 + I2, w, P:2 * P], 0.5,
                                        sco[w][64:64 + I2, P:2 * P], ALU.mult, ALU.mult)
                ve.scalar_tensor_tensor(ehT[:, w, 0:P], eh[:, w, 0:P], 0.5, sco[w][:, 2 * P:3 * P],
                                        ALU.mult, ALU.mult).then_inc(s_eh, 1)

            expert(0, 0)
            expert(1, 1)
            with v.Fori(1, E // 2) as it:
                for w in range(2):
                    expert(it * 2 + w, w)
            for c in range(OUT_PARTS):
                w = slice(c * OUT_TILES, (c + 1) * OUT_TILES)
                v.wait_ge(s_ew[c], 32 * (E // RING) + 32)
                link(ve.tensor_tensor(accs[:, w, :], accs[:, w, :], zall[:, w, :], ALU.add))
                link(ve.tensor_tensor(accs[:, w, :], accs[:, w, :],
                                      gm[:, 3, w.start // TT, :].unsqueeze(1).to_broadcast([P, OUT_TILES, M]), ALU.mult))
                ve.tensor_tensor(X[:, w, :], X[:, w, :], accs[:, w, :], ALU.add).then_inc(s_fin, 1)

        @block.gpsimd
        def _(pool):
            gp = nc.gpsimd
            for ph in "ABCD":
                s = LNS[ph]
                for k in ("turned", "mm", "used", "free", "hT"):
                    if k in s:
                        pool.sem_inc(s[k], 2)
            for L in (0, 1):
                s = AT[L]
                pool.sem_inc(s["exp"], 2)
                pool.sem_inc(s["xadd"], 1)
            for s, k in ((s_qk1c, 2), (s_hrow, 2), (s_shf, 2), (s_zf, 1), (s_sh, 2), (s_hst[0], 16), (s_hst[1], 16), (s_ex, 1),
                         (s_po, 1), (s_val, 2), (s_tbl, 2), (s_z, 2), (s_xc, 2), (s_eh, 2), (s_ys, 2)):
                pool.sem_inc(s, k)

            def copies(ph):
                s = LNS[ph]
                with pool.Fori(0, NT // 2) as it:
                    for u in range(2):
                        t = it * 2 + u
                        pool.wait_ge(s["hT"], t + 3)
                        gp.tensor_copy(hT[:, :, bass.ds(t * P, P)], hTs[:, u]).then_inc(s["free"], 1)

            def attention(L):
                s, np_ = AT[L], NPROJ[L]
                lo, mid = (0, 64) if L == 0 else (64, 96)

                def roped(b, half, m, done, theirs=START_DVE[L]):
                    pool.wait_ge(s["pc"], done + 1)
                    mine = done - theirs
                    r, w = rt[:, HEADS[L].index(m) % 2], slice(half * HALF, (half + 1) * HALF)
                    q = QT[:, m, w] if m < HG else K1 if half else K0[b]
                    gp.tensor_tensor(r[lo:P, 0, :], q[lo:P], rope[lo:P, 0, w], ALU.mult).then_inc(s["ropem"], 1)
                    pool.wait_ge(s["ropem"], mine * 3 + 1)
                    gp.tensor_tensor(r[lo:mid, 1, :], q[mid:P], rope[mid:P, 1, w], ALU.mult).then_inc(s["ropem"], 1)
                    pool.wait_ge(s["ropem"], mine * 3 + 2)
                    gp.tensor_tensor(r[mid:P, 1, :], q[lo:mid], rope[lo:mid, 1, w], ALU.mult).then_inc(s["ropem"], 1)
                    pool.wait_ge(s["ropem"], mine * 3 + 3)
                    gp.tensor_tensor(q[lo:P], r[lo:P, 0, :], r[lo:P, 1, :], ALU.add).then_inc(s["qk"], 1)
                    pool.wait_ge(s["qk"], done + 1)

                def query_weights(heads):
                    gp.tensor_copy(WQ[0:QR, 0, 0:HG, :], Wq1[:, heads, :]).then_inc(s["wqs"], 1)

                def group(g, b, last):
                    n = g * B + b
                    before = n * (2 * np_) + np_
                    pool.wait_ge(s["xadd"], n * TT + 1)
                    settle(pool, s_passed)
                    if L == 0:
                        gp.tensor_copy(Vs, vbig[:, b * TT:(b + 1) * TT, bass.ds(g * D, D)]).then_inc(s["vs"], 1)
                        pool.wait_ge(s["wo"], g * 16 + 16)
                    else:
                        gp.tensor_copy(Vs[:, :, 0:KVR], V1[:, b * TT:(b + 1) * TT, :]).then_inc(s["vs"], 1)
                    nh = HG if L == 0 else 2
                    for h in range(nh):
                        src = WOr[:, h, :] if L == 0 else Wvo[:, bass.ds(g * 2 + h, 1), :].rearrange("p a m -> p (a m)")
                        last_ = gp.tensor_tensor(WO[:, h, :], src, gm[:, 0 if L == 0 else 2, b, :], ALU.mult)
                    last_.then_inc(s["wos"], 1)
                    pool.wait_ge(s["wos"], n + 1)
                    for c in range(AHEAD, np_):
                        roped(b, 1, HEADS[L][c], before + c)
                    if not last:
                        if L == 1 and b == B - 1:
                            pool.wait_ge(s["proj"], before + np_)
                            query_weights(bass.ds(g * HG + HG, HG))
                            pool.wait_ge(s["wqs"], g + 2)
                        for c, m in enumerate(HEADS[L]):
                            roped(1 - b, 0, m, before + (np_ + c))
                        for c in range(AHEAD):
                            roped(1 - b, 1, HEADS[L][c], before + (2 * np_ + c))

                if L == 1:
                    query_weights(slice(0, HG))
                    pool.wait_ge(s["wqs"], 1)
                for c, m in enumerate(HEADS[L][:np_ - START_DVE[L]]):
                    roped(0, 0, m, c, 0)
                for c in range(AHEAD):
                    roped(0, 1, HEADS[L][c], np_ + c)
                with pool.Fori(0, G - 1) as g:
                    for b in range(B):
                        group(g, b, False)
                for b in range(B):
                    group(G - 1, b, b == B - 1)

            copies("A")
            pool.wait_ge(s_sg, 3)
            pool.wait_ge(s_c, 16 * 10)
            attention(0)
            for t in range(NT):
                pool.wait_ge(LNS["B"]["used"], t + 3)
                gp.tensor_tensor(gffo[:, t, :], ffo[:, t, :], gm[:, 1, t // TT, :], ALU.mult).then_inc(s_fff, 1)
            pool.wait_ge(s_rope1, 32)
            for b in range(B):
                tiles = slice(b * TT, (b + 1) * TT)
                x1, x2 = raw[:, tiles, QR + KVR:QR + KVR + 32], raw[:, tiles, QR + KVR + 32:RAW]
                pool.wait_ge(LNS["C"]["used"], (b + 1) * TT + 2)
                gp.tensor_tensor(krows[:, tiles, KVR:P], raw[:, tiles, QR + KVR:RAW], kcs[:, 0], ALU.mult).then_inc(s_v1, 1)
                gp.tensor_tensor(rope_b[:, tiles, 0:32], x2, kcs[:, 1, :, 0:32], ALU.mult).then_inc(s_v1, 1)
                gp.tensor_tensor(rope_b[:, tiles, 32:64], x1, kcs[:, 1, :, 32:64], ALU.mult).then_inc(s_v1, 1)
                pool.wait_ge(s_v1, b * 4 + 3)
                gp.tensor_tensor(krows[:, tiles, KVR:P], krows[:, tiles, KVR:P], rope_b[:, tiles, :], ALU.add).then_inc(s_v1, 1)
            pool.wait_ge(s_v1, 4 * B)
            pool.wait_ge(s_qk1, NT)
            pool.wait_ge(s_cwc, 4)
            pool.wait_ge(s_rope1, 32)
            attention(1)
            pool.wait_ge(AT[1]["xadd"], B * G * TT + 1)
            gp.memset(zero, 0.0).then_inc(s_zero, 1)
            with pool.Fori(0, B) as b:
                with pool.Fori(0, TT // 2) as it:
                    for u in range(2):
                        t = b * TT + it * 2 + u
                        one_cb = sm[:, 1, bass.ds(b, 1), :].rearrange("p a m -> p (a m)")
                        sb_row = sm[:, 0, bass.ds(b, 1), :].rearrange("p a m -> p (a m)")
                        pool.wait_ge(LNS["D"]["xn"], t + 1)
                        pool.wait_ge(s_hst[u], (b * (TT // 2) + it) * 16 + 16)
                        settle(pool, s_passed)
                        gp.tensor_tensor(hrow[:, u, :], xn[:, u, :], one_cb, ALU.mult).then_inc(s_hp, 1)
                        pool.wait_ge(s_hp, t + 1)
                        settle(pool, s_passed)
                        gp.tensor_tensor(hrow[:, u, :], hrow[:, u, :], sb_row, ALU.add).then_inc(s_hrow, 1)
                        wide = [P, TOPK, 2, E]
                        pool.wait_ge(s_oh, t + 1)
                        pool.wait_ge(s_tbl, t + 1)
                        settle(pool, s_passed)
                        gp.tensor_tensor(VAL[:, u], oh[:, u].unsqueeze(2).to_broadcast(wide),
                                         pv[:, u].unsqueeze(3).to_broadcast(wide), ALU.mult).then_inc(s_val, 1)
            pool.wait_ge(s_tok, 1)
            pool.wait_ge(s_pad, 48)
            for u in range(2):
                pool.wait_ge(s_hst[u], 16 * (NT // 2) + 16)

            def gather(e, w):
                gp.tensor_copy(tokc[:, w:w + 1], toku[:, bass.ds(e, 1)]).then_inc(s_tc, 1)
                pool.wait_ge(s_tc, e + 1)
                settle(pool, s_passed)
                gp.indirect_dma_start(xe[:, w % 4, :], None, hd, bass.IndirectOffsetOnAxis(tokc[:, w:w + 1], 0)).then_inc(s_xe[w % 4], 16)

            def expert(r, w, first=False, last=False):
                e = r * 8 + w
                if not (last and w >= 4):
                    pool.wait_ge(s_xt, e + 1)
                    gather(e + 4, (w + 4) % 8)
                pool.wait_ge(s_ys, e + 3)
                if not (first and w < 2):
                    pool.wait_ge(s_add[w % 2], r * 64 + 16 * (w // 2))
                settle(pool, s_passed)
                gp.indirect_dma_start(accd[w % 2], bass.IndirectOffsetOnAxis(tokc[:, w:w + 1], 0), ys[:, w % 4, :], None,
                                      compute_op=ALU.add).then_inc(s_add[w % 2], 16)

            for e in range(4):
                gather(e, e)
            for w in range(8):
                expert(0, w, first=True)
            with pool.Fori(1, E // 8 - 1) as r:
                for w in range(8):
                    expert(r, w)
            for w in range(8):
                expert(E // 8 - 1, w, last=True)


def _layouts(np, z):
    f = lambda a: np.ascontiguousarray(a)
    kp = lambda w: f(w.reshape(w.shape[0] // 128, 128, -1).transpose(1, 0, 2))
    a = {"x": f(z["L0_attn_x"])}
    a["cT"] = f(np.concatenate([z["L0_c"], z["L1_c"]], 0).T.reshape(2, 128, 4).transpose(1, 0, 2))
    a["wmod"] = f(np.stack([z["L0_wmod"], z["L1_wmod"]]).reshape(2, 2, 128, 1536).transpose(2, 0, 1, 3))
    wq = z["L0_attn_w_aq"].reshape(4, 4, 2, 128, 128).transpose(0, 3, 2, 1, 4)
    wk = z["L0_attn_w_ak"].reshape(4, 1, 2, 128, 128).transpose(0, 3, 2, 1, 4)
    a["wq"] = f(np.concatenate([wq, wk], 3))
    a["wv"] = f(z["L0_attn_w_av"].transpose(1, 0, 2).reshape(2, 128, 512).transpose(1, 0, 2))
    a["wo0"] = f(z["L0_attn_w_ao"].transpose(0, 2, 1, 3))
    a["wff"] = kp(z["L0_ffn_weight"])
    a["ffs"] = f(z["L0_ffn_scale"].reshape(1, 256))
    halves = np.r_[0:64:2, 1:64:2]
    a["wdown"] = kp(np.concatenate([z["L1_attn_wq_down"], z["L1_attn_wkv_down"], z["L1_attn_wk_rope"][:, halves]], 1))
    a["qw"], a["kvw"] = f(z["L1_attn_q_norm_w"].reshape(1, 96)), f(z["L1_attn_kv_norm_w"].reshape(1, 64))
    a["wqu"] = f(z["L1_attn_wq_up"].reshape(96, 16, 128).transpose(2, 1, 0))
    kv = z["L1_attn_wkv_up"].reshape(64, 16, 256)
    a["wku"], a["wvu"] = f(kv[:, :, :128].transpose(2, 1, 0)), f(kv[:, :, 128:].transpose(2, 1, 0))
    a["wo1"] = f(z["L1_attn_wo"].reshape(16, 128, 256).transpose(1, 0, 2))
    a["wqr"] = f(z["L1_attn_wq_rope"].reshape(96, 16, 64)[:, :, halves])
    a["gateT"] = kp(z["L1_ffn_gate_w"].T)
    sw = np.zeros((128, 2, 2, 384), np.float32)
    for w, n in enumerate(("L1_ffn_sw1", "L1_ffn_sw3")):
        sw[:, :, w, :352] = kp(z[n].T)
    a["sw13"] = sw
    sw2 = np.zeros((384, 256), np.float32)
    sw2[:352] = z["L1_ffn_sw2"].T
    a["sw2"] = kp(sw2)
    w1, w3 = (z[n].transpose(0, 2, 1).reshape(64, 2, 128, 176).transpose(0, 2, 1, 3) for n in ("L1_ffn_w1", "L1_ffn_w3"))
    gap = np.zeros((64, 128, 2, 16), np.float32)
    up = np.concatenate([w1[..., :128], w3[..., :128], w1[..., 128:], gap, w3[..., 128:]], 3)
    w2 = z["L1_ffn_w2"].transpose(0, 2, 1)
    a["we"] = f(np.concatenate([up.reshape(64, 128, 736), w2[:, :128]], 2))
    a["we2"] = f(w2[:, 128:])
    return a


def _constants(np):
    bf = np.dtype("bfloat16")
    c = {"ident": np.eye(128, dtype=np.float32), "identb": np.eye(128).astype(bf)}
    c["maskb"] = np.where(np.arange(128)[:, None] < np.arange(128)[None, :], -1e30, 0.0).astype(bf)
    c["trib"] = np.triu(np.ones((128, 128)), 1).astype(bf)
    c["onesb"] = np.ones((128, 128)).astype(bf)
    c["iota"] = np.tile(np.arange(128, dtype=np.float32), (128, 1))
    c["padid"] = (2049 + np.arange(128, dtype=np.float32))[:, None]
    c["tokid"] = (np.arange(16)[None, :] * 128 + np.arange(128)[:, None]).astype(np.float32)
    pos = np.arange(1024, dtype=np.float32)
    f0 = np.power(np.float32(10000.0), -np.arange(64, dtype=np.float32) / np.float32(64))
    ang = (pos[:, None] * f0[None, :]).astype(np.float32).astype(np.float64).T
    q = 128 ** -0.25
    r0 = np.zeros((128, 2, 1024), np.float32)
    r0[:64, 0] = r0[64:, 0] = np.cos(ang) * q
    r0[:64, 1] = np.sin(ang) * q
    r0[64:, 1] = -np.sin(ang) * q
    c["rope0"] = r0
    f1 = (np.float32(1.0) / np.power(np.float32(10000.0), np.arange(0, 64, 2, dtype=np.float32) / np.float32(64))).astype(np.float32)
    ang = (pos[:, None] * f1[None, :]).astype(np.float32).astype(np.float64)
    cos, sin = np.cos(ang), np.sin(ang)
    r1 = np.zeros((128, 2, 1024), np.float32)
    r1[64:96, 0] = r1[96:, 0] = cos.T
    r1[64:96, 1], r1[96:, 1] = sin.T, -sin.T
    c["rope1"] = r1
    k = np.zeros((128, 2, 8, 64), np.float32)
    cs, sn = (m.reshape(8, 128, 32).transpose(1, 0, 2) for m in (cos, sin))
    k[:, 0, :, :32] = k[:, 0, :, 32:] = cs
    k[:, 1, :, :32], k[:, 1, :, 32:] = -sn, sn
    c["kcs"] = k
    return c


def kernel(**inputs):
    import numpy as np
    import concourse.bacc as bacc
    from concourse.bass_utils import run_bass_kernel_spmd

    nc = bacc.Bacc("TRN2", target_bir_lowering=False, num_devices=1)
    arrays = {**_layouts(np, {k: np.asarray(v) for k, v in inputs.items()}), **_constants(np)}
    aps = {k: nc.dram_tensor(f"in_{k}", v.shape, mybir.dt.from_np(v.dtype), kind="ExternalInput").ap() for k, v in arrays.items()}
    out = nc.dram_tensor("out_x", (B, T, M), F32, kind="ExternalOutput").ap()
    program(nc, aps, out)
    r = run_bass_kernel_spmd(nc, [{f"in_{k}": v for k, v in arrays.items()}], core_ids=[0])
    return r.results[0]["out_x"]
```
